# Optimizing a Trainium2 kernel written in Bass

```python
import numpy as np
import jax
import jax.numpy as jnp

def _softmax(x, axis=-1):
    return jax.nn.softmax(x, axis=axis)

def _gelu(x):
    return jax.nn.gelu(x, approximate=True)

def _silu(x):
    return jax.nn.silu(x)

def _sigmoid(x):
    return jax.nn.sigmoid(x)

def _layernorm(x, axis=-1, eps=1e-05):
    m = jnp.mean(x, axis=axis, keepdims=True)
    v = jnp.var(x, axis=axis, keepdims=True)
    return (x - m) / jnp.sqrt(v + eps)

def _scatter_add(tgt, idx, src, axis=0):
    return tgt.at[idx].add(src)

def _segment_sum(src, seg, n):
    return jax.ops.segment_sum(src, seg, n)
kernel_name = 'mk_flamingo_gated_d2_seqx_r4_9b6004'

def setup_inputs(seed: int=0):
    np.random.seed(seed)
    _w = jnp.asarray

    def _rec_inputs():
        import jax
        import jax.numpy as jnp
        _rk = jax.random.key(seed)
        x = -0.000125 + 0.9999 * jax.random.normal(jax.random.fold_in(_rk, 1), (8, 256, 512), jnp.float32)
        _lenS = 256 - jax.random.randint(jax.random.fold_in(_rk, 7), (8,), 0, max(1, 256 // 4) + 1, jnp.int32)
        _lenS2 = 256 - jax.random.randint(jax.random.fold_in(_rk, 8), (8,), 0, max(1, 256 // 4) + 1, jnp.int32)
        _ctx_2048P = jax.random.normal(jax.random.fold_in(_rk, 11), (8, 16, 512), jnp.float32)
        _ctx_2048c = jax.random.dirichlet(jax.random.fold_in(_rk, 511), 0.3 * jnp.ones((16,), jnp.float32), (8, 256))
        _ctx_2048t = jnp.einsum('bsk,bkd->bsd', _ctx_2048c, _ctx_2048P)
        _ctx_2048t = _ctx_2048t * jax.lax.rsqrt(jnp.mean(jnp.square(_ctx_2048t)) + 1e-12) * 0.953939
        ctx_2048 = 1.72703e-05 + 1.00003 * (_ctx_2048t + 0.3 * jax.random.normal(jax.random.fold_in(_rk, 611), (8, 256, 512), jnp.float32))
        _g = jax.random.normal(jax.random.fold_in(_rk, 9001), (2, 2), jnp.float32)
        _g = jnp.sign(_g) * jnp.maximum(jnp.abs(_g), 1.0) + (_g == 0) * 1.0
        g_xattn = _g[0]
        g_ffn = _g[1]
        return (x, ctx_2048, g_xattn, g_ffn)
    x, ctx_2048, g_xattn, g_ffn = _rec_inputs()

    def _L0_xattn_setup():
        import jax, jax.numpy as jnp
        import numpy as np
        DIM = 512
        NH = 16
        HD = DIM // NH
        EPS = 1e-06
        IMG_LEN = 257

        def rms_norm(x, w, eps=EPS):
            xf = x.astype(jnp.float32)
            y = xf * jax.lax.rsqrt(jnp.mean(xf * xf, axis=-1, keepdims=True) + eps)
            return y.astype(x.dtype) * w

        def linear(x, w, b):
            return jnp.einsum('blc,oc->blo', x, w) + b

        def attention(q, k, v):
            scale = 1.0 / jnp.sqrt(jnp.asarray(HD, q.dtype))
            scores = jnp.einsum('bqhd,bkhd->bhqk', q, k) * scale
            probs = jax.nn.softmax(scores, axis=-1)
            return jnp.einsum('bhqk,bkhd->bqhd', probs, v)
        key = jax.random.key(seed)
        ks = jax.random.split(key, 12)
        B, L = (2, 2048)
        s = 0.02
        inp = {'x': jax.random.normal(ks[0], (B, L, DIM), jnp.float32), 'context': jax.random.normal(ks[1], (B, 769, DIM), jnp.float32), 'q_w': jax.random.normal(ks[2], (DIM, DIM), jnp.float32) * s, 'q_b': jnp.zeros((DIM,), jnp.float32), 'k_w': jax.random.normal(ks[3], (DIM, DIM), jnp.float32) * s, 'k_b': jnp.zeros((DIM,), jnp.float32), 'v_w': jax.random.normal(ks[4], (DIM, DIM), jnp.float32) * s, 'v_b': jnp.zeros((DIM,), jnp.float32), 'k_img_w': jax.random.normal(ks[5], (DIM, DIM), jnp.float32) * s, 'k_img_b': jnp.zeros((DIM,), jnp.float32), 'v_img_w': jax.random.normal(ks[6], (DIM, DIM), jnp.float32) * s, 'v_img_b': jnp.zeros((DIM,), jnp.float32), 'o_w': jax.random.normal(ks[7], (DIM, DIM), jnp.float32) * s, 'o_b': jnp.zeros((DIM,), jnp.float32), 'norm_q_w': jnp.ones((DIM,), jnp.float32), 'norm_k_w': jnp.ones((DIM,), jnp.float32), 'norm_k_img_w': jnp.ones((DIM,), jnp.float32)}
        return inp
    _L0_xattn_all = _L0_xattn_setup()
    _L0_xattn_in = {k: v for k, v in _L0_xattn_all.items() if k in ('q_w', 'q_b', 'k_w', 'k_b', 'v_w', 'v_b', 'k_img_w', 'k_img_b', 'v_img_w', 'v_img_b', 'o_w', 'o_b', 'norm_q_w', 'norm_k_w', 'norm_k_img_w')}
    del _L0_xattn_all

    def _L0_ffn_setup():
        import jax, jax.numpy as jnp
        import numpy as np
        EPS = 1e-05
        RMS_EPS = 1e-06

        def activation_quant(x, num_bits=8):
            qn = -2 ** (num_bits - 1)
            qp = 2 ** (num_bits - 1) - 1
            xf = x.astype(jnp.float32)
            s = qp / jnp.clip(jnp.max(jnp.abs(xf), axis=-1, keepdims=True), EPS, None)
            return (jnp.clip(jnp.round(xf * s), qn, qp) / s).astype(x.dtype)

        def weight_quant(w):
            wf = w.astype(jnp.float32)
            s = 1.0 / jnp.clip(jnp.mean(jnp.abs(wf)), EPS, None)
            return (jnp.clip(jnp.round(wf * s), -1.0, 1.0) / s).astype(w.dtype)

        def bit_linear(x, w):
            qx = x + jax.lax.stop_gradient(activation_quant(x) - x)
            qw = w + jax.lax.stop_gradient(weight_quant(w) - w)
            return jnp.einsum('bsh,oh->bso', qx, qw)

        def rms_norm(x, weight, eps=RMS_EPS):
            xf = x.astype(jnp.float32)
            var = jnp.mean(xf * xf, axis=-1, keepdims=True)
            return weight * (xf * jax.lax.rsqrt(var + eps)).astype(x.dtype)
        key = jax.random.key(seed)
        k1, k2, k3, k4 = jax.random.split(key, 4)
        B, S, H, I = (2, 512, 512, 2048)
        scale = 1.0 / np.sqrt(H)
        return {'x': jax.random.normal(k1, (B, S, H), dtype=jnp.float32), 'w_gate': jax.random.normal(k2, (I, H), dtype=jnp.float32) * scale, 'w_up': jax.random.normal(k3, (I, H), dtype=jnp.float32) * scale, 'w_down': jax.random.normal(k4, (H, I), dtype=jnp.float32) * (1.0 / np.sqrt(I)), 'ln_weight': jnp.ones((I,), dtype=jnp.float32)}
    _L0_ffn_all = _L0_ffn_setup()
    _L0_ffn_in = {k: v for k, v in _L0_ffn_all.items() if k in ('w_gate', 'w_up', 'w_down', 'ln_weight')}
    del _L0_ffn_all

    def _L1_xattn_setup():
        import jax, jax.numpy as jnp
        import numpy as np
        B, S, D = (8, 256, 512)
        H, HD = (16, 128)
        key = jax.random.key(seed)
        ks = jax.random.split(key, 6)
        fan_in = 1.0 / np.sqrt(D)
        return {'inputs_q': jax.random.normal(ks[0], (B, S, D), jnp.float32), 'inputs_kv': jax.random.normal(ks[1], (B, S, D), jnp.float32), 'Wq': jax.random.normal(ks[2], (D, H * HD), jnp.float32) * fan_in, 'Wk': jax.random.normal(ks[3], (D, H * HD), jnp.float32) * fan_in, 'Wv': jax.random.normal(ks[4], (D, H * HD), jnp.float32) * fan_in, 'Wo': jax.random.normal(ks[5], (H * HD, D), jnp.float32) * (1.0 / np.sqrt(H * HD))}
    _L1_xattn_all = _L1_xattn_setup()
    _L1_xattn_in = {k: v for k, v in _L1_xattn_all.items() if k in ('Wq', 'Wk', 'Wv', 'Wo')}
    del _L1_xattn_all

    def _L1_ffn_setup():
        import jax, jax.numpy as jnp
        import numpy as np
        B, S, H = (4, 256, 512)
        NH = 16
        HD = H // NH
        RD = HD // 2
        LAT = H // 4
        I = 256
        NE = 8
        NSH = 1
        NR = NE - NSH
        TOPK = 2
        EPS = 1e-05
        SCALING = 8.0

        def _w(key, shape, fan_in):
            return jax.random.normal(key, shape, dtype=jnp.float32) / np.sqrt(fan_in)

        def rmsnorm(x, w):
            rms = jax.lax.rsqrt(jnp.mean(x * x, axis=-1, keepdims=True) + EPS)
            return w * rms * x

        def rope_cos_sin(seq_len):
            inv_freq = 1.0 / 10000.0 ** (jnp.arange(0, RD, 2, dtype=jnp.float32) / RD)
            t = jnp.arange(seq_len, dtype=jnp.float32)
            ang = jnp.outer(t, inv_freq)
            emb = jnp.concatenate([ang, ang], axis=-1)
            return (jnp.cos(emb), jnp.sin(emb))

        def apply_rope(x, cos, sin):
            c = cos[None, :, None, :]
            s = sin[None, :, None, :]
            x1, x2 = jnp.split(x, 2, axis=-1)
            rot = jnp.concatenate([-x2, x1], axis=-1)
            return x * c + rot * s

        def expert_ffn(x, wg, wu, wd):
            h = jax.nn.silu(x @ wg) * (x @ wu) / SCALING
            return h @ wd

        def attention(x, kv_d_w, q_d_w, k_u_w, v_u_w, q_u_w, rope_k_w, rope_q_w, o_w):
            b, s, _ = x.shape
            kv_d = x @ kv_d_w
            q_d = x @ q_d_w
            k_p = (kv_d @ k_u_w).reshape(b, s, NH, RD)
            q_p = (q_d @ q_u_w).reshape(b, s, NH, RD)
            v = (kv_d @ v_u_w).reshape(b, s, NH, HD)
            k_r = (x @ rope_k_w).reshape(b, s, NH, RD)
            q_r = (q_d @ rope_q_w).reshape(b, s, NH, RD)
            cos, sin = rope_cos_sin(s)
            k_r = apply_rope(k_r, cos, sin)
            q_r = apply_rope(q_r, cos, sin)
            k = jnp.concatenate([k_p, k_r], axis=-1)
            q = jnp.concatenate([q_p, q_r], axis=-1)
            scale = 1.0 / np.sqrt(HD)
            scores = jnp.einsum('bqhd,bkhd->bhqk', q, k) * scale
            causal = jnp.tril(jnp.ones((s, s), dtype=bool))
            scores = jnp.where(causal[None, None], scores, jnp.finfo(scores.dtype).min)
            probs = jax.nn.softmax(scores, axis=-1)
            out = jnp.einsum('bhqk,bkhd->bqhd', probs, v).reshape(b, s, H)
            return out @ o_w

        def moe(x, sh_gate, sh_up, sh_down, r_gate, r_up, r_down, router_w, router_b):
            shared = expert_ffn(x, sh_gate, sh_up, sh_down)
            logits = x @ router_w + router_b
            probs = jax.nn.sigmoid(logits)
            scores, idx = jax.lax.top_k(probs, TOPK)
            scores = scores / jnp.sum(scores, axis=-1, keepdims=True)
            w = jnp.sum(jax.nn.one_hot(idx, NR, dtype=x.dtype) * scores[..., None], axis=-2)
            combined = jnp.zeros_like(x)
            for e in range(NR):
                combined = combined + w[..., e:e + 1] * expert_ffn(x, r_gate[e], r_up[e], r_down[e])
            return shared + combined
        key = jax.random.key(seed)
        ks = jax.random.split(key, 24)
        return {'x': jax.random.normal(ks[0], (B, S, H), dtype=jnp.float32), 'ln1_w': jnp.ones((H,), jnp.float32), 'ln2_w': jnp.ones((H,), jnp.float32), 'kv_d_w': _w(ks[1], (H, LAT), H), 'q_d_w': _w(ks[2], (H, LAT), H), 'k_u_w': _w(ks[3], (LAT, H // 2), LAT), 'v_u_w': _w(ks[4], (LAT, H), LAT), 'q_u_w': _w(ks[5], (LAT, H // 2), LAT), 'rope_k_w': _w(ks[6], (H, H // 2), H), 'rope_q_w': _w(ks[7], (LAT, H // 2), LAT), 'o_w': _w(ks[8], (H, H), H), 'sh_gate': _w(ks[9], (H, I), H), 'sh_up': _w(ks[10], (H, I), H), 'sh_down': _w(ks[11], (I, H), I), 'r_gate': _w(ks[12], (NR, H, I), H), 'r_up': _w(ks[13], (NR, H, I), H), 'r_down': _w(ks[14], (NR, I, H), I), 'router_w': _w(ks[15], (H, NR), H), 'router_b': jnp.zeros((NR,), jnp.float32)}
    _L1_ffn_all = _L1_ffn_setup()
    _L1_ffn_in = {k: v for k, v in _L1_ffn_all.items() if k in ('ln1_w', 'ln2_w', 'kv_d_w', 'q_d_w', 'k_u_w', 'v_u_w', 'q_u_w', 'rope_k_w', 'rope_q_w', 'o_w', 'sh_gate', 'sh_up', 'sh_down', 'r_gate', 'r_up', 'r_down', 'router_w', 'router_b')}
    del _L1_ffn_all
    return {'x': x, 'ctx_2048': ctx_2048, 'g_xattn': g_xattn, 'g_ffn': g_ffn, 'L0_xattn_q_w': _L0_xattn_in['q_w'], 'L0_xattn_q_b': _L0_xattn_in['q_b'], 'L0_xattn_k_w': _L0_xattn_in['k_w'], 'L0_xattn_k_b': _L0_xattn_in['k_b'], 'L0_xattn_v_w': _L0_xattn_in['v_w'], 'L0_xattn_v_b': _L0_xattn_in['v_b'], 'L0_xattn_k_img_w': _L0_xattn_in['k_img_w'], 'L0_xattn_k_img_b': _L0_xattn_in['k_img_b'], 'L0_xattn_v_img_w': _L0_xattn_in['v_img_w'], 'L0_xattn_v_img_b': _L0_xattn_in['v_img_b'], 'L0_xattn_o_w': _L0_xattn_in['o_w'], 'L0_xattn_o_b': _L0_xattn_in['o_b'], 'L0_xattn_norm_q_w': _L0_xattn_in['norm_q_w'], 'L0_xattn_norm_k_w': _L0_xattn_in['norm_k_w'], 'L0_xattn_norm_k_img_w': _L0_xattn_in['norm_k_img_w'], 'L0_ffn_w_gate': _L0_ffn_in['w_gate'], 'L0_ffn_w_up': _L0_ffn_in['w_up'], 'L0_ffn_w_down': _L0_ffn_in['w_down'], 'L0_ffn_ln_weight': _L0_ffn_in['ln_weight'], 'L1_xattn_Wq': _L1_xattn_in['Wq'], 'L1_xattn_Wk': _L1_xattn_in['Wk'], 'L1_xattn_Wv': _L1_xattn_in['Wv'], 'L1_xattn_Wo': _L1_xattn_in['Wo'], 'L1_ffn_ln1_w': _L1_ffn_in['ln1_w'], 'L1_ffn_ln2_w': _L1_ffn_in['ln2_w'], 'L1_ffn_kv_d_w': _L1_ffn_in['kv_d_w'], 'L1_ffn_q_d_w': _L1_ffn_in['q_d_w'], 'L1_ffn_k_u_w': _L1_ffn_in['k_u_w'], 'L1_ffn_v_u_w': _L1_ffn_in['v_u_w'], 'L1_ffn_q_u_w': _L1_ffn_in['q_u_w'], 'L1_ffn_rope_k_w': _L1_ffn_in['rope_k_w'], 'L1_ffn_rope_q_w': _L1_ffn_in['rope_q_w'], 'L1_ffn_o_w': _L1_ffn_in['o_w'], 'L1_ffn_sh_gate': _L1_ffn_in['sh_gate'], 'L1_ffn_sh_up': _L1_ffn_in['sh_up'], 'L1_ffn_sh_down': _L1_ffn_in['sh_down'], 'L1_ffn_r_gate': _L1_ffn_in['r_gate'], 'L1_ffn_r_up': _L1_ffn_in['r_up'], 'L1_ffn_r_down': _L1_ffn_in['r_down'], 'L1_ffn_router_w': _L1_ffn_in['router_w'], 'L1_ffn_router_b': _L1_ffn_in['router_b']}

def reference(x, ctx_2048, g_xattn, g_ffn, L0_xattn_q_w, L0_xattn_q_b, L0_xattn_k_w, L0_xattn_k_b, L0_xattn_v_w, L0_xattn_v_b, L0_xattn_k_img_w, L0_xattn_k_img_b, L0_xattn_v_img_w, L0_xattn_v_img_b, L0_xattn_o_w, L0_xattn_o_b, L0_xattn_norm_q_w, L0_xattn_norm_k_w, L0_xattn_norm_k_img_w, L0_ffn_w_gate, L0_ffn_w_up, L0_ffn_w_down, L0_ffn_ln_weight, L1_xattn_Wq, L1_xattn_Wk, L1_xattn_Wv, L1_xattn_Wo, L1_ffn_ln1_w, L1_ffn_ln2_w, L1_ffn_kv_d_w, L1_ffn_q_d_w, L1_ffn_k_u_w, L1_ffn_v_u_w, L1_ffn_q_u_w, L1_ffn_rope_k_w, L1_ffn_rope_q_w, L1_ffn_o_w, L1_ffn_sh_gate, L1_ffn_sh_up, L1_ffn_sh_down, L1_ffn_r_gate, L1_ffn_r_up, L1_ffn_r_down, L1_ffn_router_w, L1_ffn_router_b):
    import jax
    import jax.numpy as jnp

    def _L0_xattn_ref(x, context, q_w, q_b, k_w, k_b, v_w, v_b, k_img_w, k_img_b, v_img_w, v_img_b, o_w, o_b, norm_q_w, norm_k_w, norm_k_img_w):
        import jax, jax.numpy as jnp
        import numpy as np
        DIM = 512
        NH = 16
        HD = DIM // NH
        EPS = 1e-06
        IMG_LEN = 257

        def rms_norm(x, w, eps=EPS):
            xf = x.astype(jnp.float32)
            y = xf * jax.lax.rsqrt(jnp.mean(xf * xf, axis=-1, keepdims=True) + eps)
            return y.astype(x.dtype) * w

        def linear(x, w, b):
            return jnp.einsum('blc,oc->blo', x, w) + b

        def attention(q, k, v):
            scale = 1.0 / jnp.sqrt(jnp.asarray(HD, q.dtype))
            scores = jnp.einsum('bqhd,bkhd->bhqk', q, k) * scale
            probs = jax.nn.softmax(scores, axis=-1)
            return jnp.einsum('bhqk,bkhd->bqhd', probs, v)
        B, L, _ = x.shape
        ctx_img = context[:, :IMG_LEN]
        ctx_txt = context[:, IMG_LEN:]
        q = rms_norm(linear(x, q_w, q_b), norm_q_w).reshape(B, L, NH, HD)
        k = rms_norm(linear(ctx_txt, k_w, k_b), norm_k_w).reshape(B, -1, NH, HD)
        v = linear(ctx_txt, v_w, v_b).reshape(B, -1, NH, HD)
        k_img = rms_norm(linear(ctx_img, k_img_w, k_img_b), norm_k_img_w).reshape(B, -1, NH, HD)
        v_img = linear(ctx_img, v_img_w, v_img_b).reshape(B, -1, NH, HD)
        img_x = attention(q, k_img, v_img)
        txt_x = attention(q, k, v)
        out = (txt_x + img_x).reshape(B, L, DIM)
        return linear(out, o_w, o_b)

    def _L0_ffn_ref(x, w_gate, w_up, w_down, ln_weight):
        import jax, jax.numpy as jnp
        import numpy as np
        EPS = 1e-05
        RMS_EPS = 1e-06

        def activation_quant(x, num_bits=8):
            qn = -2 ** (num_bits - 1)
            qp = 2 ** (num_bits - 1) - 1
            xf = x.astype(jnp.float32)
            s = qp / jnp.clip(jnp.max(jnp.abs(xf), axis=-1, keepdims=True), EPS, None)
            return (jnp.clip(jnp.round(xf * s), qn, qp) / s).astype(x.dtype)

        def weight_quant(w):
            wf = w.astype(jnp.float32)
            s = 1.0 / jnp.clip(jnp.mean(jnp.abs(wf)), EPS, None)
            return (jnp.clip(jnp.round(wf * s), -1.0, 1.0) / s).astype(w.dtype)

        def bit_linear(x, w):
            qx = x + jax.lax.stop_gradient(activation_quant(x) - x)
            qw = w + jax.lax.stop_gradient(weight_quant(w) - w)
            return jnp.einsum('bsh,oh->bso', qx, qw)

        def rms_norm(x, weight, eps=RMS_EPS):
            xf = x.astype(jnp.float32)
            var = jnp.mean(xf * xf, axis=-1, keepdims=True)
            return weight * (xf * jax.lax.rsqrt(var + eps)).astype(x.dtype)
        h = jax.nn.silu(bit_linear(x, w_gate)) * bit_linear(x, w_up)
        h = rms_norm(h, ln_weight)
        return bit_linear(h, w_down)

    def _L1_xattn_ref(inputs_q, inputs_kv, Wq, Wk, Wv, Wo):
        import jax, jax.numpy as jnp
        import numpy as np
        B, S, D = (8, 256, 512)
        H, HD = (16, 128)
        b, sq, _ = inputs_q.shape
        skv = inputs_kv.shape[1]
        q = (inputs_q @ Wq).reshape(b, sq, H, HD) * (1.0 / np.sqrt(HD))
        k = (inputs_kv @ Wk).reshape(b, skv, H, HD)
        v = (inputs_kv @ Wv).reshape(b, skv, H, HD)
        scores = jnp.einsum('bqhd,bkhd->bhqk', q, k)
        attn = jax.nn.softmax(scores, axis=-1)
        ctx = jnp.einsum('bhqk,bkhd->bqhd', attn, v).reshape(b, sq, H * HD)
        return ctx @ Wo

    def _L1_ffn_ref(x, ln1_w, ln2_w, kv_d_w, q_d_w, k_u_w, v_u_w, q_u_w, rope_k_w, rope_q_w, o_w, sh_gate, sh_up, sh_down, r_gate, r_up, r_down, router_w, router_b):
        import jax, jax.numpy as jnp
        import numpy as np
        B, S, H = (4, 256, 512)
        NH = 16
        HD = H // NH
        RD = HD // 2
        LAT = H // 4
        I = 256
        NE = 8
        NSH = 1
        NR = NE - NSH
        TOPK = 2
        EPS = 1e-05
        SCALING = 8.0

        def _w(key, shape, fan_in):
            return jax.random.normal(key, shape, dtype=jnp.float32) / np.sqrt(fan_in)

        def rmsnorm(x, w):
            rms = jax.lax.rsqrt(jnp.mean(x * x, axis=-1, keepdims=True) + EPS)
            return w * rms * x

        def rope_cos_sin(seq_len):
            inv_freq = 1.0 / 10000.0 ** (jnp.arange(0, RD, 2, dtype=jnp.float32) / RD)
            t = jnp.arange(seq_len, dtype=jnp.float32)
            ang = jnp.outer(t, inv_freq)
            emb = jnp.concatenate([ang, ang], axis=-1)
            return (jnp.cos(emb), jnp.sin(emb))

        def apply_rope(x, cos, sin):
            c = cos[None, :, None, :]
            s = sin[None, :, None, :]
            x1, x2 = jnp.split(x, 2, axis=-1)
            rot = jnp.concatenate([-x2, x1], axis=-1)
            return x * c + rot * s

        def expert_ffn(x, wg, wu, wd):
            h = jax.nn.silu(x @ wg) * (x @ wu) / SCALING
            return h @ wd

        def attention(x, kv_d_w, q_d_w, k_u_w, v_u_w, q_u_w, rope_k_w, rope_q_w, o_w):
            b, s, _ = x.shape
            kv_d = x @ kv_d_w
            q_d = x @ q_d_w
            k_p = (kv_d @ k_u_w).reshape(b, s, NH, RD)
            q_p = (q_d @ q_u_w).reshape(b, s, NH, RD)
            v = (kv_d @ v_u_w).reshape(b, s, NH, HD)
            k_r = (x @ rope_k_w).reshape(b, s, NH, RD)
            q_r = (q_d @ rope_q_w).reshape(b, s, NH, RD)
            cos, sin = rope_cos_sin(s)
            k_r = apply_rope(k_r, cos, sin)
            q_r = apply_rope(q_r, cos, sin)
            k = jnp.concatenate([k_p, k_r], axis=-1)
            q = jnp.concatenate([q_p, q_r], axis=-1)
            scale = 1.0 / np.sqrt(HD)
            scores = jnp.einsum('bqhd,bkhd->bhqk', q, k) * scale
            causal = jnp.tril(jnp.ones((s, s), dtype=bool))
            scores = jnp.where(causal[None, None], scores, jnp.finfo(scores.dtype).min)
            probs = jax.nn.softmax(scores, axis=-1)
            out = jnp.einsum('bhqk,bkhd->bqhd', probs, v).reshape(b, s, H)
            return out @ o_w

        def moe(x, sh_gate, sh_up, sh_down, r_gate, r_up, r_down, router_w, router_b):
            shared = expert_ffn(x, sh_gate, sh_up, sh_down)
            logits = x @ router_w + router_b
            probs = jax.nn.sigmoid(logits)
            scores, idx = jax.lax.top_k(probs, TOPK)
            scores = scores / jnp.sum(scores, axis=-1, keepdims=True)
            w = jnp.sum(jax.nn.one_hot(idx, NR, dtype=x.dtype) * scores[..., None], axis=-2)
            combined = jnp.zeros_like(x)
            for e in range(NR):
                combined = combined + w[..., e:e + 1] * expert_ffn(x, r_gate[e], r_up[e], r_down[e])
            return shared + combined
        h = x + attention(rmsnorm(x, ln1_w), kv_d_w, q_d_w, k_u_w, v_u_w, q_u_w, rope_k_w, rope_q_w, o_w)
        out = h + moe(rmsnorm(h, ln2_w), sh_gate, sh_up, sh_down, r_gate, r_up, r_down, router_w, router_b)
        return out
    x = x + jnp.tanh(g_xattn[0]) * _L0_xattn_ref(_layernorm(x, axis=-1), ctx_2048, L0_xattn_q_w, L0_xattn_q_b, L0_xattn_k_w, L0_xattn_k_b, L0_xattn_v_w, L0_xattn_v_b, L0_xattn_k_img_w, L0_xattn_k_img_b, L0_xattn_v_img_w, L0_xattn_v_img_b, L0_xattn_o_w, L0_xattn_o_b, L0_xattn_norm_q_w, L0_xattn_norm_k_w, L0_xattn_norm_k_img_w)
    x = x + jnp.tanh(g_ffn[0]) * _L0_ffn_ref(_layernorm(x, axis=-1), L0_ffn_w_gate, L0_ffn_w_up, L0_ffn_w_down, L0_ffn_ln_weight)
    x = x + jnp.tanh(g_xattn[1]) * _L1_xattn_ref(_layernorm(x, axis=-1), ctx_2048, L1_xattn_Wq, L1_xattn_Wk, L1_xattn_Wv, L1_xattn_Wo)
    x = x + jnp.tanh(g_ffn[1]) * _L1_ffn_ref(_layernorm(x, axis=-1), L1_ffn_ln1_w, L1_ffn_ln2_w, L1_ffn_kv_d_w, L1_ffn_q_d_w, L1_ffn_k_u_w, L1_ffn_v_u_w, L1_ffn_q_u_w, L1_ffn_rope_k_w, L1_ffn_rope_q_w, L1_ffn_o_w, L1_ffn_sh_gate, L1_ffn_sh_up, L1_ffn_sh_down, L1_ffn_r_gate, L1_ffn_r_up, L1_ffn_r_down, L1_ffn_router_w, L1_ffn_router_b)
    return x

_drawn_inputs = setup_inputs


def setup_inputs(seed=0):
    import zlib

    import numpy as np

    out = dict(_drawn_inputs(seed))
    spreads = {'g_ffn': (-1.0, 0.2),
     'L0_xattn_q_b': (0.0, 0.391),
     'L0_xattn_k_b': (0.0, 0.1),
     'L0_xattn_v_b': (0.0, 0.1),
     'L0_xattn_k_img_b': (0.0, 0.643),
     'L0_xattn_v_img_b': (0.0, 0.1),
     'L0_xattn_o_b': (0.0, 0.1),
     'L0_xattn_norm_q_w': (1.0, 0.6),
     'L0_xattn_norm_k_w': (1.0, 0.2),
     'L0_xattn_norm_k_img_w': (1.0, 0.6),
     'L0_ffn_ln_weight': (1.0, 0.2),
     'L1_ffn_ln1_w': (1.0, 0.2),
     'L1_ffn_ln2_w': (1.0, 0.2),
     'L1_ffn_router_b': (0.0, 0.305)}
    factors = {}
    for name, (base, spread) in spreads.items():
        noise = np.random.default_rng([zlib.crc32(name.encode()), seed]).standard_normal(out[name].shape)
        drawn = base * np.exp(spread * noise) if base else spread * noise
        out[name] = jnp.asarray(drawn.astype(out[name].dtype))
    for name, factor in factors.items():
        out[name] = (out[name] * factor).astype(out[name].dtype)
    return out
```

```python
from contextlib import ExitStack

import numpy as np

import concourse.bass as bass
from concourse import mybir

ALU = mybir.AluOpType
ACT = mybir.ActivationFunctionType
AX = mybir.AxisListType
F32 = mybir.dt.float32
F32R = mybir.dt.float32r
BF16 = mybir.dt.bfloat16
I32 = mybir.dt.int32
U32 = mybir.dt.uint32

P = 128
BATCH, SEQ, D = 8, 256, 512
TOK = BATCH * SEQ
TILES = TOK // P
TB = SEQ // P
C = D // P
NH = 16
ROUND = 12582912.0
LN_EPS = 1e-5
RMS_EPS = 1e-6


def f32(ap):
    return ap.bitcast(F32)


def at(b, per, k):
    return b * per + max(k, 0)


def split_product(pe, out, lhs, rhs, first, last):
    pe.matmul(out, lhs[0], rhs[1], start=first, stop=False)
    pe.matmul(out, lhs[0], rhs[0], start=False, stop=False)
    return pe.matmul(out, lhs[1], rhs[0], start=False, stop=last)


def wait_apart(eng, sem, value, begun):
    eng.wait_ge(sem, value)
    eng.wait_ge(begun, 1)


class Chain:

    def __init__(self, eng, sem, begun):
        self.eng, self.sem, self.begun, self.base, self.n = eng, sem, begun, 0, 0

    def turn(self, base):
        self.base, self.n = base, 0

    def step(self, ins):
        ins.then_inc(self.sem, 1)
        self.n += 1

    def wait(self):
        self.eng.wait_ge(self.sem, self.base + self.n)


def inverse_sqrt(dve, chain, out, var, tmp):
    chain.step(dve.tensor_scalar(out.bitcast(I32), var.bitcast(I32), -0.5, 1597463007.0, ALU.mult, ALU.add))
    for _ in range(4):
        chain.wait()
        chain.step(dve.tensor_tensor(tmp, out, out, ALU.mult))
        chain.wait()
        chain.step(dve.tensor_tensor(tmp, tmp, var, ALU.mult))
        chain.wait()
        chain.step(dve.tensor_scalar(tmp, tmp, -0.5, 1.5, ALU.mult, ALU.add))
        chain.wait()
        chain.step(dve.tensor_tensor(out, out, tmp, ALU.mult))


INVERSE_SQRT_STEPS = 17


def layer_norm(dve, chain, out, x, small, tiles, done, to=None):
    stats, agg, var, rstd, tmp = small
    for t in range(tiles):
        chain.step(dve.bn_stats(stats[:, t, :], x(t)))
    chain.wait()
    chain.step(dve.tensor_copy(tmp[:, 0:1], stats[:, 0, 0:1]))
    for t in range(tiles):
        chain.step(dve.bn_aggr(agg[:, t, :], stats[:, t, :]))
    chain.wait()
    chain.step(dve.tensor_scalar(var[:, 0:tiles], agg[:, :, 1], LN_EPS, None, ALU.add))
    chain.wait()
    inverse_sqrt(dve, chain, rstd[:, 0:tiles], var[:, 0:tiles], tmp[:, 0:tiles])
    chain.wait()
    for t in range(tiles):
        dve.tensor_scalar(out[:, t, :] if to is None else to(t), x(t), agg[:, t, 0:1], rstd[:, t:t + 1], ALU.subtract, ALU.mult).then_inc(done, 1)


def layer_norm_steps(tiles):
    return 2 * tiles + 2 + INVERSE_SQRT_STEPS


def tile_of(x, n):
    return x[:, bass.ds(n, 1), :].rearrange("p o n -> p (o n)")


def chunks(bank):
    return bank.rearrange("p (c q) -> p c q", c=C)


class Attention:

    def __init__(self, nc, ctx, tag, begun, ident, units, scale, turned_buffers, causal=False):
        self.begun, self.ident, self.units, self.scale, self.buffers = begun, ident[:, :], units, scale, turned_buffers
        self.groups = units // TB
        self.causal = causal

        def sb(name, shape, dt=F32):
            return ctx.enter_context(nc.sbuf_tensor(f"{tag}_{name}", shape, dt))

        self.prob = sb("prob", [P, 2, 4, SEQ])
        self.prob_t = sb("prob_t", [P, turned_buffers, TB, 4, SEQ])
        self.peak, self.neg_peak, self.mass, self.inv_mass = (sb(n, [P, 2, 4]) for n in ("peak", "neg_peak", "mass", "inv_mass"))
        self.s_ps = ctx.enter_context(nc.psum_tensor(f"{tag}_s_ps", [P, 4, SEQ], F32))
        self.t_ps = ctx.enter_context(nc.psum_tensor(f"{tag}_t_ps", [P, TB, 512], F32))
        self.o_ps = ctx.enter_context(nc.psum_tensor(f"{tag}_o_ps", [P, 2, 512], F32))

        def sem(name):
            return nc.alloc_semaphore(f"{tag}_{name}")

        self.s_ready, self.peak_found, self.peak_done, self.exp_done = sem("s_ready"), sem("peak_found"), sem("peak_done"), sem("exp_done")
        self.mass_inverted, self.prob_done, self.t_ready = sem("mass_inverted"), sem("prob_done"), sem("t_ready")
        self.turned0, self.turned1 = sem("turned0"), sem("turned1")
        self.o_ready, self.o_hi_done, self.o_lo_done = sem("o_ready"), sem("o_hi_done"), sem("o_lo_done")

    def keys(self, u):
        return P if self.causal and u % 2 == 0 else SEQ

    def key_tiles(self, u):
        return self.keys(u) // P

    def scores(self, pe, b, u, q_of, k_of, mask=None, ident_b=None):
        n, w = b * self.units + u, self.keys(u)
        pe.wait_ge(self.exp_done, n)
        for j in range(4):
            if mask is not None:
                pe.matmul(self.s_ps[:, j, w - P:w], ident_b, mask, start=True, stop=False, skip_group_check=True)
            mm = pe.matmul(self.s_ps[:, j, 0:w], q_of(u, j), k_of(u, j)[:, 0:w], start=mask is None, stop=True,
                           skip_group_check=mask is not None)
        mm.then_inc(self.s_ready, 1)

    def find_peak(self, dve, b, u, scale=None):
        n, w = b * self.units + u, self.keys(u)
        dve.wait_ge(self.s_ready, n + 1)
        dve.tensor_reduce(self.peak[:, u % 2, :], self.s_ps[:, :, 0:w], AX.X, ALU.max).then_inc(self.peak_found, 1)
        dve.wait_ge(self.peak_found, n + 1)
        if scale is None:
            ins = dve.tensor_scalar(self.neg_peak[:, u % 2, :], self.peak[:, u % 2, :], -self.scale, None, ALU.mult)
        else:
            ins = dve.tensor_scalar(self.neg_peak[:, u % 2, :], self.peak[:, u % 2, :], scale, -1.0, ALU.mult, ALU.mult)
        ins.then_inc(self.peak_done, 1)

    def exponentials(self, act, b, u, scale=None):
        n, w = b * self.units + u, self.keys(u)
        act.wait_ge(self.t_ready, at(b, TB * self.units, TB * (u - 1)))
        act.wait_ge(self.peak_done, n + 1)
        for j in range(4):
            ins = act.activation(self.prob[:, u % 2, j, 0:w], self.s_ps[:, j, 0:w], ACT.Exp, bias=self.neg_peak[:, u % 2, j:j + 1],
                                 scale=self.scale if scale is None else scale, accum_out=self.mass[:, u % 2, j:j + 1])
        ins.then_inc(self.exp_done, 1)

    def invert_mass(self, dve, b, u):
        dve.wait_ge(self.exp_done, b * self.units + u + 1)
        dve.reciprocal(self.inv_mass[:, u % 2, :], self.mass[:, u % 2, :]).then_inc(self.mass_inverted, 1)

    def normalise(self, pool, b, u):
        w = self.keys(u)
        pool.wait_ge(self.mass_inverted, b * self.units + u + 1)
        part = self.prob[:, u % 2, :, 0:w]
        pool.tensor_tensor(part, part, self.inv_mass[:, u % 2, :].unsqueeze(2).to_broadcast([P, 4, w]), ALU.mult).then_inc(self.prob_done, 1)

    def turn(self, pe, b, u):
        n = b * self.units + u
        pe.wait_ge(self.prob_done, n + 1)
        for t, free in zip(range(TB), (self.turned0, self.turned1)):
            if t < self.key_tiles(u):
                pe.wait_ge(free, n - u % 2 if self.causal and t else n)
                for j in range(4):
                    mm = pe.transpose(self.t_ps[:, t, j * P:(j + 1) * P], self.prob[:, u % 2, j, t * P:(t + 1) * P], self.ident)
                mm.then_inc(self.t_ready, TB // self.key_tiles(u))

    def copy_turned(self, eng, b, u, t, par):
        n, g = b * self.units + u, u // TB
        if u % TB == (1 if self.causal and t else 0):
            eng.wait_ge(self.o_ready, at(b, self.groups, g - (self.buffers - 1)))
        if t < self.key_tiles(u):
            eng.wait_ge(self.t_ready, TB * n + t + 1)
        buf = (par * self.groups + g) % self.buffers
        to = self.prob_t[:, buf, t, :, (u % TB) * P:(u % TB + 1) * P]
        of = self.t_ps[:, t, :].rearrange("p (j q) -> p j q", j=4)
        if t == 0:
            eng.tensor_copy(to, of).then_inc(self.turned0, 1)
        elif self.key_tiles(u) == TB:
            eng.activation(to, of, ACT.Copy).then_inc(self.turned1, TB if self.causal else 1)

    def weigh(self, pe, b, g, par, v_of, out_of, banks):
        n = b * self.units + TB * g + TB
        pe.wait_ge(self.turned0, n)
        pe.wait_ge(self.turned1, n)
        pe.wait_ge(self.o_lo_done, at(b, self.groups, g - (banks - 1)))
        buf = (par * self.groups + g) % self.buffers
        for j, t in ([(j, t) for t in range(TB) for j in range(4)] if banks == 2 else [(j, t) for j in range(4) for t in range(TB)]):
            mm = pe.matmul(out_of(g, j), v_of(g, j, t), self.prob_t[:, buf, t, j, :], start=(t == 0), stop=(t == TB - 1))
        mm.then_inc(self.o_ready, 1)

    def output_high(self, act, b, g, to, of):
        act.wait_ge(self.o_ready, b * self.groups + g + 1)
        act.activation(to, of, ACT.Copy).then_inc(self.o_hi_done, 1)

    def output_low(self, dve, b, g, to, high, of):
        dve.wait_ge(self.o_hi_done, b * self.groups + g + 1)
        dve.tensor_tensor(to, of, f32(high), ALU.subtract).then_inc(self.o_lo_done, 1)


def image_attention(nc, x_res, ident, begun, x_in, ctx_t, w_t, rows, gate):
    tag = "a"
    HD = D // NH
    SCALE = float(HD) ** -0.5
    UNITS = NH // 4 * TB
    FRONT = 12
    TURN = FRONT + TB
    STEPS = layer_norm_steps(TB) + 2 * (1 + INVERSE_SQRT_STEPS)
    QB, KB, VB, OB, NQ, NK = range(6)

    with ExitStack() as ctx:
        def sb(name, shape, dt=F32):
            return ctx.enter_context(nc.sbuf_tensor(f"{tag}_{name}", shape, dt))

        def sem(name):
            return nc.alloc_semaphore(f"{tag}_{name}")

        w_hi = [sb(f"w_hi{n}", [P, C, D], F32R) for n in range(4)]
        w_lo = [sb(f"w_lo{n}", [P, C, D], F32R) for n in range(4)]
        row = sb("row", [P, 6, D])
        gate_sb = sb("gate_sb", [P, 1])
        gain = sb("gain", [P, 1])
        ctx_f = sb("ctx_f", [P, C, SEQ])
        ctx_hi, ctx_lo = sb("ctx_hi", [P, C, SEQ], F32R), sb("ctx_lo", [P, C, SEQ], F32R)
        xn = sb("xn", [P, TB, D])
        xt_hi, xt_lo = sb("xt_hi", [P, C, SEQ], F32R), sb("xt_lo", [P, C, SEQ], F32R)
        qf, kf = sb("qf", [P, TB, D]), sb("kf", [P, TB, D])
        q_head = sb("q_head", [P, 4, C, SEQ])
        kt = sb("kt", [P, C, SEQ])
        v = sb("v", [P, 2, TB, D])
        o_hi, o_lo = sb("o_hi", [P, C, SEQ], F32R), sb("o_lo", [P, C, SEQ], F32R)
        small = (sb("stats", [P, TB, 6]), sb("agg", [P, TB, 2]), sb("var", [P, TB]), sb("rstd", [P, TB]), sb("tmp", [P, TB]))
        sq_sum = sb("sq_sum", [P, 2, TB])
        k_rstd = sb("k_rstd", [P, TB])
        junk = sb("junk", [P, D])
        q_scale = sb("q_scale", [P, 2, TB])
        att = Attention(nc, ctx, tag, begun, ident, UNITS, None, 2)
        raw = att.prob_t[:, :, :, :, :].rearrange("p a t j s -> p a (t j s)").rearrange("p a (c n) -> p a c n", c=C)
        ring = ctx.enter_context(nc.psum_tensor(f"{tag}_ring", [P, 2, 512], F32))

        x_first, x_rest, ctx_in, rows_in = sem("x_first"), sem("x_rest"), sem("ctx_in"), sem("rows_in")
        w_in = [sem("w_in0"), sem("w_in1")]
        w_hi_done, w_lo_done, rows_done, gain_done, zeroed = sem("w_hi_done"), sem("w_lo_done"), sem("rows_done"), sem("gain_done"), sem("zeroed")
        ctx_hi_done, ctx_lo_done, steps, xn_done = sem("ctx_hi_done"), sem("ctx_lo_done"), sem("steps"), sem("xn_done")
        ring_ready, ring_free, xt_hi_done = sem("ring_ready"), sem("ring_free"), sem("xt_hi_done")
        squared, q_scaled, k_hat_done = sem("squared"), sem("q_scaled"), sem("k_hat_done")
        q_act_done, x_done = sem("q_act_done"), sem("x_done")
        block = ctx.enter_context(nc.Block())

        def ring_base(b, ahead):
            return TURN * (b + ahead)

        def output_uses(b, last):
            return TURN * (b + 1) + (0 if last else FRONT)

        @block.sync
        def _(sp):
            sp.dma_start(x_res[:, 0:TB, :], x_in[:, 0:TB, :]).then_inc(x_first, 16)
            sp.dma_start(ctx_f[:, :, :], ctx_t[0]).then_inc(ctx_in, 16)
            sp.dma_start(raw[:, 0], w_t[0]).then_inc(w_in[0], 16)
            sp.dma_start(raw[:, 1], w_t[1]).then_inc(w_in[1], 16)
            sp.dma_start(row[:, :, :], rows).then_inc(rows_in, 16)
            sp.dma_start(gate_sb[:, :], gate).then_inc(rows_in, 16)
            for n in (2, 3):
                sp.wait_ge(w_lo_done, n - 1)
                sp.dma_start(raw[:, n % 2], w_t[n]).then_inc(w_in[n % 2], 16)
            sp.dma_start(x_res[:, TB:, :], x_in[:, TB:, :]).then_inc(x_rest, 16)
            with sp.Fori(1, BATCH) as b:
                wait_apart(sp, ctx_lo_done, b, begun)
                sp.dma_start(ctx_f[:, :, :], ctx_t[bass.ds(b, 1)].rearrange("b p c t -> p (b c) t")).then_inc(ctx_in, 16)

        @block.gpsimd
        def _(pool):
            pool.memset(q_head[:, :, :, :], 0.0).then_inc(zeroed, 1)

            def context_low(b, ahead):
                pool.wait_ge(ring_ready, ring_base(b, ahead))
                pool.wait_ge(ctx_hi_done, b + ahead + 1)
                pool.tensor_tensor(ctx_lo[:, :, :], ctx_f[:, :, :], f32(ctx_hi[:, :, :]), ALU.subtract).then_inc(ctx_lo_done, 1)

            def sample(b, last):
                for u in range(UNITS):
                    att.normalise(pool, b, u)
                    if u == 0 and not last:
                        context_low(b, 1)

            context_low(0, 0)
            with pool.Fori(0, BATCH - 1) as b:
                sample(b, False)
            sample(BATCH - 1, True)

        @block.tensor
        def _(pe):
            def use(k0, k, emit, count=1):
                if not isinstance(k0, int) or k0 + k >= 2:
                    pe.wait_ge(ring_free, k0 + (k - 1))
                emit(ring[:, k % 2, :]).then_inc(ring_ready, count)

            def turned(of):
                def emit(bank):
                    for c in range(C):
                        mm = pe.transpose(bank[:, c * P:(c + 1) * P], of[:, c * P:(c + 1) * P], ident[:, :])
                    return mm
                return emit

            def projected(hi, lo, n, t):
                def emit(bank):
                    for c in range(C):
                        mm = split_product(pe, bank, (hi[:, c, t * P:(t + 1) * P], lo[:, c, t * P:(t + 1) * P]),
                                           (w_hi[n][:, c, :], w_lo[n][:, c, :]), c == 0, c == C - 1)
                    return mm
                return emit

            def front(b, ahead, u):
                k0 = ring_base(b, ahead)
                if u == 1:
                    pe.wait_ge(xn_done, TB * (b + ahead) + TB)
                    for t in range(TB):
                        use(k0, t, turned(xn[:, t, :]))
                if u in (2, 3):
                    if isinstance(b, int) and b + ahead == 0:
                        pe.wait_ge(w_lo_done, 1)
                    pe.wait_ge(ring_free, k0 + TB)
                    use(k0, u, projected(xt_hi, xt_lo, 0, u - 2))
                if 4 <= u < 8:
                    if isinstance(b, int) and b + ahead == 0:
                        pe.wait_ge(w_lo_done, u // 2)
                    pe.wait_ge(ctx_lo_done, b + ahead + 1)
                    use(k0, u, projected(ctx_hi, ctx_lo, u // 2 - 1, u % 2))
                if u == 8:
                    pe.wait_ge(k_hat_done, TB * (b + ahead) + TB)
                    for t in range(TB):
                        use(k0, 8 + t, turned(kf[:, t, :]))
                    for t in range(TB):
                        use(k0, 10 + t, turned(qf[:, t, :]), 1 + TB * (t == TB - 1 and ahead == 0))

            def attend(b, u, par):
                if u < UNITS:
                    att.scores(pe, b, u, lambda u, j: q_head[:, j, u // 2, (u % 2) * P:(u % 2 + 1) * P], lambda u, j: kt[:, u // 2, :])
                if 1 <= u <= UNITS:
                    att.turn(pe, b, u - 1)
                    if u % 2 == 0:
                        att.weigh(pe, b, u // 2 - 1, par, lambda g, j, t: v[:, par, t, (4 * g + j) * HD:(4 * g + j + 1) * HD],
                                  lambda g, j: att.o_ps[HD * j:HD * (j + 1), g % 2, 0:SEQ], 2)

            def sample(b, par, last):
                pe.wait_ge(ring_free, ring_base(b, 0) + FRONT)
                for u in range(UNITS):
                    attend(b, u, par)
                    if not last:
                        front(b, 1, u)
                if not last:
                    front(b, 1, 8)
                attend(b, UNITS, par)
                pe.wait_ge(att.o_lo_done, UNITS // 2 * (b + 1))
                k0 = output_uses(b, last)
                for t in range(TB):
                    use(k0, t, projected(o_hi, o_lo, 3, t))

            pe.wait_ge(begun, 1)
            for u in range(9):
                front(0, 0, u)
            with pe.Fori(0, BATCH // 2 - 1) as i:
                for par in range(2):
                    sample(i * 2 + par, par, False)
            sample(BATCH - 2, 0, False)
            sample(BATCH - 1, 1, True)

        @block.scalar
        def _(act):
            def context_high(b, ahead):
                act.wait_ge(ctx_in, 16 * (b + ahead) + 16)
                act.wait_ge(ring_ready, ring_base(b, ahead))
                act.activation(ctx_hi[:, :, :], ctx_f[:, :, :], ACT.Copy).then_inc(ctx_hi_done, 1)

            def front(b, ahead, u):
                k0 = ring_base(b, ahead)
                if u == 1:
                    act.wait_ge(ring_ready, k0)
                    for t in range(TB):
                        act.wait_ge(ring_ready, k0 + t + 1)
                        act.activation(xt_hi[:, :, t * P:(t + 1) * P], chunks(ring[:, t, :]),
                                       ACT.Copy).then_inc(xt_hi_done, 1)
                if 2 <= u < 6:
                    act.wait_ge(ring_free, k0 + u + 1)
                    of = (qf if u < 4 else kf)[:, u % 2, :]
                    act.wait_ge(squared, 4 * (b + ahead) + u - 2)
                    act.activation(junk[:, :], of, ACT.Square, accum_out=sq_sum[:, u // 2 - 1, u % 2:u % 2 + 1]).then_inc(squared, 1)
                if u == 8:
                    for t in range(TB):
                        act.wait_ge(ring_ready, k0 + 10 + t + 1)
                        for j in range(3):
                            ins = act.activation(q_head[HD * j:HD * (j + 1), j, :, t * P:(t + 1) * P],
                                                 chunks(ring[HD * j:HD * (j + 1), t, :]), ACT.Copy)
                        ins.then_inc(q_act_done, 1)

            def sample(b, par, last):
                for u in range(UNITS + 1):
                    if u < UNITS:
                        if u == 0:
                            act.wait_ge(q_scaled, b + 1)
                        att.exponentials(act, b, u, q_scale[:, par, u % 2:u % 2 + 1])
                    if u == UNITS and not last:
                        front(b, 1, 8)
                    if u == 0 and not last:
                        context_high(b, 1)
                    if u >= 1:
                        att.copy_turned(act, b, u - 1, 1, par)
                        if u % 2 == 0:
                            g = u // 2 - 1
                            if g == 0:
                                act.wait_ge(ring_ready, ring_base(b, 1))
                            att.output_high(act, b, g, o_hi[:, g, :], att.o_ps[:, g % 2, 0:SEQ])
                    if u < UNITS and not last:
                        front(b, 1, u)

            act.wait_ge(rows_in, 32)
            act.activation(gain[:, :], gate_sb[:, :], ACT.Tanh).then_inc(gain_done, 1)
            context_high(0, 0)
            act.wait_ge(zeroed, 1)
            for u in range(9):
                if u % 2 == 0 and u >= 2:
                    n = u // 2 - 1
                    act.wait_ge(w_in[n % 2], 16 * (n // 2) + 16)
                    act.activation(w_hi[n][:, :, :], raw[:, n % 2], ACT.Copy).then_inc(w_hi_done, 1)
                front(0, 0, u)
            with act.Fori(0, BATCH // 2 - 1) as i:
                for par in range(2):
                    sample(i * 2 + par, par, False)
            sample(BATCH - 2, 0, False)
            sample(BATCH - 1, 1, True)

        @block.vector
        def _(dve):
            chain = Chain(dve, steps, begun)

            def norm(b, ahead):
                chain.turn(STEPS * (b + ahead))
                dve.wait_ge(ring_ready, ring_base(b, ahead))
                layer_norm(dve, chain, xn, lambda t: tile_of(x_res, (b + ahead) * TB + t), small, TB, xn_done)

            def inverse_rms(out, of):
                _, _, var, rstd, tmp = small
                chain.wait()
                chain.step(dve.tensor_scalar(var[:, :], of, 1.0 / D, RMS_EPS, ALU.mult, ALU.add))
                chain.wait()
                inverse_sqrt(dve, chain, out, var[:, :], tmp[:, :])
                chain.wait()

            def front(b, ahead, u, par):
                k0 = ring_base(b, ahead)
                if u == 1:
                    for t in range(TB):
                        dve.wait_ge(xt_hi_done, TB * (b + ahead) + t + 1)
                        dve.tensor_tensor(xt_lo[:, :, t * P:(t + 1) * P], chunks(ring[:, t, :]),
                                          f32(xt_hi[:, :, t * P:(t + 1) * P]), ALU.subtract).then_inc(ring_free, 1)
                if u == 4:
                    dve.wait_ge(squared, 4 * (b + ahead) + 2)
                    inverse_rms(small[3][:, :], sq_sum[:, 0, :])
                    dve.tensor_scalar(q_scale[:, par, :], small[3][:, :], SCALE, None, ALU.mult).then_inc(q_scaled, 1)
                if u == 6:
                    dve.wait_ge(squared, 4 * (b + ahead) + 4)
                    inverse_rms(k_rstd[:, :], sq_sum[:, 1, :])
                    for t in range(TB):
                        dve.scalar_tensor_tensor(kf[:, t, :], kf[:, t, :], k_rstd[:, t:t + 1], row[:, NQ, :], ALU.mult,
                                                 ALU.mult).then_inc(k_hat_done, 1)
                if 2 <= u < 8:
                    dve.wait_ge(ring_ready, k0 + u + 1)
                    to = (qf[:, u % 2, :], kf[:, u % 2, :], v[:, par, u % 2, :])[u // 2 - 1]
                    ins = dve.tensor_tensor(to, ring[:, u % 2, :], row[:, u // 2 - 1, :], ALU.add)
                    ins.then_inc(ring_free, 1)
                if u == 8:
                    for t in range(TB):
                        dve.wait_ge(ring_ready, k0 + 8 + t + 1)
                        dve.tensor_copy(kt[:, :, t * P:(t + 1) * P], chunks(ring[:, t, :])).then_inc(ring_free, 1)
                    for t in range(TB):
                        dve.wait_ge(q_act_done, TB * (b + ahead) + t + 1)
                        dve.tensor_copy(q_head[3 * HD:, 3, :, t * P:(t + 1) * P], chunks(ring[3 * HD:, t, :])).then_inc(
                            ring_free, 1 + TB * (t == TB - 1 and ahead == 0))

            def sample(b, par, last):
                for u in range(UNITS + 1):
                    if u < UNITS:
                        att.find_peak(dve, b, u, q_scale[:, par, u % 2:u % 2 + 1])
                    if u == UNITS and not last:
                        front(b, 1, 8, 1 - par)
                    if u == 0 and not last:
                        norm(b, 1)
                    if u >= 1:
                        att.copy_turned(dve, b, u - 1, 0, par)
                        if u % 2 == 0:
                            g = u // 2 - 1
                            att.output_low(dve, b, g, o_lo[:, g, :], o_hi[:, g, :], att.o_ps[:, g % 2, 0:SEQ])
                    if u < UNITS:
                        att.invert_mass(dve, b, u)
                        if not last:
                            front(b, 1, u, 1 - par)
                k0 = output_uses(b, last)
                for t in range(TB):
                    x = tile_of(x_res, b * TB + t)
                    dve.wait_ge(ring_ready, k0 + t + 1)
                    dve.scalar_tensor_tensor(x, ring[:, t, :], gain[:, 0:1], x, ALU.mult, ALU.add).then_inc(ring_free, 1)
                    dve.wait_ge(ring_free, k0 + t + 1)
                    dve.tensor_tensor(x, x, row[:, OB, :], ALU.add).then_inc(x_done, 1)

            dve.wait_ge(x_first, 16)
            norm(0, 0)
            dve.wait_ge(rows_in, 32)
            dve.wait_ge(gain_done, 1)
            dve.tensor_scalar(row[:, OB, :], row[:, OB, :], gain[:, 0:1], None, ALU.mult).then_inc(rows_done, 1)
            dve.tensor_tensor(row[:, NQ, :], row[:, NQ, :], row[:, NK, :], ALU.mult).then_inc(rows_done, 1)
            dve.wait_ge(rows_done, 2)
            for u in range(9):
                if u % 2 == 0 and u >= 2:
                    n = u // 2 - 1
                    dve.wait_ge(w_hi_done, n + 1)
                    dve.tensor_tensor(w_lo[n][:, :, :], raw[:, n % 2], f32(w_hi[n][:, :, :]), ALU.subtract).then_inc(w_lo_done, 1)
                front(0, 0, u, 0)
            dve.wait_ge(x_rest, 16)
            with dve.Fori(0, BATCH // 2 - 1) as i:
                for par in range(2):
                    sample(i * 2 + par, par, False)
            sample(BATCH - 2, 0, False)
            sample(BATCH - 1, 1, True)


def quantised_ffn(nc, x_res, ident, begun, w_dram, ln_row, gate):
    F = 2048
    FC = F // P
    NB = F // 512
    WEIGHTS = D * F

    with ExitStack() as ctx:
        def sb(name, shape, dt=F32):
            return ctx.enter_context(nc.sbuf_tensor(f"b_{name}", shape, dt))

        def sem(name):
            return nc.alloc_semaphore(f"b_{name}")

        wq = [sb(f"wq{n}", [P, WEIGHTS // P], BF16) for n in range(3)]
        w_mean = sb("w_mean", [P, 3])
        gate_sb, gain = sb("gate_sb", [P, 1]), sb("gain", [P, 1])
        lnw = sb("lnw", [P, F])
        ident_b = sb("ident_b", [P, P], BF16)

        with ExitStack() as prep:
            raw = [prep.enter_context(nc.sbuf_tensor(f"b_raw{n}", [P, WEIGHTS // P], F32)) for n in range(3)]
            ones = prep.enter_context(nc.sbuf_tensor("b_ones", [P, P], F32))
            part, scale = (prep.enter_context(nc.sbuf_tensor(f"b_{n}", [P, 3], F32)) for n in ("part", "scale"))
            total = prep.enter_context(nc.psum_tensor("b_total", [P, 512], F32))
            w_in = [sem(f"w_in{n}") for n in range(3)]
            small_in, summed, ones_done, total_ready, scaled, spread, rounded = (
                sem(n) for n in ("small_in", "summed", "ones_done", "total_ready", "scaled", "spread", "rounded"))
            block = prep.enter_context(nc.Block())

            @block.sync
            def _(sp):
                for n in range(3):
                    sp.dma_start(raw[n][:, :], w_dram[n]).then_inc(w_in[n], 16)
                sp.dma_start(gate_sb[:, :], gate).then_inc(small_in, 16)
                sp.dma_start(lnw[:, :], ln_row).then_inc(small_in, 16)

            @block.scalar
            def _(act):
                act.wait_ge(w_in[0], 16)
                act.activation(wq[0][:, :], raw[0][:, :], ACT.Abs, accum_out=part[:, 0:1]).then_inc(summed, 1)
                act.wait_ge(w_in[2], 16)
                act.activation(wq[2][:, :], raw[2][:, :], ACT.Abs, accum_out=part[:, 2:3]).then_inc(summed, 1)
                act.wait_ge(small_in, 32)
                act.activation(gain[:, :], gate_sb[:, :], ACT.Tanh)
                for n in range(3):
                    act.wait_ge(spread, 2 * n + 2)
                    act.activation(wq[n][:, :], raw[n][:, :], ACT.Copy, bias=-ROUND).then_inc(rounded, 1)

            @block.tensor
            def _(pe):
                pe.wait_ge(ones_done, 1)
                pe.wait_ge(summed, 3)
                pe.matmul(total[:, 0:3], ones[:, :], part[:, :], start=True, stop=True).then_inc(total_ready, 1)

            @block.vector
            def _(dve):
                dve.memset(ones[:, :], 1.0).then_inc(ones_done, 1)
                dve.tensor_copy(ident_b[:, :], ident[:, :])
                dve.wait_ge(w_in[1], 16)
                dve.tensor_reduce(part[:, 1:2], raw[1][:, :], AX.X, ALU.add, apply_absolute_value=True).then_inc(summed, 1)
                dve.wait_ge(total_ready, 1)
                dve.tensor_scalar(w_mean[:, :], total[:, 0:3], 1.0 / WEIGHTS, 1e-5, ALU.mult, ALU.max).then_inc(scaled, 1)
                dve.wait_ge(scaled, 1)
                dve.reciprocal(scale[:, :], w_mean[:, :]).then_inc(scaled, 1)
                dve.wait_ge(scaled, 2)
                for n in range(3):
                    dve.tensor_scalar(raw[n][:, :], raw[n][:, :], scale[:, n:n + 1], 1.0, ALU.mult, ALU.min).then_inc(spread, 1)
                    dve.wait_ge(spread, 2 * n + 1)
                    dve.tensor_scalar(raw[n][:, :], raw[n][:, :], -1.0, ROUND, ALU.max, ALU.add).then_inc(spread, 1)

        xn = sb("xn", [P, TB, D])
        xq = sb("xq", [P, TB, D], BF16)
        xqt = sb("xqt", [P, C, TB, P], BF16)
        sg = sb("sg", [P, 2, 512])
        h = sb("h", [P, 2, F])
        hw = sb("hw", [P, 2, F])
        hq = sb("hq", [P, 2, F], BF16)
        hqt = sb("hqt", [P, FC, P], BF16)
        junk = sb("junk", [P, 512], BF16)
        small = (sb("stats", [P, TB, 6]), sb("agg", [P, TB, 2]), sb("var", [P, TB]), sb("rstd", [P, TB]), sb("tmp", [P, TB]))
        x_peak, x_scale = sb("x_peak", [P, TB]), sb("x_scale", [P, TB])
        up_scale, gate_scale = sb("up_scale", [P, TB]), sb("gate_scale", [P, TB])
        sq_sum, h_peak = sb("sq_sum", [P, 2, NB]), sb("h_peak", [P, 2, NB])
        sq_all, h_all, h_rstd, h_scale, down_scale = (sb(n, [P, 2]) for n in ("sq_all", "h_all", "h_rstd", "h_scale", "down_scale"))
        g_ps = ctx.enter_context(nc.psum_tensor("b_g_ps", [P, 2, 512], F32))
        u_ps = ctx.enter_context(nc.psum_tensor("b_u_ps", [P, 2, 512], F32))
        xt_ps = ctx.enter_context(nc.psum_tensor("b_xt_ps", [P, C, TB, P], BF16))
        ht_ps = ctx.enter_context(nc.psum_tensor("b_ht_ps", [P, 2, FC // 2, P], BF16))
        d_ps = ctx.enter_context(nc.psum_tensor("b_d_ps", [P, 512], F32))
        steps, xn_done, spread_x, xq_done, xt_ready, xqt_done = (sem(n) for n in ("steps", "xn_done", "spread_x", "xq_done", "xt_ready", "xqt_done"))
        g_ready, u_ready, sg_done, h_done, hw_done, squared = (sem(n) for n in ("g_ready", "u_ready", "sg_done", "h_done", "hw_done", "squared"))
        spread_h, hq_done, ht_ready, hqt_dve, hqt_act, d_ready, x_done = (
            sem(n) for n in ("spread_h", "hq_done", "ht_ready", "hqt_dve", "hqt_act", "d_ready", "x_done"))
        scales_half, scales_done, down_done = sem("scales_half"), sem("scales_done"), sem("down_done")
        down_gain = sb("down_gain", [P, 1])
        block = ctx.enter_context(nc.Block())
        w_gate, w_up = (wq[n][:, :].rearrange("p (c n) -> p c n", c=C) for n in (0, 1))
        w_down = wq[2][:, :].rearrange("p (k n) -> p k n", k=FC)
        PAIRS = TILES // 2

        @block.gpsimd
        def _(pool):
            with pool.Fori(0, PAIRS) as i:
                for par in range(2):
                    n = i * 2 + par
                    for k in range(NB):
                        pool.wait_ge(hq_done, i * 2)
                        pool.wait_ge(h_done, n * NB + k + 1)
                        cols = slice(k * 512, (k + 1) * 512)
                        pool.tensor_tensor(hw[:, par, cols], h[:, par, cols], lnw[:, cols], ALU.mult).then_inc(hw_done, 1)

        @block.tensor
        def _(pe):
            def turn_x(i):
                pe.wait_ge(xq_done, i + 1)
                pe.wait_ge(xqt_done, i)
                for t in range(TB):
                    for c in range(C):
                        mm = pe.transpose(xt_ps[:, c, t, :], xq[:, t, c * P:(c + 1) * P], ident_b[:, :])
                mm.then_inc(xt_ready, 1)

            def up(i, t):
                n = i * 2 + t
                pe.wait_ge(xqt_done, i + 1)
                for k in range(NB):
                    for ps, w, free, ready in ((g_ps, w_gate, sg_done, g_ready), (u_ps, w_up, h_done, u_ready)):
                        if not isinstance(n, int) or n * NB + k >= 2:
                            pe.wait_ge(free, n * NB + (k - 1))
                        for c in range(C):
                            mm = pe.matmul(ps[:, k % 2, :], xqt[:, c, t, :], w[:, c, k * 512:(k + 1) * 512], start=c == 0, stop=c == C - 1)
                        mm.then_inc(ready, 1)

            def down(n, par):
                pe.wait_ge(hq_done, n + 1)
                pe.wait_ge(hqt_dve, n)
                pe.wait_ge(hqt_act, n)
                for k in range(FC):
                    mm = pe.transpose(ht_ps[:, k // 8, k % 8, :], hq[:, par, k * P:(k + 1) * P], ident_b[:, :])
                    if k % 8 == 7:
                        mm.then_inc(ht_ready, 1)
                pe.wait_ge(x_done, n)
                for k in range(FC):
                    if k % 8 == 0:
                        pe.wait_ge((hqt_dve, hqt_act)[k // 8], n + 1)
                    mm = pe.matmul(d_ps[:, :], hqt[:, k, :], w_down[:, k, :], start=k == 0, stop=k == FC - 1)
                mm.then_inc(d_ready, 1)

            def pair(i, first, last):
                up(i, 0)
                if not first:
                    down(i * 2 - 1, 1)
                up(i, 1)
                if not last:
                    turn_x(i + 1)
                down(i * 2, 0)

            turn_x(0)
            pair(0, True, False)
            with pe.Fori(1, PAIRS - 1) as i:
                pair(i, False, False)
            pair(PAIRS - 1, False, True)
            down(TILES - 1, 1)

        @block.scalar
        def _(act):
            def round_x(i):
                act.wait_ge(spread_x, i * TB + TB)
                act.wait_ge(xt_ready, i)
                act.activation(xq[:, :, :], xn[:, :, :], ACT.Copy, bias=-ROUND).then_inc(xq_done, 1)

            def copy_x(i, first):
                act.wait_ge(xt_ready, i + 1)
                if not first:
                    act.wait_ge(u_ready, i * 2 * NB)
                act.activation(xqt[:, :, :, :], xt_ps[:, :, :, :], ACT.Copy).then_inc(xqt_done, 1)

            def up(i, t):
                n = i * 2 + t
                act.wait_ge(scales_done, i + 1)
                for k in range(NB):
                    act.wait_ge(g_ready, n * NB + k + 1)
                    if not isinstance(n, int) or n * NB + k >= 2:
                        act.wait_ge(h_done, n * NB + (k - 1))
                    act.activation(sg[:, k % 2, :], g_ps[:, k % 2, :], ACT.Silu, scale=gate_scale[:, t:t + 1]).then_inc(sg_done, 1)
                for k in range(NB):
                    act.wait_ge(h_done, n * NB + k + 1)
                    act.wait_ge(squared, n * NB + k)
                    act.activation(junk[:, :], h[:, t, k * 512:(k + 1) * 512], ACT.Square, accum_out=sq_sum[:, t, k:k + 1]).then_inc(squared, 1)

            def round_h(n, par):
                act.wait_ge(spread_h, n + 1)
                act.activation(hq[:, par, :], hw[:, par, :], ACT.Copy, bias=-ROUND).then_inc(hq_done, 1)

            def copy_h(n):
                act.wait_ge(ht_ready, n * 2 + 2)
                act.wait_ge(d_ready, n)
                act.activation(hqt[:, FC // 2:, :], ht_ps[:, 1], ACT.Copy).then_inc(hqt_act, 1)

            def pair(i, first, last):
                up(i, 0)
                if not first:
                    copy_h(i * 2 - 1)
                round_h(i * 2, 0)
                if not last:
                    round_x(i + 1)
                up(i, 1)
                if not last:
                    copy_x(i + 1, False)
                copy_h(i * 2)
                round_h(i * 2 + 1, 1)

            round_x(0)
            copy_x(0, True)
            pair(0, True, False)
            with act.Fori(1, PAIRS - 1) as i:
                pair(i, False, False)
            pair(PAIRS - 1, False, True)
            copy_h(TILES - 1)

        @block.vector
        def _(dve):
            chain = Chain(dve, steps, begun)
            X_STEPS = layer_norm_steps(TB) + 3
            H_STEPS = INVERSE_SQRT_STEPS + 7
            PAIR_STEPS = X_STEPS + 2 * H_STEPS

            def quantise_x(i):
                dve.wait_ge(xq_done, i)
                layer_norm(dve, chain, xn, lambda t: tile_of(x_res, i * TB + t), small, TB, xn_done)
                dve.wait_ge(xn_done, i * TB + TB)
                chain.step(dve.tensor_reduce(x_peak[:, :], xn[:, :, :], AX.X, ALU.max, apply_absolute_value=True))
                chain.wait()
                chain.step(dve.tensor_scalar(x_peak[:, :], x_peak[:, :], 1e-5, 1.0 / 127.0, ALU.max, ALU.mult))
                chain.wait()
                chain.step(dve.reciprocal(x_scale[:, :], x_peak[:, :]))
                chain.wait()
                for t in range(TB):
                    dve.tensor_scalar(xn[:, t, :], xn[:, t, :], x_scale[:, t:t + 1], ROUND, ALU.mult, ALU.add).then_inc(spread_x, 1)

            def scales(i):
                dve.wait_ge(squared, i * 2 * NB)
                dve.tensor_scalar(up_scale[:, :], x_peak[:, :], w_mean[:, 1:2], None, ALU.mult).then_inc(scales_half, 1)
                dve.tensor_scalar(gate_scale[:, :], x_peak[:, :], w_mean[:, 0:1], None, ALU.mult).then_inc(scales_done, 1)

            def up(i, t):
                n = i * 2 + t
                dve.wait_ge(scales_half, i + 1)
                dve.wait_ge(squared, i * 2 * NB)
                dve.wait_ge(hw_done, i * 2 * NB)
                for k in range(NB):
                    dve.wait_ge(u_ready, n * NB + k + 1)
                    dve.wait_ge(sg_done, n * NB + k + 1)
                    cols = slice(k * 512, (k + 1) * 512)
                    dve.scalar_tensor_tensor(h[:, t, cols], u_ps[:, k % 2, :], up_scale[:, t:t + 1], sg[:, k % 2, :],
                                             ALU.mult, ALU.mult).then_inc(h_done, 1)
                for k in range(NB):
                    dve.wait_ge(hw_done, n * NB + k + 1)
                    ins = dve.tensor_reduce(h_peak[:, t, k:k + 1], hw[:, t, k * 512:(k + 1) * 512], AX.X, ALU.max, apply_absolute_value=True)
                chain.step(ins)

            def quantise_h(n, t):
                _, _, var, _, tmp = small
                one = slice(t, t + 1)
                dve.wait_ge(squared, n * NB + NB)
                chain.step(dve.tensor_reduce(sq_all[:, one], sq_sum[:, t, :], AX.X, ALU.add))
                chain.wait()
                chain.step(dve.tensor_scalar(var[:, 0:1], sq_all[:, one], 1.0 / F, RMS_EPS, ALU.mult, ALU.add))
                chain.wait()
                inverse_sqrt(dve, chain, h_rstd[:, one], var[:, 0:1], tmp[:, 0:1])
                chain.wait()
                chain.step(dve.tensor_reduce(h_all[:, one], h_peak[:, t, :], AX.X, ALU.max))
                chain.wait()
                chain.step(dve.tensor_scalar(h_all[:, one], h_all[:, one], h_rstd[:, one], 1e-5, ALU.mult, ALU.max))
                chain.wait()
                chain.step(dve.reciprocal(h_scale[:, one], h_all[:, one]))
                dve.tensor_scalar(down_scale[:, one], h_all[:, one], down_gain[:, 0:1], None, ALU.mult).then_inc(down_done, 1)
                chain.wait()
                chain.step(dve.tensor_scalar(h_scale[:, one], h_scale[:, one], h_rstd[:, one], 127.0, ALU.mult, ALU.mult))
                chain.wait()
                dve.tensor_scalar(hw[:, t, :], hw[:, t, :], h_scale[:, one], ROUND, ALU.mult, ALU.add).then_inc(spread_h, 1)

            def copy_h(n):
                dve.wait_ge(ht_ready, n * 2 + 1)
                dve.wait_ge(d_ready, n)
                dve.tensor_copy(hqt[:, 0:FC // 2, :], ht_ps[:, 0]).then_inc(hqt_dve, 1)

            def add_to_x(n, par):
                dve.wait_ge(d_ready, n + 1)
                dve.wait_ge(down_done, n + 1)
                x = tile_of(x_res, n)
                dve.scalar_tensor_tensor(x, d_ps[:, :], down_scale[:, par:par + 1], x, ALU.mult, ALU.add).then_inc(x_done, 1)

            def pair(i, first, last):
                chain.turn(PAIR_STEPS * i + (X_STEPS + 1))
                scales(i)
                up(i, 0)
                if not first:
                    copy_h(i * 2 - 1)
                    add_to_x(i * 2 - 1, 1)
                quantise_h(i * 2, 0)
                if not last:
                    quantise_x(i + 1)
                up(i, 1)
                copy_h(i * 2)
                quantise_h(i * 2 + 1, 1)
                add_to_x(i * 2, 0)

            chain.turn(0)
            chain.step(dve.tensor_scalar(down_gain[:, :], w_mean[:, 2:3], gain[:, 0:1], 1.0 / 127.0, ALU.mult, ALU.mult))
            quantise_x(0)
            pair(0, True, False)
            with dve.Fori(1, PAIRS - 1) as i:
                pair(i, False, False)
            pair(PAIRS - 1, False, True)
            copy_h(TILES - 1)
            add_to_x(TILES - 1, 1)


def cross_attention(nc, x_res, ident, begun, xnt_dram, ctx_t, w_t, gate):
    HD = 2048 // NH
    GROUPS = NH // 4
    SCALE = float(HD) ** -0.5
    FRONT, TURN = 6, 6 + TB

    with ExitStack() as ctx:
        def sb(name, shape, dt=F32):
            return ctx.enter_context(nc.sbuf_tensor(f"cn_{name}", shape, dt))

        def sem(name):
            return nc.alloc_semaphore(f"cn_{name}")

        xn, xt = sb("xn", [P, 2, TB, D]), sb("xt", [P, 2, C, SEQ])
        small = (sb("stats", [P, TB, 6]), sb("agg", [P, TB, 2]), sb("var", [P, TB]), sb("rstd", [P, TB]), sb("tmp", [P, TB]))
        bank = ctx.enter_context(nc.psum_tensor("cn_bank", [P, 2, TB, 512], F32))
        steps, xn_done, turned, copied, stored = sem("steps"), sem("xn_done"), sem("turned"), sem("copied"), [sem("stored0"), sem("stored1")]
        block = ctx.enter_context(nc.Block())

        @block.vector
        def _(dve):
            chain = Chain(dve, steps, begun)
            with dve.Fori(0, BATCH // 2) as i:
                for par in range(2):
                    b = i * 2 + par
                    chain.turn(layer_norm_steps(TB) * b)
                    dve.wait_ge(turned, i * 2)
                    layer_norm(dve, chain, xn[:, par], lambda t: tile_of(x_res, b * TB + t), small, TB, xn_done)

        @block.tensor
        def _(pe):
            with pe.Fori(0, BATCH // 2) as i:
                for par in range(2):
                    b = i * 2 + par
                    pe.wait_ge(xn_done, b * TB + TB)
                    pe.wait_ge(copied, i * 2)
                    for t in range(TB):
                        for c in range(C):
                            mm = pe.transpose(bank[:, par, t, c * P:(c + 1) * P], xn[:, par, t, c * P:(c + 1) * P], ident[:, :])
                    mm.then_inc(turned, 1)

        @block.scalar
        def _(act):
            with act.Fori(0, BATCH // 2) as i:
                for par in range(2):
                    b = i * 2 + par
                    act.wait_ge(turned, b + 1)
                    act.wait_ge(stored[par], i * 16)
                    for t in range(TB):
                        ins = act.activation(xt[:, par, :, t * P:(t + 1) * P], chunks(bank[:, par, t, :]), ACT.Copy)
                    ins.then_inc(copied, 1)

        @block.sync
        def _(sp):
            with sp.Fori(0, BATCH // 2) as i:
                for par in range(2):
                    b = i * 2 + par
                    wait_apart(sp, copied, b + 1, begun)
                    sp.dma_start(xnt_dram[bass.ds(b, 1)].rearrange("b p c t -> p (b c) t"), xt[:, par]).then_inc(stored[par], 16)
            for par in range(2):
                sp.wait_ge(stored[par], 16 * BATCH // 2)

    with ExitStack() as ctx:
        def sb(name, shape, dt=F32):
            return ctx.enter_context(nc.sbuf_tensor(f"c_{name}", shape, dt))

        def sem(name):
            return nc.alloc_semaphore(f"c_{name}")

        w_hi = [sb(f"w_hi{n}", [P, C, D], F32R) for n in range(4)]
        w_lo = [sb(f"w_lo{n}", [P, C, D], F32R) for n in range(4)]
        raw = sb("raw", [P, 2, C, D])
        gate_sb, gain = sb("gate_sb", [P, 1]), sb("gain", [P, 1])
        xt_f, ctx_f = sb("xt_f", [P, C, SEQ]), sb("ctx_f", [P, C, SEQ])
        xt_hi, xt_lo = sb("xt_hi", [P, C, SEQ], F32R), sb("xt_lo", [P, C, SEQ], F32R)
        ctx_hi, ctx_lo = sb("ctx_hi", [P, C, SEQ], F32R), sb("ctx_lo", [P, C, SEQ], F32R)
        qt, kt = sb("qt", [P, 2, 4, SEQ]), sb("kt", [P, 2, 4, SEQ])
        v = sb("v", [P, 2, TB, 4 * HD])
        o_hi, o_lo = sb("o_hi", [P, 4, SEQ], F32R), sb("o_lo", [P, 4, SEQ], F32R)
        att = Attention(nc, ctx, "c", begun, ident, TB, SCALE, 1)
        ring = ctx.enter_context(nc.psum_tensor("c_ring", [P, 2, 512], F32))
        gate_in, w_in, w_hi_done, w_lo_done, gain_done = sem("gate_in"), [sem("w_in0"), sem("w_in1")], sem("w_hi_done"), sem("w_lo_done"), sem("gain_done")
        xt_in, ctx_in, xt_hi_done, xt_lo_done = sem("xt_in"), sem("ctx_in"), sem("xt_hi_done"), sem("xt_lo_done")
        ctx_hi_done, ctx_lo_done, ring_ready, ring_free = sem("ctx_hi_done"), sem("ctx_lo_done"), sem("ring_ready"), sem("ring_free")
        block = ctx.enter_context(nc.Block())
        USES = TURN * BATCH

        def front_base(g, b):
            return g * USES + (b * TURN + FRONT)

        def turns(eng, head, turn):
            with eng.Fori(0, GROUPS) as g:
                head(g)
                with eng.Fori(0, BATCH // 2 - 1) as i:
                    for par in range(2):
                        turn(g, i * 2 + par, par, False)
                turn(g, BATCH - 2, 0, False)
                turn(g, BATCH - 1, 1, True)

        @block.sync
        def _(sp):
            sp.dma_start(gate_sb[:, :], gate).then_inc(gate_in, 16)

            def load_weights(g, n):
                if not isinstance(g, int) or 4 * g + n >= 2:
                    wait_apart(sp, w_lo_done, g * 4 + (n - 1), begun)
                sp.dma_start(raw[:, n % 2], w_t[g, n] if isinstance(g, int) else
                             w_t[bass.ds(g, 1), n].rearrange("g p c n -> p (g c) n")).then_inc(w_in[n % 2], 16)

            def load_inputs(n, b):
                if not isinstance(n, int) or n > 0:
                    wait_apart(sp, xt_lo_done, n, begun)
                of = xnt_dram[b] if isinstance(b, int) else xnt_dram[bass.ds(b, 1)].rearrange("b p c t -> p (b c) t")
                sp.dma_start(xt_f[:, :, :], of).then_inc(xt_in, 16)
                if not isinstance(n, int) or n > 0:
                    wait_apart(sp, ctx_lo_done, n, begun)
                of = ctx_t[b] if isinstance(b, int) else ctx_t[bass.ds(b, 1)].rearrange("b p c t -> p (b c) t")
                sp.dma_start(ctx_f[:, :, :], of).then_inc(ctx_in, 16)

            load_weights(0, 0)
            load_inputs(0, 0)
            load_weights(0, 1)

            def head(g):
                load_weights(g, 2)
                load_inputs(g * BATCH + 1, 1)
                load_weights(g, 3)

            def turn(g, b, par, last):
                if not last:
                    load_inputs(g * BATCH + b + 2, (b + 2) % BATCH if isinstance(b, int) else b + 2)

            def group(g):
                head(g)
                with sp.Fori(0, BATCH // 2 - 1) as i:
                    for par in range(2):
                        turn(g, i * 2 + par, par, False)
                turn(g, BATCH - 2, 0, False)

            with sp.Fori(0, GROUPS - 1) as g:
                group(g)
                load_weights(g + 1, 0)
                load_weights(g + 1, 1)
            group(GROUPS - 1)

        @block.gpsimd
        def _(pool):
            def inputs_low(n):
                pool.wait_ge(xt_hi_done, n + 1)
                pool.tensor_tensor(xt_lo[:, :, :], xt_f[:, :, :], f32(xt_hi[:, :, :]), ALU.subtract).then_inc(xt_lo_done, 1)

            def context_low(n):
                pool.wait_ge(ctx_hi_done, n + 1)
                pool.tensor_tensor(ctx_lo[:, :, :], ctx_f[:, :, :], f32(ctx_hi[:, :, :]), ALU.subtract).then_inc(ctx_lo_done, 1)

            inputs_low(0)
            context_low(0)

            def head(g):
                inputs_low(g * BATCH + 1)
                context_low(g * BATCH + 1)

            def turn(g, b, par, last):
                s = g * BATCH + b
                att.normalise(pool, s, 0)
                att.normalise(pool, s, 1)
                if not last:
                    inputs_low(s + 2)
                    context_low(s + 2)

            turns(pool, head, turn)

        @block.tensor
        def _(pe):
            def use(k0, k, emit, first=False):
                pe.wait_ge(ring_free, k0 if first else k0 + (k - 1))
                emit(ring[:, k % 2, :]).then_inc(ring_ready, 1)

            def heads(n, hi, lo, k):
                def emit(bank):
                    for h in range(2):
                        cols = slice((2 * k + h) * HD, (2 * k + h + 1) * HD)
                        for c in range(C):
                            mm = split_product(pe, bank[:, h * SEQ:(h + 1) * SEQ], (w_hi[n][:, c, cols], w_lo[n][:, c, cols]),
                                               (hi[:, c, :], lo[:, c, :]), c == 0, c == C - 1)
                    return mm
                return emit

            def tokens(n, hi, lo, t):
                def emit(bank):
                    for c in range(C):
                        mm = split_product(pe, bank, (hi[:, c, t * P:(t + 1) * P], lo[:, c, t * P:(t + 1) * P]),
                                           (w_hi[n][:, c, :], w_lo[n][:, c, :]), c == 0, c == C - 1)
                    return mm
                return emit

            def front(k0, k, n, first=False):
                if k == 0:
                    pe.wait_ge(xt_lo_done, n + 1)
                    use(k0, 0, heads(0, xt_hi, xt_lo, 0), first)
                if k == 1:
                    use(k0, 1, heads(0, xt_hi, xt_lo, 1))
                if k == 2:
                    pe.wait_ge(ctx_lo_done, n + 1)
                if k in (2, 3):
                    use(k0, k, heads(1, ctx_hi, ctx_lo, k - 2))
                if k in (4, 5):
                    use(k0, k, tokens(2, ctx_hi, ctx_lo, k - 4))

            def head(g):
                for k in range(FRONT):
                    if k % 2 == 0:
                        pe.wait_ge(w_lo_done, g * 4 + (k // 2 + 1))
                    front(g * USES, k, g * BATCH, k == 0)

            def turn(g, b, par, last):
                s, k0 = g * BATCH + b, front_base(g, b)

                def fronts(*ks):
                    if not last:
                        for k in ks:
                            front(k0, k, s + 1)

                q_of, k_of = (lambda u, j: qt[:, par, j, u * P:(u + 1) * P]), (lambda u, j: kt[:, par, j, :])
                pe.wait_ge(ring_free, k0)
                att.scores(pe, s, 0, q_of, k_of)
                fronts(0, 1)
                att.scores(pe, s, 1, q_of, k_of)
                att.turn(pe, s, 0)
                fronts(2, 3)
                att.turn(pe, s, 1)
                fronts(4)
                att.weigh(pe, s, 0, par, lambda g_, j, t: v[:, par, t, j * HD:(j + 1) * HD],
                          lambda g_, j: att.o_ps[:, j // 2, (j % 2) * SEQ:(j % 2 + 1) * SEQ], 1)
                fronts(5)
                pe.wait_ge(w_lo_done, g * 4 + 4)
                pe.wait_ge(att.o_lo_done, s + 1)
                for t in range(TB):
                    use(k0 + (0 if last else FRONT), t, tokens(3, o_hi, o_lo, t))

            turns(pe, head, turn)

        @block.scalar
        def _(act):
            def inputs_high(n, after):
                act.wait_ge(xt_in, n * 16 + 16)
                if after is not None:
                    act.wait_ge(ring_ready, after)
                    act.wait_ge(xt_lo_done, n)
                act.activation(xt_hi[:, :, :], xt_f[:, :, :], ACT.Copy).then_inc(xt_hi_done, 1)

            def context_high(n, after):
                act.wait_ge(ctx_in, n * 16 + 16)
                if after is not None:
                    act.wait_ge(ring_ready, after)
                act.activation(ctx_hi[:, :, :], ctx_f[:, :, :], ACT.Copy).then_inc(ctx_hi_done, 1)

            act.wait_ge(gate_in, 16)
            act.activation(gain[:, :], gate_sb[:, :], ACT.Tanh).then_inc(gain_done, 1)
            inputs_high(0, None)
            context_high(0, None)

            def head(g):
                act.wait_ge(ring_ready, g * USES)
                for n in range(4):
                    act.wait_ge(w_in[n % 2], g * 32 + (16 * (n // 2) + 16))
                    act.activation(w_hi[n][:, :, :], raw[:, n % 2], ACT.Copy).then_inc(w_hi_done, 1)
                inputs_high(g * BATCH + 1, g * USES + 2)
                context_high(g * BATCH + 1, g * USES + FRONT)

            def turn(g, b, par, last):
                s, k0 = g * BATCH + b, front_base(g, b)
                att.exponentials(act, s, 0)
                att.exponentials(act, s, 1)
                if not last:
                    inputs_high(s + 2, k0 + 2)
                att.copy_turned(act, s, 0, 1, par)
                att.copy_turned(act, s, 1, 1, par)
                act.wait_ge(ring_ready, k0)
                att.output_high(act, s, 0, o_hi[:, :, :], att.o_ps[:, :, :].rearrange("p k (j q) -> p (k j) q", j=2))
                if not last:
                    context_high(s + 2, k0 + FRONT)

            turns(act, head, turn)

        @block.vector
        def _(dve):
            def front(k0, k, par):
                dve.wait_ge(ring_ready, k0 + k + 1)
                to = ((qt, kt)[k // 2][:, par, 2 * (k % 2):2 * (k % 2) + 2, :].rearrange("p j q -> p (j q)") if k < 4
                      else v[:, par, k - 4, :])
                dve.tensor_copy(to, ring[:, k % 2, :]).then_inc(ring_free, 1)

            dve.wait_ge(gain_done, 1)

            def head(g):
                for n in range(4):
                    dve.wait_ge(w_hi_done, g * 4 + n + 1)
                    dve.tensor_tensor(w_lo[n][:, :, :], raw[:, n % 2], f32(w_hi[n][:, :, :]), ALU.subtract).then_inc(w_lo_done, 1)
                for k in range(FRONT):
                    front(g * USES, k, 0)

            def turn(g, b, par, last):
                s, k0 = g * BATCH + b, front_base(g, b)

                def fronts(*ks):
                    if not last:
                        for k in ks:
                            front(k0, k, 1 - par)

                att.find_peak(dve, s, 0)
                fronts(0)
                att.invert_mass(dve, s, 0)
                fronts(1)
                att.find_peak(dve, s, 1)
                att.copy_turned(dve, s, 0, 0, par)
                fronts(2)
                att.invert_mass(dve, s, 1)
                fronts(3)
                att.copy_turned(dve, s, 1, 0, par)
                fronts(4)
                att.output_low(dve, s, 0, o_lo[:, :, :], o_hi[:, :, :], att.o_ps[:, :, :].rearrange("p k (j q) -> p (k j) q", j=2))
                fronts(5)
                for t in range(TB):
                    x = tile_of(x_res, b * TB + t)
                    dve.wait_ge(ring_ready, k0 + (0 if last else FRONT) + t + 1)
                    dve.scalar_tensor_tensor(x, ring[:, t, :], gain[:, 0:1], x, ALU.mult, ALU.add).then_inc(ring_free, 1)

            turns(dve, head, turn)


def latent_attention(nc, x_res, h_res, ident, begun, w_dram, ln_row, rope_dram):
    HD = D // NH
    RD = HD // 2
    HALF = NH * RD
    SCALE = float(HD) ** -0.5
    UNITS = NH // 4 * TB
    FRONT = 14
    TURN = FRONT + TB
    STEPS = layer_norm_steps(TB) + 1 + INVERSE_SQRT_STEPS
    WIDTHS = (("kv_d", C * P), ("q_d", C * P), ("k_u", HALF), ("q_u", 2 * HALF), ("v_u", D), ("rope_k", C * HALF), ("o", C * D))
    W = sum(n for _, n in WIDTHS)

    with ExitStack() as ctx:
        def sb(name, shape, dt=F32):
            return ctx.enter_context(nc.sbuf_tensor(f"d_{name}", shape, dt))

        def sem(name):
            return nc.alloc_semaphore(f"d_{name}")

        w_hi, w_lo = sb("w_hi", [P, W], F32R), sb("w_lo", [P, W], F32R)
        ln = sb("ln_row", [P, D])
        rope = sb("rope_sb", [P, 2, TB, RD])
        ident_b, mask = sb("ident_b", [P, P], BF16), sb("mask", [P, P], BF16)

        with ExitStack() as prep:
            raw = prep.enter_context(nc.sbuf_tensor("d_raw", [P, W], F32))
            blank = prep.enter_context(nc.sbuf_tensor("d_blank", [P, P], F32))
            w_in, small_in, w_hi_done, zeroed, masked = (sem(n) for n in ("w_in", "small_in", "w_hi_done", "zeroed", "masked"))
            block = prep.enter_context(nc.Block())

            @block.sync
            def _(sp):
                sp.dma_start(raw[:, :], w_dram).then_inc(w_in, 16)
                sp.dma_start(ln[:, :], ln_row).then_inc(small_in, 16)
                sp.dma_start(rope[:, :, :, :], rope_dram).then_inc(small_in, 16)
                sp.wait_ge(small_in, 32)

            @block.gpsimd
            def _(pool):
                pool.memset(blank[:, :], 0.0).then_inc(zeroed, 1)
                pool.wait_ge(zeroed, 1)
                pool.affine_select(out=blank[:, :], in_=blank[:, :], compare_op=ALU.is_ge, fill=-1e30, base=0,
                                   pattern=[[-1, P]], channel_multiplier=1).then_inc(masked, 1)

            @block.scalar
            def _(act):
                act.wait_ge(w_in, 16)
                act.activation(w_hi[:, :], raw[:, :], ACT.Copy).then_inc(w_hi_done, 1)

            @block.vector
            def _(dve):
                dve.wait_ge(masked, 1)
                dve.tensor_copy(mask[:, :], blank[:, :])
                dve.tensor_copy(ident_b[:, :], ident[:, :])
                dve.wait_ge(w_hi_done, 1)
                dve.tensor_tensor(w_lo[:, :], raw[:, :], f32(w_hi[:, :]), ALU.subtract)

        at_col, parts = 0, {}
        for name, n in WIDTHS:
            parts[name] = [w[:, at_col:at_col + n] for w in (w_hi, w_lo)]
            at_col += n
        for name in ("kv_d", "q_d", "rope_k", "o"):
            parts[name] = [w.rearrange("p (c n) -> p c n", c=C) for w in parts[name]]

        a = sb("a", [P, TB, D])
        at_hi, at_lo = sb("at_hi", [P, C, SEQ], F32R), sb("at_lo", [P, C, SEQ], F32R)
        lat_hi, lat_lo = sb("lat_hi", [P, 2, SEQ], F32R), sb("lat_lo", [P, 2, SEQ], F32R)
        kf, qf = sb("kf", [P, TB, NH, HD]), sb("qf", [P, TB, NH, HD])
        rot = sb("rot", [P, 2, NH, RD])
        q_head = sb("q_head", [P, 4, C, SEQ])
        kt = sb("kt", [P, C, SEQ])
        v = sb("v", [P, 2, TB, D])
        o_hi, o_lo = sb("o_hi", [P, C, SEQ], F32R), sb("o_lo", [P, C, SEQ], F32R)
        junk = sb("junk", [P, D], BF16)
        small = (sb("stats", [P, TB, 6]), sb("agg", [P, TB, 2]), sb("var", [P, TB]), sb("rstd", [P, TB]), sb("tmp", [P, TB]))
        sq_sum, a_rstd = sb("sq_sum", [P, TB]), sb("a_rstd", [P, TB])
        att = Attention(nc, ctx, "d", begun, ident, UNITS, SCALE, 1, causal=True)
        ring = ctx.enter_context(nc.psum_tensor("d_ring", [P, 2, 512], F32))
        zeroed2, steps, y_done, squared, a_done = (sem(n) for n in ("zeroed2", "steps", "y_done", "squared", "a_done"))
        ring_ready, ring_free, hi_done, turned_k, rotated, q_act_done = (
            sem(n) for n in ("ring_ready", "ring_free", "hi_done", "turned_k", "rotated", "q_act_done"))
        plain_done, products = sem("plain_done"), sem("products")
        block = ctx.enter_context(nc.Block())

        def ring_base(b, ahead):
            return TURN * (b + ahead)

        def output_uses(b, last):
            return TURN * (b + 1) + (0 if last else FRONT)

        @block.gpsimd
        def _(pool):
            pool.memset(q_head[:, :, :, :], 0.0)
            pool.memset(att.prob_t[:, :, 1, :, 0:P], 0.0).then_inc(zeroed2, 1)

            def sample(b):
                for u in range(UNITS):
                    att.normalise(pool, b, u)

            with pool.Fori(0, BATCH) as b:
                sample(b)

        @block.tensor
        def _(pe):
            def use(k0, k, emit, count=1):
                if not isinstance(k0, int) or k0 + k >= 2:
                    pe.wait_ge(ring_free, k0 + (k - 1))
                emit(ring[:, k % 2, :]).then_inc(ring_ready, count)

            def turned(of):
                def emit(bank):
                    for c in range(C):
                        mm = pe.transpose(bank[:, c * P:(c + 1) * P], of[:, c * P:(c + 1) * P], ident[:, :])
                    return mm
                return emit

            def latents(w):
                def emit(bank):
                    for c in range(C):
                        mm = split_product(pe, bank[:, 0:SEQ], (w[0][:, c, :], w[1][:, c, :]), (at_hi[:, c, :], at_lo[:, c, :]),
                                           c == 0, c == C - 1)
                    return mm
                return emit

            def from_latents(n, t, w, bank):
                tok = slice(t * P, (t + 1) * P)
                return split_product(pe, bank, (lat_hi[:, n, tok], lat_lo[:, n, tok]), w, True, True)

            def keys_of(t):
                def emit(bank):
                    from_latents(0, t, parts["k_u"], bank[:, 0:HALF])
                    for c in range(C):
                        mm = split_product(pe, bank[:, HALF:], (at_hi[:, c, t * P:(t + 1) * P], at_lo[:, c, t * P:(t + 1) * P]),
                                           [w[:, c, :] for w in parts["rope_k"]], c == 0, c == C - 1)
                    return mm
                return emit

            def outputs(t):
                def emit(bank):
                    for c in range(C):
                        mm = split_product(pe, bank, (o_hi[:, c, t * P:(t + 1) * P], o_lo[:, c, t * P:(t + 1) * P]),
                                           [w[:, c, :] for w in parts["o"]], c == 0, c == C - 1)
                    return mm
                return emit

            def front(b, ahead, u):
                k0 = ring_base(b, ahead)
                if u == 1:
                    pe.wait_ge(a_done, TB * (b + ahead) + TB)
                    for t in range(TB):
                        use(k0, t, turned(a[:, t, :]))
                if u == 2:
                    pe.wait_ge(ring_free, k0 + TB)
                    use(k0, 2, latents(parts["kv_d"]))
                    use(k0, 3, latents(parts["q_d"]))
                if u == 3:
                    pe.wait_ge(ring_free, k0 + 4)
                    for t in range(TB):
                        use(k0, 4 + t, keys_of(t))
                if u == 4:
                    for t in range(TB):
                        use(k0, 6 + t, lambda bank: from_latents(1, t, parts["q_u"], bank))
                if u == 5:
                    for t in range(TB):
                        use(k0, 8 + t, lambda bank: from_latents(0, t, parts["v_u"], bank))
                if u == 8:
                    pe.wait_ge(rotated, 4 * (b + ahead) + 4)
                    for t in range(TB):
                        use(k0, 10 + t, turned(kf[:, t].rearrange("p h d -> p (h d)")))
                    for t in range(TB):
                        use(k0, 12 + t, turned(qf[:, t].rearrange("p h d -> p (h d)")), 1 + TB * (t == TB - 1 and ahead == 0))

            def attend(b, u, par):
                if u < UNITS:
                    att.scores(pe, b, u, lambda u, j: q_head[:, j, u // 2, (u % 2) * P:(u % 2 + 1) * P], lambda u, j: kt[:, u // 2, :],
                               mask[:, :], ident_b[:, :])
                if 1 <= u <= UNITS:
                    att.turn(pe, b, u - 1)
                    if u % 2 == 0:
                        att.weigh(pe, b, u // 2 - 1, par, lambda g, j, t: v[:, par, t, (4 * g + j) * HD:(4 * g + j + 1) * HD],
                                  lambda g, j: att.o_ps[HD * j:HD * (j + 1), g % 2, 0:SEQ], 2)

            def sample(b, par, last):
                pe.wait_ge(ring_free, ring_base(b, 0) + FRONT)
                for u in range(UNITS):
                    attend(b, u, par)
                    if not last:
                        front(b, 1, u)
                if not last:
                    front(b, 1, 8)
                attend(b, UNITS, par)
                pe.wait_ge(att.o_lo_done, UNITS // 2 * (b + 1))
                k0 = output_uses(b, last)
                for t in range(TB):
                    use(k0, t, outputs(t))

            for u in range(9):
                front(0, 0, u)
            with pe.Fori(0, BATCH // 2 - 1) as i:
                for par in range(2):
                    sample(i * 2 + par, par, False)
            sample(BATCH - 2, 0, False)
            sample(BATCH - 1, 1, True)

        @block.scalar
        def _(act):
            def front(b, ahead, u):
                k0 = ring_base(b, ahead)
                if u == 0:
                    for t in range(TB):
                        act.wait_ge(y_done, TB * (b + ahead) + t + 1)
                        act.wait_ge(squared, TB * (b + ahead) + t)
                        act.activation(junk[:, :], tile_of(h_res, (b + ahead) * TB + t), ACT.Square,
                                       accum_out=sq_sum[:, t:t + 1]).then_inc(squared, 1)
                if u == 1:
                    for t in range(TB):
                        act.wait_ge(ring_ready, k0 + t + 1)
                        act.activation(at_hi[:, :, t * P:(t + 1) * P], chunks(ring[:, t, :]), ACT.Copy).then_inc(hi_done, 1)
                if u == 2:
                    for n in range(2):
                        act.wait_ge(ring_ready, k0 + 2 + n + 1)
                        act.activation(lat_hi[:, n, :], ring[:, n, 0:SEQ], ACT.Copy).then_inc(hi_done, 1)
                if u in (3, 4):
                    for t in range(TB):
                        act.wait_ge(ring_ready, k0 + 2 * u - 2 + t + 1)
                        act.activation((kf, qf)[u - 3][:, t, :, 0:RD], ring[:, t, 0:HALF].rearrange("p (h d) -> p h d", h=NH),
                                       ACT.Copy).then_inc(plain_done, 1)
                if u == 8:
                    for t in range(TB):
                        act.wait_ge(ring_ready, k0 + 12 + t + 1)
                        for j in range(3):
                            ins = act.activation(q_head[HD * j:HD * (j + 1), j, :, t * P:(t + 1) * P],
                                                 chunks(ring[HD * j:HD * (j + 1), t, :]), ACT.Copy)
                        ins.then_inc(q_act_done, 1)

            def sample(b, par, last):
                for u in range(UNITS + 1):
                    if u < UNITS:
                        att.exponentials(act, b, u)
                    if u == UNITS and not last:
                        front(b, 1, 8)
                    if u >= 1:
                        att.copy_turned(act, b, u - 1, 1, par)
                        if u % 2 == 0:
                            g = u // 2 - 1
                            if g == 0:
                                act.wait_ge(ring_ready, ring_base(b, 1))
                            att.output_high(act, b, g, o_hi[:, g, :], att.o_ps[:, g % 2, 0:SEQ])
                    if u < UNITS and not last:
                        front(b, 1, u)

            act.wait_ge(zeroed2, 1)
            for u in range(9):
                front(0, 0, u)
            with act.Fori(0, BATCH // 2 - 1) as i:
                for par in range(2):
                    sample(i * 2 + par, par, False)
            sample(BATCH - 2, 0, False)
            sample(BATCH - 1, 1, True)

        @block.vector
        def _(dve):
            chain = Chain(dve, steps, begun)

            def norm(b, ahead):
                chain.turn(STEPS * (b + ahead))
                stats, agg, var, rstd, tmp = small
                layer_norm(dve, chain, None, lambda t: tile_of(x_res, (b + ahead) * TB + t), small, TB, y_done,
                           lambda t: tile_of(h_res, (b + ahead) * TB + t))

            def front(b, ahead, u, par):
                k0 = ring_base(b, ahead)
                if u == 0:
                    dve.wait_ge(squared, TB * (b + ahead) + TB)
                    dve.wait_ge(ring_ready, k0)
                    _, _, var, _, tmp = small
                    chain.step(dve.tensor_scalar(var[:, :], sq_sum[:, :], 1.0 / D, LN_EPS, ALU.mult, ALU.add))
                    chain.wait()
                    inverse_sqrt(dve, chain, a_rstd[:, :], var[:, :], tmp[:, :])
                    chain.wait()
                    for t in range(TB):
                        dve.scalar_tensor_tensor(a[:, t, :], tile_of(h_res, (b + ahead) * TB + t), a_rstd[:, t:t + 1], ln[:, :],
                                                 ALU.mult, ALU.mult).then_inc(a_done, 1)
                if u == 1:
                    for t in range(TB):
                        dve.wait_ge(hi_done, 4 * (b + ahead) + t + 1)
                        dve.tensor_tensor(at_lo[:, :, t * P:(t + 1) * P], chunks(ring[:, t, :]),
                                          f32(at_hi[:, :, t * P:(t + 1) * P]), ALU.subtract).then_inc(ring_free, 1)
                if u == 2:
                    for n in range(2):
                        dve.wait_ge(hi_done, 4 * (b + ahead) + 2 + n + 1)
                        dve.tensor_tensor(lat_lo[:, n, :], ring[:, n, 0:SEQ], f32(lat_hi[:, n, :]), ALU.subtract).then_inc(ring_free, 1)
                if u in (3, 4):
                    for t in range(TB):
                        n = 4 * (b + ahead) + 2 * (u - 3) + t
                        half = ring[:, t, HALF:].rearrange("p (h d) -> p h d", h=NH)
                        cos, sin = (rope[:, m, t, :].unsqueeze(1).to_broadcast([P, NH, RD]) for m in range(2))
                        dve.wait_ge(plain_done, n + 1)
                        dve.wait_ge(rotated, n)
                        dve.tensor_tensor(rot[:, 0], half, cos, ALU.mult).then_inc(products, 1)
                        dve.tensor_tensor(rot[:, 1, :, 0:RD // 2], half[:, :, RD // 2:], sin[:, :, 0:RD // 2], ALU.mult).then_inc(products, 1)
                        dve.tensor_tensor(rot[:, 1, :, RD // 2:], half[:, :, 0:RD // 2], sin[:, :, RD // 2:], ALU.mult).then_inc(ring_free, 1)
                        dve.wait_ge(products, 2 * n + 2)
                        dve.wait_ge(ring_free, k0 + 2 * u - 2 + t + 1)
                        dve.tensor_tensor((kf, qf)[u - 3][:, t, :, RD:], rot[:, 0], rot[:, 1], ALU.add).then_inc(rotated, 1)
                if u == 5:
                    for t in range(TB):
                        dve.wait_ge(ring_ready, k0 + 8 + t + 1)
                        dve.tensor_copy(v[:, par, t, :], ring[:, t, :]).then_inc(ring_free, 1)
                if u == 8:
                    for t in range(TB):
                        dve.wait_ge(ring_ready, k0 + 10 + t + 1)
                        dve.tensor_copy(kt[:, :, t * P:(t + 1) * P], chunks(ring[:, t, :])).then_inc(ring_free, 1)
                    for t in range(TB):
                        dve.wait_ge(q_act_done, TB * (b + ahead) + t + 1)
                        dve.tensor_copy(q_head[3 * HD:, 3, :, t * P:(t + 1) * P], chunks(ring[3 * HD:, t, :])).then_inc(
                            ring_free, 1 + TB * (t == TB - 1 and ahead == 0))

            def sample(b, par, last):
                for u in range(UNITS + 1):
                    if u < UNITS:
                        att.find_peak(dve, b, u)
                    if u == UNITS and not last:
                        front(b, 1, 8, 1 - par)
                    if u == 0 and not last:
                        norm(b, 1)
                    if u >= 1:
                        att.copy_turned(dve, b, u - 1, 0, par)
                        if u % 2 == 0:
                            g = u // 2 - 1
                            att.output_low(dve, b, g, o_lo[:, g, :], o_hi[:, g, :], att.o_ps[:, g % 2, 0:SEQ])
                    if u < UNITS:
                        att.invert_mass(dve, b, u)
                        if not last:
                            front(b, 1, u, 1 - par)
                k0 = output_uses(b, last)
                for t in range(TB):
                    dve.wait_ge(ring_ready, k0 + t + 1)
                    y = tile_of(h_res, b * TB + t)
                    dve.tensor_tensor(y, ring[:, t, :], y, ALU.add).then_inc(ring_free, 1)

            norm(0, 0)
            for u in range(9):
                front(0, 0, u, 0)
            with dve.Fori(0, BATCH // 2 - 1) as i:
                for par in range(2):
                    sample(i * 2 + par, par, False)
            sample(BATCH - 2, 0, False)
            sample(BATCH - 1, 1, True)


def expert_ffn(nc, x_res, h_res, ident, begun, w_dram, ln_row, router_dram, bias_dram, gate, out):
    EXPERTS = w_dram.shape[0]
    ROUTED = EXPERTS - 1
    I = w_dram.shape[2] // (3 * C)
    IC = I // P
    W = w_dram.shape[2]
    SLOTS = 8

    with ExitStack() as ctx:
        def sb(name, shape, dt=F32, of=None):
            return (of or ctx).enter_context(nc.sbuf_tensor(f"e_{name}", shape, dt))

        def sem(name):
            return nc.alloc_semaphore(f"e_{name}")

        rt_hi, rt_lo = sb("rt_hi", [P, C, TOK], F32R), sb("rt_lo", [P, C, TOK], F32R)
        raw = sb("raw", [P, W])
        w_hi, w_lo = sb("w_hi", [P, 2, W], F32R), sb("w_lo", [P, 2, W], F32R)
        share = sb("share", [P, TILES, EXPERTS])
        gate_sb, gain = sb("gate_sb", [P, 1]), sb("gain", [P, 1])
        w_in, w_hi_done, w_lo_done, gate_in = sem("w_in"), sem("w_hi_done"), sem("w_lo_done"), sem("gate_in")

        with ExitStack() as prep:
            ln = sb("ln_row", [P, D], F32, prep)
            r = sb("r", [P, 2, TB, D], F32, prep)
            router = sb("router", [P, C, P], F32, prep)
            router_hi, router_lo = (w[:, 1, 0:C * P].rearrange("p (c n) -> p c n", c=C) for w in (w_hi, w_lo))
            bias = sb("bias", [P, 1], F32, prep)
            junk = sb("junk", [P, D], BF16, prep)
            sq_sum, var, rstd, tmp = (sb(n, [P, TILES], F32, prep) for n in ("sq_sum", "var", "rstd", "tmp"))
            prob_t = sb("prob_t", [P, 2, SEQ], F32, prep)
            prob, rank, place, first, second = (sb(n, [P, TILES, SLOTS], F32, prep) for n in ("prob", "rank", "place", "first", "second"))
            best, next_best, spot, total = (sb(n, [P, TILES], F32, prep) for n in ("best", "next_best", "spot", "total"))
            t_ps = prep.enter_context(nc.psum_tensor("e_t_ps", [P, 2, TB, 512], F32))
            lg_ps = prep.enter_context(nc.psum_tensor("e_lg_ps", [P, 2, 512], F32))
            pt_ps = prep.enter_context(nc.psum_tensor("e_pt_ps", [P, 2, 512], F32))
            small_in, blank, router_in, router_hi_done, router_done, squared, steps = (
                sem(n) for n in ("small_in", "blank", "router_in", "router_hi_done", "router_done", "squared", "steps"))
            r_done, t_ready, rt_hi_done, rt_done, lg_ready, prob_done, pt_ready, ranked = (
                sem(n) for n in ("r_done", "t_ready", "rt_hi_done", "rt_done", "lg_ready", "prob_done", "pt_ready", "ranked"))
            prob_in = sem("prob_in")
            block = prep.enter_context(nc.Block())

            def tokens(b, t=0, n=SEQ):
                return bass.ds(b * SEQ + t * P, n)

            @block.sync
            def _(sp):
                sp.dma_start(raw[:, :], w_dram[0]).then_inc(w_in, 16)
                sp.dma_start(ln[:, :], ln_row).then_inc(small_in, 16)
                sp.dma_start(bias[:, :], bias_dram).then_inc(small_in, 16)
                sp.dma_start(gate_sb[:, :], gate).then_inc(gate_in, 16)
                sp.wait_ge(blank, 1)
                sp.dma_start(router[:, :, 0:SLOTS], router_dram).then_inc(router_in, 16)
                sp.wait_ge(w_lo_done, 1)
                sp.dma_start(raw[:, :], w_dram[1]).then_inc(w_in, 16)

            @block.gpsimd
            def _(pool):
                pool.memset(router[:, :, :], 0.0).then_inc(blank, 1)
                for j in range(SLOTS):
                    ins = pool.memset(rank[:, :, j], float(SLOTS - j))
                ins.then_inc(ranked, 1)
                pool.wait_ge(w_hi_done, 1)
                pool.tensor_tensor(w_lo[:, 0, :], raw[:, :], f32(w_hi[:, 0, :]), ALU.subtract).then_inc(w_lo_done, 1)

            @block.tensor
            def _(pe):
                def turn(b, par):
                    pe.wait_ge(r_done, b + 1)
                    if not isinstance(b, int) or b > 1:
                        pe.wait_ge(rt_done, TB * (b - 1))
                    for t in range(TB):
                        for c in range(C):
                            mm = pe.transpose(t_ps[:, par, t, c * P:(c + 1) * P], r[:, par, t, c * P:(c + 1) * P], ident[:, :])
                        mm.then_inc(t_ready, 1)

                def logits(b, par):
                    pe.wait_ge(rt_done, TB * b + TB)
                    for c in range(C):
                        mm = split_product(pe, lg_ps[:, par, 0:SEQ], (router_hi[:, c, :], router_lo[:, c, :]),
                                           (rt_hi[:, c, tokens(b)], rt_lo[:, c, tokens(b)]), c == 0, c == C - 1)
                    mm.then_inc(lg_ready, 1)
                    pe.wait_ge(prob_done, b + 1)
                    if not isinstance(b, int) or b > 1:
                        pe.wait_ge(prob_in, b - 1)
                    for t in range(TB):
                        mm = pe.transpose(pt_ps[:, par, t * P:(t + 1) * P], prob_t[:, par, t * P:(t + 1) * P], ident[:, :])
                    mm.then_inc(pt_ready, 1)

                pe.wait_ge(router_done, 1)
                turn(0, 0)
                turn(1, 1)
                logits(0, 0)
                turn(2, 0)
                logits(1, 1)
                with pe.Fori(1, BATCH // 2 - 1) as i:
                    for k in (0, 1):
                        turn(i * 2 + (k + 1), (k + 1) % 2)
                        logits(i * 2 + k, k)
                turn(BATCH - 1, 1)
                logits(BATCH - 2, 0)
                logits(BATCH - 1, 1)

            @block.scalar
            def _(act):
                def split(b, par):
                    for t in range(TB):
                        act.wait_ge(t_ready, TB * b + t + 1)
                        act.activation(rt_hi[:, :, tokens(b, t, P)], chunks(t_ps[:, par, t, :]), ACT.Copy).then_inc(rt_hi_done, 1)

                def sigmoid(b, par):
                    act.wait_ge(lg_ready, b + 1)
                    act.activation(prob_t[:, par, :], lg_ps[:, par, 0:SEQ], ACT.Sigmoid, bias=bias[:, :]).then_inc(prob_done, 1)

                with act.Fori(0, TILES) as n:
                    act.wait_ge(squared, n)
                    act.activation(junk[:, :], tile_of(h_res, n), ACT.Square, accum_out=sq_sum[:, bass.ds(n, 1)]).then_inc(squared, 1)
                act.wait_ge(router_in, 16)
                act.activation(router_hi[:, :, :], router[:, :, :], ACT.Copy).then_inc(router_hi_done, 1)
                act.wait_ge(gate_in, 16)
                act.activation(gain[:, :], gate_sb[:, :], ACT.Tanh)
                act.wait_ge(w_in, 16)
                act.activation(w_hi[:, 0, :], raw[:, :], ACT.Copy).then_inc(w_hi_done, 1)
                act.wait_ge(small_in, 32)
                split(0, 0)
                with act.Fori(0, BATCH // 2 - 1) as i:
                    for k in (0, 1):
                        split(i * 2 + (k + 1), (k + 1) % 2)
                        sigmoid(i * 2 + k, k % 2)
                split(BATCH - 1, 1)
                sigmoid(BATCH - 2, 0)
                sigmoid(BATCH - 1, 1)

            @block.vector
            def _(dve):
                chain = Chain(dve, steps, begun)

                def norm(b, par):
                    for t in range(TB):
                        ins = dve.scalar_tensor_tensor(r[:, par, t, :], tile_of(h_res, b * TB + t), rstd[:, bass.ds(b * TB + t, 1)],
                                                       ln[:, :], ALU.mult, ALU.mult)
                    ins.then_inc(r_done, 1)

                def split_low(b, par):
                    for t in range(TB):
                        dve.wait_ge(rt_hi_done, TB * b + t + 1)
                        dve.tensor_tensor(rt_lo[:, :, tokens(b, t, P)], chunks(t_ps[:, par, t, :]), f32(rt_hi[:, :, tokens(b, t, P)]),
                                          ALU.subtract).then_inc(rt_done, 1)

                def collect(b, par):
                    dve.wait_ge(pt_ready, b + 1)
                    if isinstance(b, int):
                        dve.wait_ge(steps, 1)
                    dve.tensor_copy(prob[:, bass.ds(b * TB, TB), 0:ROUTED],
                                    pt_ps[:, par, 0:TB * P].rearrange("p (t s) -> p t s", s=P)[:, :, 0:ROUTED]).then_inc(prob_in, 1)

                def spread(x):
                    return x[:, :].unsqueeze(2).to_broadcast([P, TILES, SLOTS])

                chain.step(dve.memset(prob[:, :, :], -1.0))
                dve.memset(share[:, :, 0], 1.0)
                dve.wait_ge(router_hi_done, 1)
                dve.tensor_tensor(router_lo[:, :, :], router[:, :, :], f32(router_hi[:, :, :]), ALU.subtract).then_inc(router_done, 1)
                dve.wait_ge(squared, TILES)
                chain.step(dve.tensor_scalar(var[:, :], sq_sum[:, :], 1.0 / D, LN_EPS, ALU.mult, ALU.add))
                chain.wait()
                inverse_sqrt(dve, chain, rstd[:, :], var[:, :], tmp[:, :])
                chain.wait()
                dve.wait_ge(small_in, 32)
                norm(0, 0)
                norm(1, 1)
                with dve.Fori(0, BATCH // 2 - 1) as i:
                    for k in (0, 1):
                        split_low(i * 2 + k, k)
                        norm(i * 2 + (k + 2), k)
                        collect(i * 2 + k, k)
                for k in (0, 1):
                    split_low(BATCH - 2 + k, k)
                for k in (0, 1):
                    collect(BATCH - 2 + k, k)

                dve.wait_ge(prob_in, BATCH)
                dve.wait_ge(ranked, 1)
                for value, hot in ((best, first), (next_best, second)):
                    chain.step(dve.tensor_reduce(value[:, :], prob[:, :, :], AX.X, ALU.max))
                    chain.wait()
                    chain.step(dve.tensor_tensor(place[:, :, :], prob[:, :, :], spread(value), ALU.is_equal))
                    chain.wait()
                    chain.step(dve.tensor_tensor(place[:, :, :], place[:, :, :], rank[:, :, :], ALU.mult))
                    chain.wait()
                    chain.step(dve.tensor_reduce(spot[:, :], place[:, :, :], AX.X, ALU.max))
                    chain.wait()
                    chain.step(dve.tensor_tensor(hot[:, :, :], place[:, :, :], spread(spot), ALU.is_equal))
                    chain.wait()
                    if hot is first:
                        chain.step(dve.scalar_tensor_tensor(prob[:, :, :], first[:, :, :], -2.0, prob[:, :, :], ALU.mult, ALU.add))
                        chain.wait()
                chain.step(dve.tensor_tensor(first[:, :, :], first[:, :, :], spread(best), ALU.mult))
                chain.step(dve.tensor_tensor(second[:, :, :], second[:, :, :], spread(next_best), ALU.mult))
                chain.step(dve.tensor_tensor(total[:, :], best[:, :], next_best[:, :], ALU.add))
                chain.wait()
                chain.step(dve.tensor_tensor(first[:, :, :], first[:, :, :], second[:, :, :], ALU.add))
                chain.step(dve.reciprocal(spot[:, :], total[:, :]))
                chain.wait()
                dve.tensor_tensor(share[:, :, 1:EXPERTS], first[:, :, 0:ROUTED], spot[:, :].unsqueeze(2).to_broadcast([P, TILES, ROUTED]), ALU.mult)

        sg = sb("sg", [P, 2, IC * SEQ])
        act_f = sb("act_f", [P, IC * SEQ])
        act_hi, act_lo = sb("act_hi", [P, 2, IC, SEQ], F32R), sb("act_lo", [P, 2, IC, SEQ], F32R)
        g_ps = ctx.enter_context(nc.psum_tensor("e_g_ps", [P, 2, IC * SEQ], F32))
        u_ps = ctx.enter_context(nc.psum_tensor("e_u_ps", [P, 2, IC * SEQ], F32))
        d_ps = ctx.enter_context(nc.psum_tensor("e_d_ps", [P, 2, TB, D], F32))
        g_ready, u_ready, sg_done, act_done, hi_done, lo_done, d_ready, added, x_done, stored = (
            sem(n) for n in ("g_ready", "u_ready", "sg_done", "act_done", "hi_done", "lo_done", "d_ready", "added", "x_done", "stored"))
        block = ctx.enter_context(nc.Block())

        def weights(par):
            of = [[w[:, par, k * C * I:(k + 1) * C * I] for w in (w_hi, w_lo)] for k in range(3)]
            gate_w, up_w = ([w.rearrange("p (c i) -> p c i", c=C) for w in of[k]] for k in range(2))
            return gate_w, up_w, [w.rearrange("p (c n) -> p c n", c=IC) for w in of[2]]

        def unit(e, s):
            return e * BATCH + s

        def experts(eng, one):
            one(0, 0)
            with eng.Fori(0, (EXPERTS - 2) // 2) as i:
                one(i * 2 + 1, 1)
                one(i * 2 + 2, 0)
            one(EXPERTS - 1, 1)

        @block.sync
        def _(sp):
            with sp.Fori(2, EXPERTS) as e:
                wait_apart(sp, w_lo_done, e, begun)
                sp.dma_start(raw[:, :], w_dram[bass.ds(e, 1)].rearrange("o p n -> (o p) n")).then_inc(w_in, 16)
            for b in range(BATCH):
                sp.wait_ge(x_done, b + 1)
                sp.dma_start(out[:, b * TB:(b + 1) * TB, :], x_res[:, b * TB:(b + 1) * TB, :]).then_inc(stored, 16)
            sp.wait_ge(stored, 16 * BATCH)

        @block.gpsimd
        def _(pool):
            def split_low(e, par):
                pool.wait_ge(w_hi_done, e + 1)
                pool.tensor_tensor(w_lo[:, par, :], raw[:, :], f32(w_hi[:, par, :]), ALU.subtract).then_inc(w_lo_done, 1)

            with pool.Fori(0, (EXPERTS - 2) // 2) as i:
                split_low(i * 2 + 1, 1)
                split_low(i * 2 + 2, 0)
            split_low(EXPERTS - 1, 1)

        @block.tensor
        def _(pe):
            def up(e, s, par, w):
                n = unit(e, s)
                if not isinstance(n, int) or n > 1:
                    pe.wait_ge(act_done, n - 1)
                here = bass.ds(s * SEQ, SEQ)
                for ps, side, ready in ((g_ps, w[0], g_ready), (u_ps, w[1], u_ready)):
                    for k in range(IC):
                        for c in range(C):
                            cols = slice(k * P, (k + 1) * P)
                            mm = split_product(pe, ps[:, par, k * SEQ:(k + 1) * SEQ], (side[0][:, c, cols], side[1][:, c, cols]),
                                               (rt_hi[:, c, here], rt_lo[:, c, here]), c == 0, c == C - 1)
                    mm.then_inc(ready, 1)

            def down(e, s, par, w):
                n = unit(e, s)
                pe.wait_ge(lo_done, n + 1)
                if not isinstance(n, int) or n > 1:
                    pe.wait_ge(added, n - 1)
                for t in range(TB):
                    for k in range(IC):
                        tok = slice(t * P, (t + 1) * P)
                        mm = split_product(pe, d_ps[:, par, t, :], (act_hi[:, par, k, tok], act_lo[:, par, k, tok]),
                                           (w[2][0][:, k, :], w[2][1][:, k, :]), k == 0, k == IC - 1)
                mm.then_inc(d_ready, 1)

            def expert(e, par_w):
                w = weights(par_w)
                pe.wait_ge(w_lo_done, e + 1)
                up(e, 0, 0, w)
                if not isinstance(e, int) or e > 0:
                    down(e - 1, BATCH - 1, 1, weights(1 - par_w))
                up(e, 1, 1, w)
                down(e, 0, 0, w)
                with pe.Fori(1, BATCH // 2) as i:
                    for par in range(2):
                        up(e, i * 2 + par, par, w)
                        down(e, i * 2 + (par - 1), 1 - par, w)

            experts(pe, expert)
            down(EXPERTS - 1, BATCH - 1, 1, weights((EXPERTS - 1) % 2))

        @block.scalar
        def _(act):
            def split_weights(e, par):
                act.wait_ge(w_in, 16 * e + 16)
                act.wait_ge(d_ready, unit(e - 1, 0))
                act.activation(w_hi[:, par, :], raw[:, :], ACT.Copy).then_inc(w_hi_done, 1)

            def sample(e, s, par):
                n = unit(e, s)
                act.wait_ge(g_ready, n + 1)
                if not isinstance(n, int) or n > 1:
                    act.wait_ge(act_done, n - 1)
                act.activation(sg[:, par, :], g_ps[:, par, :], ACT.Silu).then_inc(sg_done, 1)
                act.wait_ge(act_done, n + 1)
                if not isinstance(n, int) or n > 1:
                    act.wait_ge(d_ready, n - 1)
                act.activation(act_hi[:, par, :, :].rearrange("p k q -> p (k q)"), act_f[:, :], ACT.Copy).then_inc(hi_done, 1)

            def expert(e, par_w):
                sample(e, 0, 0)
                sample(e, 1, 1)
                if not isinstance(e, int) or e < EXPERTS - 1:
                    split_weights(e + 1, 1 - par_w)
                with act.Fori(1, BATCH // 2) as i:
                    for par in range(2):
                        sample(e, i * 2 + par, par)

            experts(act, expert)

        @block.vector
        def _(dve):
            def middle(e, s, par):
                n = unit(e, s)
                dve.wait_ge(u_ready, n + 1)
                dve.wait_ge(sg_done, n + 1)
                if not isinstance(n, int) or n > 0:
                    dve.wait_ge(lo_done, n)
                dve.scalar_tensor_tensor(act_f[:, :], u_ps[:, par, :], 0.125, sg[:, par, :], ALU.mult, ALU.mult).then_inc(act_done, 1)
                dve.wait_ge(hi_done, n + 1)
                dve.tensor_tensor(act_lo[:, par, :, :].rearrange("p k q -> p (k q)"), act_f[:, :],
                                  f32(act_hi[:, par, :, :]).rearrange("p k q -> p (k q)"), ALU.subtract).then_inc(lo_done, 1)

            def add(e, s, par):
                n = unit(e, s)
                dve.wait_ge(d_ready, n + 1)
                for t in range(TB):
                    tile = s * TB + t
                    mine = share[:, bass.ds(tile, 1), bass.ds(e, 1)].rearrange("p o e -> p (o e)")
                    h = tile_of(h_res, tile)
                    ins = dve.scalar_tensor_tensor(h, d_ps[:, par, t, :], mine, h, ALU.mult, ALU.add)
                ins.then_inc(added, 1)
                if isinstance(e, int) and e == EXPERTS - 1:
                    dve.wait_ge(added, n + 1)
                    for t in range(TB):
                        x = tile_of(x_res, s * TB + t)
                        ins = dve.scalar_tensor_tensor(x, tile_of(h_res, s * TB + t), gain[:, 0:1], x, ALU.mult, ALU.add)
                    ins.then_inc(x_done, 1)

            def expert(e, par_w):
                middle(e, 0, 0)
                if not isinstance(e, int) or e > 0:
                    add(e - 1, BATCH - 1, 1)
                middle(e, 1, 1)
                add(e, 0, 0)
                with dve.Fori(1, BATCH // 2) as i:
                    for par in range(2):
                        middle(e, i * 2 + par, par)
                        add(e, i * 2 + (par - 1), 1 - par)

            experts(dve, expert)
            add(EXPERTS - 1, BATCH - 1, 1)


def decoder(nc, a, out):
    with ExitStack() as ctx:
        x_res = ctx.enter_context(nc.sbuf_tensor("x_res", [P, TILES, D], F32))
        ident = ctx.enter_context(nc.sbuf_tensor("ident", [P, P], F32))
        begun = ctx.enter_context(nc.semaphore("begun"))
        blank = ctx.enter_context(nc.semaphore("blank"))
        with nc.Block() as block:
            @block.gpsimd
            def _(pool):
                pool.memset(ident[:, :], 0.0).then_inc(blank, 1)
                pool.wait_ge(blank, 1)
                pool.affine_select(out=ident[:, :], in_=ident[:, :], compare_op=ALU.not_equal, fill=1.0, base=0,
                                   pattern=[[-1, P]], channel_multiplier=1).then_inc(begun, 1)
        with nc.cleanup_on_exit():
            image_attention(nc, x_res, ident, begun, a["x"], a["ctx_t"], a["a_w"], a["a_rows"], a["g_xattn0"])
        with nc.cleanup_on_exit():
            quantised_ffn(nc, x_res, ident, begun, a["b_w"], a["b_ln"], a["g_ffn0"])
        xnt_dram = nc.dram_tensor("xnt_scratch", (BATCH, P, C, SEQ), F32, kind="Internal").ap()
        with nc.cleanup_on_exit():
            cross_attention(nc, x_res, ident, begun, xnt_dram, a["ctx_t"], a["c_w"], a["g_xattn1"])
        h_res = ctx.enter_context(nc.sbuf_tensor("h_res", [P, TILES, D], F32))
        with nc.cleanup_on_exit():
            latent_attention(nc, x_res, h_res, ident, begun, a["d_w"], a["d_ln"], a["rope"])
        with nc.cleanup_on_exit():
            expert_ffn(nc, x_res, h_res, ident, begun, a["e_w"], a["e_ln"], a["router"], a["router_b"], a["g_ffn1"], out)


def tiled(x):
    return np.ascontiguousarray(np.asarray(x).reshape(TILES, P, D).transpose(1, 0, 2))


def rows_on_partitions(w):
    return np.ascontiguousarray(w.reshape(-1, P, w.shape[1]).transpose(1, 0, 2))


def on_all_partitions(*vectors):
    return np.ascontiguousarray(np.broadcast_to(np.stack(vectors), (P, len(vectors), vectors[0].shape[0])))


def rope_table():
    half = D // NH // 4
    freq = (np.float32(1) / np.float32(10000) ** (np.arange(0, 2 * half, 2, dtype=np.float32) / np.float32(2 * half))).astype(np.float32)
    angle = np.outer(np.arange(SEQ, dtype=np.float32), freq).astype(np.float32)
    cos, sin = np.cos(angle, dtype=np.float32), np.sin(angle, dtype=np.float32)
    table = np.stack([np.concatenate([cos, cos], 1), np.concatenate([-sin, sin], 1)])
    return np.ascontiguousarray(table.reshape(2, TB, P, 2 * half).transpose(2, 0, 1, 3))


def layouts(i):
    a = {}
    a["x"] = tiled(i["x"])
    a["ctx_t"] = np.ascontiguousarray(i["ctx_2048"].reshape(BATCH, SEQ, C, P).transpose(0, 3, 2, 1))
    a["a_w"] = np.stack([rows_on_partitions(i[f"L0_xattn_{n}_w"].T) for n in ("q", "k_img", "v_img", "o")])
    a["a_rows"] = on_all_partitions(*(i[f"L0_xattn_{n}"] for n in ("q_b", "k_img_b", "v_img_b", "o_b", "norm_q_w", "norm_k_img_w")))
    a["b_w"] = np.stack([rows_on_partitions(i[f"L0_ffn_w_{n}"].T).reshape(P, -1) for n in ("gate", "up", "down")])
    a["b_ln"] = np.ascontiguousarray(np.broadcast_to(i["L0_ffn_ln_weight"], (P, 2048)))
    heads = [i[f"L1_xattn_W{n}"].reshape(C, P, NH // 4, D).transpose(2, 1, 0, 3) for n in "qkv"]
    a["c_w"] = np.ascontiguousarray(np.stack([*heads, i["L1_xattn_Wo"].reshape(NH // 4, 4, P, D).transpose(0, 2, 1, 3)], 1))
    f = {n: i[f"L1_ffn_{n}"] for n in ("kv_d_w", "q_d_w", "k_u_w", "q_u_w", "v_u_w", "rope_k_w", "rope_q_w", "o_w", "ln1_w", "ln2_w")}
    a["d_w"] = np.concatenate([rows_on_partitions(w).reshape(P, -1) for w in (
        f["kv_d_w"], f["q_d_w"], f["k_u_w"], np.concatenate([f["q_u_w"], f["rope_q_w"]], 1), f["v_u_w"], f["rope_k_w"], f["o_w"])], 1)
    a["d_ln"] = np.ascontiguousarray(np.broadcast_to(f["ln1_w"], (P, D)))
    a["rope"] = rope_table()
    f = {n: i[f"L1_ffn_{n}"] for n in ("sh_gate", "sh_up", "sh_down", "r_gate", "r_up", "r_down", "router_w", "router_b")}
    experts = [(f["sh_gate"], f["sh_up"], f["sh_down"]), *zip(f["r_gate"], f["r_up"], f["r_down"])]
    a["e_w"] = np.stack([np.concatenate([rows_on_partitions(w).reshape(P, -1) for w in e], 1) for e in experts])
    a["e_ln"] = np.ascontiguousarray(np.broadcast_to(i["L1_ffn_ln2_w"], (P, D)))
    a["router"] = rows_on_partitions(np.concatenate([f["router_w"], np.zeros((D, 1), np.float32)], 1))
    a["router_b"] = np.concatenate([f["router_b"], np.zeros(P - len(f["router_b"]), np.float32)]).reshape(P, 1)
    for n, g in (("g_xattn0", i["g_xattn"][0:1]), ("g_xattn1", i["g_xattn"][1:2]), ("g_ffn0", i["g_ffn"][0:1]), ("g_ffn1", i["g_ffn"][1:2])):
        a[n] = np.ascontiguousarray(np.broadcast_to(g, (P, 1)))
    return a


def kernel(**inputs):
    import concourse.bacc as bacc
    from concourse.bass_utils import run_bass_kernel_spmd

    nc = bacc.Bacc("TRN2", target_bir_lowering=False, num_devices=1)
    arrays = layouts({name: np.asarray(value) for name, value in inputs.items()})
    a = {name: nc.dram_tensor(name, value.shape, mybir.dt.from_np(value.dtype), kind="ExternalInput").ap() for name, value in arrays.items()}
    out = nc.dram_tensor("out", (P, TILES, D), F32, kind="ExternalOutput").ap()
    decoder(nc, a, out)
    result = run_bass_kernel_spmd(nc, [arrays], core_ids=[0])
    return np.asarray(result.results[0]["out"]).transpose(1, 0, 2).reshape(BATCH, SEQ, D)
```

```python
from contextlib import ExitStack

import numpy as np

import concourse.bass as bass
from concourse import mybir

ALU = mybir.AluOpType
ACT = mybir.ActivationFunctionType
AX = mybir.AxisListType
F32 = mybir.dt.float32
F32R = mybir.dt.float32r
BF16 = mybir.dt.bfloat16
I32 = mybir.dt.int32
U32 = mybir.dt.uint32

P = 128
BATCH, SEQ, D = 8, 256, 512
TOK = BATCH * SEQ
TILES = TOK // P
TB = SEQ // P
C = D // P
NH = 16
ROUND = 12582912.0
LN_EPS = 1e-5
RMS_EPS = 1e-6


def f32(ap):
    return ap.bitcast(F32)


def at(b, per, k):
    return b * per + max(k, 0)


def split_product(pe, out, lhs, rhs, first, last):
    pe.matmul(out, lhs[0], rhs[1], start=first, stop=False)
    pe.matmul(out, lhs[0], rhs[0], start=False, stop=False)
    return pe.matmul(out, lhs[1], rhs[0], start=False, stop=last)


def wait_apart(eng, sem, value, begun):
    eng.wait_ge(sem, value)
    eng.wait_ge(begun, 1)


class Chain:

    def __init__(self, eng, sem, begun):
        self.eng, self.sem, self.begun, self.base, self.n = eng, sem, begun, 0, 0

    def turn(self, base):
        self.base, self.n = base, 0

    def step(self, ins):
        ins.then_inc(self.sem, 1)
        self.n += 1

    def wait(self):
        self.eng.wait_ge(self.sem, self.base + self.n)


def inverse_sqrt(dve, chain, out, var, tmp):
    chain.step(dve.tensor_scalar(out.bitcast(I32), var.bitcast(I32), -0.5, 1597463007.0, ALU.mult, ALU.add))
    for _ in range(3):
        chain.wait()
        chain.step(dve.tensor_tensor(tmp, out, out, ALU.mult))
        chain.wait()
        chain.step(dve.scalar_tensor_tensor(tmp, tmp, -0.5, var, ALU.mult, ALU.mult))
        chain.wait()
        chain.step(dve.scalar_tensor_tensor(out, tmp, 1.5, out, ALU.add, ALU.mult))


INVERSE_SQRT_STEPS = 10


class Norm:

    def __init__(self, nc, tag, x, begun, place):
        self.x, self.begun = x, begun
        self.stats, self.agg, self.var, self.rstd, self.tmp = (
            place(nc.sbuf_tensor(f"{tag}_ln_{n}", [P, TILES, *shape], F32))
            for n, shape in (("stats", (6,)), ("agg", (2,)), ("var", ()), ("rstd", ()), ("tmp", ())))
        self.stats_done, self.steps = nc.alloc_semaphore(f"{tag}_ln_stats_done"), nc.alloc_semaphore(f"{tag}_ln_steps")

    def find_spread(self, dve, chain, first, end):
        part = slice(first, end)
        with dve.Fori(first, end) as n:
            dve.bn_stats(self.stats[:, bass.ds(n, 1), :].rearrange("p o n -> p (o n)"), tile_of(self.x, n)).then_inc(self.stats_done, 1)
        dve.wait_ge(self.stats_done, end)
        for n in range(first, end):
            ins = dve.bn_aggr(self.agg[:, n, :], self.stats[:, n, :])
        chain.step(ins)
        chain.wait()
        chain.step(dve.tensor_scalar(self.var[:, part], self.agg[:, part, 1], LN_EPS, None, ALU.add))
        chain.wait()
        inverse_sqrt(dve, chain, self.rstd[:, part], self.var[:, part], self.tmp[:, part])
        chain.wait()

    def normalised(self, dve, out, n):
        return dve.tensor_scalar(out, tile_of(self.x, n), self.agg[:, bass.ds(n, 1), 0:1].rearrange("p o e -> p (o e)"),
                                 self.rstd[:, bass.ds(n, 1)], ALU.subtract, ALU.mult)


def tile_of(x, n):
    return x[:, bass.ds(n, 1), :].rearrange("p o n -> p (o n)")


def chunks(bank):
    return bank.rearrange("p (c q) -> p c q", c=C)


class Attention:

    def __init__(self, nc, ctx, tag, begun, ident, units, scale, turned_buffers, causal=False):
        self.begun, self.ident, self.units, self.scale, self.buffers = begun, ident[:, :], units, scale, turned_buffers
        self.groups = units // TB
        self.causal = causal

        def sb(name, shape, dt=F32):
            return ctx.enter_context(nc.sbuf_tensor(f"{tag}_{name}", shape, dt))

        self.prob = sb("prob", [P, 2, 4, SEQ])
        self.prob_t = sb("prob_t", [P, turned_buffers, TB, 4, SEQ])
        self.peak, self.neg_peak, self.mass, self.inv_mass = (sb(n, [P, 2, 4]) for n in ("peak", "neg_peak", "mass", "inv_mass"))
        self.s_ps = ctx.enter_context(nc.psum_tensor(f"{tag}_s_ps", [P, 4, SEQ], F32))
        self.t_ps = ctx.enter_context(nc.psum_tensor(f"{tag}_t_ps", [P, TB, 512], F32))
        self.o_ps = ctx.enter_context(nc.psum_tensor(f"{tag}_o_ps", [P, 2, 512], F32))

        def sem(name):
            return nc.alloc_semaphore(f"{tag}_{name}")

        self.s_ready, self.peak_found, self.peak_done, self.exp_done = sem("s_ready"), sem("peak_found"), sem("peak_done"), sem("exp_done")
        self.mass_inverted, self.prob_done, self.t_ready = sem("mass_inverted"), sem("prob_done"), sem("t_ready")
        self.turned0, self.turned1 = sem("turned0"), sem("turned1")
        self.o_ready, self.o_hi_done, self.o_lo_done = sem("o_ready"), sem("o_hi_done"), sem("o_lo_done")

    def keys(self, u):
        return P if self.causal and u % 2 == 0 else SEQ

    def key_tiles(self, u):
        return self.keys(u) // P

    def scores(self, pe, b, u, q_of, k_of, mask=None, ident_b=None):
        n, w = b * self.units + u, self.keys(u)
        for j in range(4):
            if j % 2 == 0:
                pe.wait_ge(self.exp_done, 2 * n - 1 + j // 2 if u > 0 else 2 * n)
            if mask is not None:
                pe.matmul(self.s_ps[:, j, w - P:w], ident_b, mask, start=True, stop=False, skip_group_check=True)
            mm = pe.matmul(self.s_ps[:, j, 0:w], q_of(u, j), k_of(u, j)[:, 0:w], start=mask is None, stop=True,
                           skip_group_check=mask is not None)
            if j % 2 == 1:
                mm.then_inc(self.s_ready, 1)

    def find_peak(self, dve, b, u, scale=None):
        n, w = b * self.units + u, self.keys(u)
        for half in range(2):
            js = slice(2 * half, 2 * half + 2)
            peak, neg_peak = self.peak[:, u % 2, js], self.neg_peak[:, u % 2, js]
            dve.wait_ge(self.s_ready, 2 * n + (half + 1))
            dve.tensor_reduce(peak, self.s_ps[:, js, 0:w], AX.X, ALU.max).then_inc(self.peak_found, 1)
            dve.wait_ge(self.peak_found, 2 * n + (half + 1))
            if scale is None:
                ins = dve.tensor_scalar(neg_peak, peak, -self.scale, None, ALU.mult)
            else:
                ins = dve.tensor_scalar(neg_peak, peak, scale, -1.0, ALU.mult, ALU.mult)
            ins.then_inc(self.peak_done, 1)

    def exponentials(self, act, b, u, scale=None):
        n, w = b * self.units + u, self.keys(u)
        act.wait_ge(self.t_ready, at(b, TB * self.units, TB * (u - 1)))
        for j in range(4):
            if j % 2 == 0:
                act.wait_ge(self.peak_done, 2 * n + (j // 2 + 1))
            ins = act.activation(self.prob[:, u % 2, j, 0:w], self.s_ps[:, j, 0:w], ACT.Exp, bias=self.neg_peak[:, u % 2, j:j + 1],
                                 scale=self.scale if scale is None else scale, accum_out=self.mass[:, u % 2, j:j + 1])
            if j % 2 == 1:
                ins.then_inc(self.exp_done, 1)

    def invert_mass(self, dve, b, u):
        n = b * self.units + u
        for half in range(2):
            js = slice(2 * half, 2 * half + 2)
            dve.wait_ge(self.exp_done, 2 * n + (half + 1))
            dve.reciprocal(self.inv_mass[:, u % 2, js], self.mass[:, u % 2, js]).then_inc(self.mass_inverted, 1)

    def normalise(self, pool, b, u):
        n, w = b * self.units + u, self.keys(u)
        for half in range(2):
            js = slice(2 * half, 2 * half + 2)
            part = self.prob[:, u % 2, js, 0:w]
            pool.wait_ge(self.mass_inverted, 2 * n + (half + 1))
            pool.tensor_tensor(part, part, self.inv_mass[:, u % 2, js].unsqueeze(2).to_broadcast([P, 2, w]), ALU.mult).then_inc(self.prob_done, 1)

    def turn(self, pe, b, u):
        n = b * self.units + u
        tiles = range(self.key_tiles(u))
        for j in range(4):
            if j % 2 == 0:
                pe.wait_ge(self.prob_done, 2 * n + (j // 2 + 1))
            for t in tiles:
                if j == 0:
                    pe.wait_ge((self.turned0, self.turned1)[t], n - u % 2 if self.causal and t else n)
                mm = pe.transpose(self.t_ps[:, t, j * P:(j + 1) * P], self.prob[:, u % 2, j, t * P:(t + 1) * P], self.ident)
                if j == 3:
                    mm.then_inc(self.t_ready, TB // self.key_tiles(u))

    def copy_turned(self, eng, b, u, t, par):
        n, g = b * self.units + u, u // TB
        if u % TB == (1 if self.causal and t else 0):
            eng.wait_ge(self.o_ready, at(b, self.groups, g - (self.buffers - 1)))
        if t < self.key_tiles(u):
            eng.wait_ge(self.t_ready, TB * n + t + 1)
        buf = (par * self.groups + g) % self.buffers
        to = self.prob_t[:, buf, t, :, (u % TB) * P:(u % TB + 1) * P]
        of = self.t_ps[:, t, :].rearrange("p (j q) -> p j q", j=4)
        if t == 0:
            eng.tensor_copy(to, of).then_inc(self.turned0, 1)
        elif self.key_tiles(u) == TB:
            eng.activation(to, of, ACT.Copy).then_inc(self.turned1, TB if self.causal else 1)

    def weigh(self, pe, b, g, par, v_of, out_of, banks):
        n = b * self.units + TB * g + TB
        pe.wait_ge(self.turned0, n)
        pe.wait_ge(self.turned1, n)
        pe.wait_ge(self.o_lo_done, at(b, self.groups, g - (banks - 1)))
        buf = (par * self.groups + g) % self.buffers
        for j, t in ([(j, t) for t in range(TB) for j in range(4)] if banks == 2 else [(j, t) for j in range(4) for t in range(TB)]):
            mm = pe.matmul(out_of(g, j), v_of(g, j, t), self.prob_t[:, buf, t, j, :], start=(t == 0), stop=(t == TB - 1))
        mm.then_inc(self.o_ready, 1)

    def output_high(self, act, b, g, to, of):
        act.wait_ge(self.o_ready, b * self.groups + g + 1)
        act.activation(to, of, ACT.Copy).then_inc(self.o_hi_done, 1)

    def output_low(self, dve, b, g, to, high, of):
        dve.wait_ge(self.o_hi_done, b * self.groups + g + 1)
        dve.tensor_tensor(to, of, f32(high), ALU.subtract).then_inc(self.o_lo_done, 1)


def image_attention(nc, x_res, ident, begun, x_in, ctx_t, w_t, rows, gate):
    tag = "a"
    HD = D // NH
    SCALE = float(HD) ** -0.5
    UNITS = NH // 4 * TB
    FRONT = 12
    TURN = FRONT + TB
    STEPS = 1 + INVERSE_SQRT_STEPS
    QB, KB, VB, OB, NQ, NK = range(6)

    with ExitStack() as ctx:
        def sb(name, shape, dt=F32):
            return ctx.enter_context(nc.sbuf_tensor(f"{tag}_{name}", shape, dt))

        def sem(name):
            return nc.alloc_semaphore(f"{tag}_{name}")

        w_hi = [sb(f"w_hi{n}", [P, C, D], F32R) for n in range(4)]
        w_lo = [sb(f"w_lo{n}", [P, C, D], F32R) for n in range(4)]
        row = sb("row", [P, 6, D])
        gate_sb = sb("gate_sb", [P, 1])
        gain = sb("gain", [P, 1])
        ctx_f = sb("ctx_f", [P, C, SEQ])
        ctx_hi, ctx_lo = sb("ctx_hi", [P, C, SEQ], F32R), sb("ctx_lo", [P, C, SEQ], F32R)
        xn = sb("xn", [P, TB, D])
        xt_hi, xt_lo = sb("xt_hi", [P, C, SEQ], F32R), sb("xt_lo", [P, C, SEQ], F32R)
        qf, kf = sb("qf", [P, TB, D]), sb("kf", [P, TB, D])
        q_head = sb("q_head", [P, 4, C, SEQ])
        kt = sb("kt", [P, C, SEQ])
        v = sb("v", [P, 2, TB, D])
        o_hi, o_lo = sb("o_hi", [P, C, SEQ], F32R), sb("o_lo", [P, C, SEQ], F32R)
        norm_of = Norm(nc, "a", x_res, begun, ctx.enter_context)
        qk_var, qk_rstd, qk_tmp = (sb(n, [P, 2, TB]) for n in ("qk_var", "qk_rstd", "qk_tmp"))
        sq_sum = sb("sq_sum", [P, 2, TB])
        junk = sb("junk", [P, D])
        q_scale = sb("q_scale", [P, 2, TB])
        att = Attention(nc, ctx, tag, begun, ident, UNITS, None, 2)
        raw = att.prob_t[:, :, :, :, :].rearrange("p a t j s -> p a (t j s)").rearrange("p a (c n) -> p a c n", c=C)
        ring = ctx.enter_context(nc.psum_tensor(f"{tag}_ring", [P, 2, 512], F32))

        x_first, x_rest, ctx_in, rows_in = sem("x_first"), sem("x_rest"), sem("ctx_in"), sem("rows_in")
        w_in = [sem("w_in0"), sem("w_in1")]
        w_hi_done, w_lo_done, rows_done, gain_done, zeroed = sem("w_hi_done"), sem("w_lo_done"), sem("rows_done"), sem("gain_done"), sem("zeroed")
        ctx_hi_done, ctx_lo_done, steps, xn_done = sem("ctx_hi_done"), sem("ctx_lo_done"), sem("steps"), sem("xn_done")
        ring_ready, ring_free, xt_hi_done = sem("ring_ready"), sem("ring_free"), sem("xt_hi_done")
        squared, q_scaled, k_hat_done = sem("squared"), sem("q_scaled"), sem("k_hat_done")
        q_act_done, x_done = sem("q_act_done"), sem("x_done")
        block = ctx.enter_context(nc.Block())

        def ring_base(b, ahead):
            return TURN * (b + ahead)

        def groups_done(u):
            return [g for g in range(UNITS // 2) if min(2 * g + 3, UNITS) == u]

        def output_uses(b, last):
            return TURN * (b + 1) + (0 if last else FRONT)

        @block.sync
        def _(sp):
            sp.dma_start(x_res[:, 0:TB, :], x_in[:, 0:TB, :]).then_inc(x_first, 16)
            sp.dma_start(ctx_f[:, :, :], ctx_t[0]).then_inc(ctx_in, 16)
            sp.dma_start(raw[:, 0], w_t[0]).then_inc(w_in[0], 16)
            sp.dma_start(raw[:, 1], w_t[1]).then_inc(w_in[1], 16)
            sp.dma_start(row[:, :, :], rows).then_inc(rows_in, 16)
            sp.dma_start(gate_sb[:, :], gate).then_inc(rows_in, 16)
            for n in (2, 3):
                sp.wait_ge(w_lo_done, n - 1)
                sp.dma_start(raw[:, n % 2], w_t[n]).then_inc(w_in[n % 2], 16)
            sp.dma_start(x_res[:, TB:, :], x_in[:, TB:, :]).then_inc(x_rest, 16)
            with sp.Fori(1, BATCH) as b:
                wait_apart(sp, ctx_lo_done, b, begun)
                sp.dma_start(ctx_f[:, :, :], ctx_t[bass.ds(b, 1)].rearrange("b p c t -> p (b c) t")).then_inc(ctx_in, 16)

        @block.gpsimd
        def _(pool):
            pool.memset(q_head[:, :, :, :], 0.0).then_inc(zeroed, 1)

            def context_low(b, ahead):
                pool.wait_ge(ring_ready, ring_base(b, ahead))
                pool.wait_ge(ctx_hi_done, b + ahead + 1)
                pool.tensor_tensor(ctx_lo[:, :, :], ctx_f[:, :, :], f32(ctx_hi[:, :, :]), ALU.subtract).then_inc(ctx_lo_done, 1)

            def sample(b, last):
                for u in range(UNITS):
                    att.normalise(pool, b, u)
                    if u == 0 and not last:
                        context_low(b, 1)

            context_low(0, 0)
            with pool.Fori(0, BATCH - 1) as b:
                sample(b, False)
            sample(BATCH - 1, True)

        @block.tensor
        def _(pe):
            def use(k0, k, emit, count=1):
                if not isinstance(k0, int) or k0 + k >= 2:
                    pe.wait_ge(ring_free, k0 + (k - 1))
                emit(ring[:, k % 2, :]).then_inc(ring_ready, count)

            def turned(of):
                def emit(bank):
                    for c in range(C):
                        mm = pe.transpose(bank[:, c * P:(c + 1) * P], of[:, c * P:(c + 1) * P], ident[:, :])
                    return mm
                return emit

            def projected(hi, lo, n, t):
                def emit(bank):
                    for c in range(C):
                        mm = split_product(pe, bank, (hi[:, c, t * P:(t + 1) * P], lo[:, c, t * P:(t + 1) * P]),
                                           (w_hi[n][:, c, :], w_lo[n][:, c, :]), c == 0, c == C - 1)
                    return mm
                return emit

            def front(b, ahead, u):
                k0 = ring_base(b, ahead)
                if u == 1:
                    pe.wait_ge(xn_done, TB * (b + ahead) + TB)
                    for t in range(TB):
                        use(k0, t, turned(xn[:, t, :]))
                if u in (2, 3):
                    if isinstance(b, int) and b + ahead == 0:
                        pe.wait_ge(w_lo_done, 1)
                    pe.wait_ge(ring_free, k0 + TB)
                    use(k0, u, projected(xt_hi, xt_lo, 0, u - 2))
                if 4 <= u < 8:
                    if isinstance(b, int) and b + ahead == 0:
                        pe.wait_ge(w_lo_done, u // 2)
                    pe.wait_ge(ctx_lo_done, b + ahead + 1)
                    use(k0, u, projected(ctx_hi, ctx_lo, u // 2 - 1, u % 2))
                if u == 8:
                    pe.wait_ge(k_hat_done, TB * (b + ahead) + TB)
                    for t in range(TB):
                        use(k0, 8 + t, turned(kf[:, t, :]))
                    for t in range(TB):
                        use(k0, 10 + t, turned(qf[:, t, :]), 1 + TB * (t == TB - 1 and ahead == 0))

            def weigh(b, u, par):
                if u % 2 == 0 and u >= 2:
                    att.weigh(pe, b, u // 2 - 1, par, lambda g, j, t: v[:, par, t, (4 * g + j) * HD:(4 * g + j + 1) * HD],
                              lambda g, j: att.o_ps[HD * j:HD * (j + 1), g % 2, 0:SEQ], 2)

            def attend(b, u, par):
                if u < UNITS:
                    att.scores(pe, b, u, lambda u, j: q_head[:, j, u // 2, (u % 2) * P:(u % 2 + 1) * P], lambda u, j: kt[:, u // 2, :])
                weigh(b, u - 1, par)
                if u >= 1:
                    att.turn(pe, b, u - 1)

            def sample(b, par, last):
                pe.wait_ge(ring_free, ring_base(b, 0) + FRONT)
                for u in range(UNITS):
                    attend(b, u, par)
                    if not last:
                        front(b, 1, u)
                if not last:
                    front(b, 1, 8)
                attend(b, UNITS, par)
                weigh(b, UNITS, par)
                pe.wait_ge(att.o_lo_done, UNITS // 2 * (b + 1))
                k0 = output_uses(b, last)
                for t in range(TB):
                    use(k0, t, projected(o_hi, o_lo, 3, t))

            pe.wait_ge(begun, 1)
            for u in range(9):
                front(0, 0, u)
            with pe.Fori(0, BATCH // 2 - 1) as i:
                for par in range(2):
                    sample(i * 2 + par, par, False)
            sample(BATCH - 2, 0, False)
            sample(BATCH - 1, 1, True)

        @block.scalar
        def _(act):
            def context_high(b, ahead):
                act.wait_ge(ctx_in, 16 * (b + ahead) + 16)
                act.wait_ge(ring_ready, ring_base(b, ahead))
                act.activation(ctx_hi[:, :, :], ctx_f[:, :, :], ACT.Copy).then_inc(ctx_hi_done, 1)

            def front(b, ahead, u):
                k0 = ring_base(b, ahead)
                if u == 1:
                    act.wait_ge(ring_ready, k0)
                    for t in range(TB):
                        act.wait_ge(ring_ready, k0 + t + 1)
                        act.activation(xt_hi[:, :, t * P:(t + 1) * P], chunks(ring[:, t, :]),
                                       ACT.Copy).then_inc(xt_hi_done, 1)
                if 2 <= u < 6:
                    act.wait_ge(ring_free, k0 + u + 1)
                    of = (qf if u < 4 else kf)[:, u % 2, :]
                    act.wait_ge(squared, 4 * (b + ahead) + u - 2)
                    act.activation(junk[:, :], of, ACT.Square, accum_out=sq_sum[:, u // 2 - 1, u % 2:u % 2 + 1]).then_inc(squared, 1)
                if u == 8:
                    for t in range(TB):
                        act.wait_ge(ring_ready, k0 + 10 + t + 1)
                        for j in range(3):
                            ins = act.activation(q_head[HD * j:HD * (j + 1), j, :, t * P:(t + 1) * P],
                                                 chunks(ring[HD * j:HD * (j + 1), t, :]), ACT.Copy)
                        ins.then_inc(q_act_done, 1)

            def output(b, u):
                for g in groups_done(u):
                    if g == 0:
                        act.wait_ge(ring_ready, ring_base(b, 1))
                    att.output_high(act, b, g, o_hi[:, g, :], att.o_ps[:, g % 2, 0:SEQ])

            def sample(b, par, last):
                for u in range(UNITS + 1):
                    if u < UNITS:
                        if u == 0:
                            act.wait_ge(q_scaled, b + 1)
                        att.exponentials(act, b, u, q_scale[:, par, u % 2:u % 2 + 1])
                    if u == UNITS and not last:
                        front(b, 1, 8)
                    if u == 0 and not last:
                        context_high(b, 1)
                    if u >= 1:
                        att.copy_turned(act, b, u - 1, 1, par)
                    output(b, u)
                    if u < UNITS and not last:
                        front(b, 1, u)

            act.wait_ge(rows_in, 32)
            act.activation(gain[:, :], gate_sb[:, :], ACT.Tanh).then_inc(gain_done, 1)
            context_high(0, 0)
            act.wait_ge(zeroed, 1)
            for u in range(9):
                if u % 2 == 0 and u >= 2:
                    n = u // 2 - 1
                    act.wait_ge(w_in[n % 2], 16 * (n // 2) + 16)
                    act.activation(w_hi[n][:, :, :], raw[:, n % 2], ACT.Copy).then_inc(w_hi_done, 1)
                front(0, 0, u)
            with act.Fori(0, BATCH // 2 - 1) as i:
                for par in range(2):
                    sample(i * 2 + par, par, False)
            sample(BATCH - 2, 0, False)
            sample(BATCH - 1, 1, True)

        @block.vector
        def _(dve):
            chain = Chain(dve, steps, begun)

            norms = Chain(dve, norm_of.steps, begun)

            def norm(b, ahead):
                dve.wait_ge(ring_ready, ring_base(b, ahead))
                for t in range(TB):
                    norm_of.normalised(dve, xn[:, t, :], (b + ahead) * TB + t).then_inc(xn_done, 1)

            def front(b, ahead, u, par):
                k0 = ring_base(b, ahead)
                if u == 1:
                    for t in range(TB):
                        dve.wait_ge(xt_hi_done, TB * (b + ahead) + t + 1)
                        dve.tensor_tensor(xt_lo[:, :, t * P:(t + 1) * P], chunks(ring[:, t, :]),
                                          f32(xt_hi[:, :, t * P:(t + 1) * P]), ALU.subtract).then_inc(ring_free, 1)
                if u == 6:
                    dve.wait_ge(squared, 4 * (b + ahead) + 4)
                    chain.turn(STEPS * (b + ahead))
                    chain.step(dve.tensor_scalar(qk_var[:, :, :], sq_sum[:, :, :], 1.0 / D, RMS_EPS, ALU.mult, ALU.add))
                    chain.wait()
                    inverse_sqrt(dve, chain, qk_rstd[:, :, :], qk_var[:, :, :], qk_tmp[:, :, :])
                    chain.wait()
                    dve.tensor_scalar(q_scale[:, par, :], qk_rstd[:, 0, :], SCALE, None, ALU.mult).then_inc(q_scaled, 1)
                    for t in range(TB):
                        dve.scalar_tensor_tensor(kf[:, t, :], kf[:, t, :], qk_rstd[:, 1, t:t + 1], row[:, NQ, :], ALU.mult,
                                                 ALU.mult).then_inc(k_hat_done, 1)
                if 2 <= u < 8:
                    dve.wait_ge(ring_ready, k0 + u + 1)
                    to = (qf[:, u % 2, :], kf[:, u % 2, :], v[:, par, u % 2, :])[u // 2 - 1]
                    ins = dve.tensor_tensor(to, ring[:, u % 2, :], row[:, u // 2 - 1, :], ALU.add)
                    ins.then_inc(ring_free, 1)
                if u == 8:
                    for t in range(TB):
                        dve.wait_ge(ring_ready, k0 + 8 + t + 1)
                        dve.tensor_copy(kt[:, :, t * P:(t + 1) * P], chunks(ring[:, t, :])).then_inc(ring_free, 1)
                    for t in range(TB):
                        dve.wait_ge(q_act_done, TB * (b + ahead) + t + 1)
                        dve.tensor_copy(q_head[3 * HD:, 3, :, t * P:(t + 1) * P], chunks(ring[3 * HD:, t, :])).then_inc(
                            ring_free, 1 + TB * (t == TB - 1 and ahead == 0))

            def sample(b, par, last):
                for u in range(UNITS + 1):
                    if u < UNITS:
                        att.find_peak(dve, b, u, q_scale[:, par, u % 2:u % 2 + 1])
                    if u == UNITS and not last:
                        front(b, 1, 8, 1 - par)
                    if u == 0 and not last:
                        norm(b, 1)
                    if u >= 1:
                        att.copy_turned(dve, b, u - 1, 0, par)
                    if u < UNITS:
                        att.invert_mass(dve, b, u)
                    if u < UNITS and not last:
                        front(b, 1, u, 1 - par)
                    for g in groups_done(u):
                        att.output_low(dve, b, g, o_lo[:, g, :], o_hi[:, g, :], att.o_ps[:, g % 2, 0:SEQ])
                k0 = output_uses(b, last)
                for t in range(TB):
                    x = tile_of(x_res, b * TB + t)
                    dve.wait_ge(ring_ready, k0 + t + 1)
                    dve.scalar_tensor_tensor(x, ring[:, t, :], gain[:, 0:1], x, ALU.mult, ALU.add).then_inc(ring_free, 1)
                    dve.wait_ge(ring_free, k0 + t + 1)
                    dve.tensor_tensor(x, x, row[:, OB, :], ALU.add).then_inc(x_done, 1)

            dve.wait_ge(x_first, 16)
            norm_of.find_spread(dve, norms, 0, TB)
            norm(0, 0)
            dve.wait_ge(rows_in, 32)
            dve.wait_ge(gain_done, 1)
            dve.tensor_scalar(row[:, OB, :], row[:, OB, :], gain[:, 0:1], None, ALU.mult).then_inc(rows_done, 1)
            dve.tensor_tensor(row[:, NQ, :], row[:, NQ, :], row[:, NK, :], ALU.mult).then_inc(rows_done, 1)
            dve.wait_ge(rows_done, 2)
            for u in range(9):
                if u % 2 == 0 and u >= 2:
                    n = u // 2 - 1
                    dve.wait_ge(w_hi_done, n + 1)
                    dve.tensor_tensor(w_lo[n][:, :, :], raw[:, n % 2], f32(w_hi[n][:, :, :]), ALU.subtract).then_inc(w_lo_done, 1)
                front(0, 0, u, 0)
            dve.wait_ge(x_rest, 16)
            norm_of.find_spread(dve, norms, TB, TILES)
            with dve.Fori(0, BATCH // 2 - 1) as i:
                for par in range(2):
                    sample(i * 2 + par, par, False)
            sample(BATCH - 2, 0, False)
            sample(BATCH - 1, 1, True)


def quantised_ffn(nc, x_res, ident, begun, w_dram, ln_row, gate):
    F = 2048
    FC = F // P
    NB = F // 512
    WEIGHTS = D * F

    with ExitStack() as ctx:
        def sb(name, shape, dt=F32):
            return ctx.enter_context(nc.sbuf_tensor(f"b_{name}", shape, dt))

        def sem(name):
            return nc.alloc_semaphore(f"b_{name}")

        wq = [sb(f"wq{n}", [P, WEIGHTS // P], BF16) for n in range(3)]
        w_mean = sb("w_mean", [P, 3])
        gate_sb, gain = sb("gate_sb", [P, 1]), sb("gain", [P, 1])
        lnw = sb("lnw", [P, F])
        ident_b = sb("ident_b", [P, P], BF16)
        norm_of = Norm(nc, "b", x_res, begun, ctx.enter_context)

        with ExitStack() as prep:
            raw = [prep.enter_context(nc.sbuf_tensor(f"b_raw{n}", [P, WEIGHTS // P], F32)) for n in range(3)]
            ones = prep.enter_context(nc.sbuf_tensor("b_ones", [P, P], F32))
            part, scale = (prep.enter_context(nc.sbuf_tensor(f"b_{n}", [P, 3], F32)) for n in ("part", "scale"))
            total = prep.enter_context(nc.psum_tensor("b_total", [P, 512], F32))
            w_in = [sem(f"w_in{n}") for n in range(3)]
            small_in, summed, ones_done, total_ready, scaled, spread, rounded = (
                sem(n) for n in ("small_in", "summed", "ones_done", "total_ready", "scaled", "spread", "rounded"))
            block = prep.enter_context(nc.Block())

            @block.sync
            def _(sp):
                for n in range(3):
                    sp.dma_start(raw[n][:, :], w_dram[n]).then_inc(w_in[n], 16)
                sp.dma_start(gate_sb[:, :], gate).then_inc(small_in, 16)
                sp.dma_start(lnw[:, :], ln_row).then_inc(small_in, 16)

            @block.scalar
            def _(act):
                def sum_up(n):
                    act.wait_ge(w_in[n], 16)
                    act.activation(wq[n][:, :], raw[n][:, :], ACT.Abs, accum_out=part[:, n:n + 1]).then_inc(summed, 1)

                def round_off(n):
                    act.wait_ge(spread, 2 * n + 2)
                    act.activation(wq[n][:, :], raw[n][:, :], ACT.Copy, bias=-ROUND).then_inc(rounded, 1)

                sum_up(0)
                sum_up(1)
                round_off(0)
                sum_up(2)
                round_off(1)
                act.wait_ge(small_in, 32)
                act.activation(gain[:, :], gate_sb[:, :], ACT.Tanh)
                round_off(2)

            @block.tensor
            def _(pe):
                pe.wait_ge(ones_done, 1)
                for n in range(3):
                    pe.wait_ge(summed, n + 1)
                    pe.wait_ge(scaled, 2 * n)
                    pe.matmul(total[:, n:n + 1], ones[:, :], part[:, n:n + 1], start=True, stop=True).then_inc(total_ready, 1)

            @block.vector
            def _(dve):
                dve.memset(ones[:, :], 1.0).then_inc(ones_done, 1)
                dve.tensor_copy(ident_b[:, :], ident[:, :])
                norm_of.find_spread(dve, Chain(dve, norm_of.steps, begun), 0, TILES)
                for n in range(3):
                    one = slice(n, n + 1)
                    dve.wait_ge(total_ready, n + 1)
                    dve.tensor_scalar(w_mean[:, one], total[:, one], 1.0 / WEIGHTS, 1e-5, ALU.mult, ALU.max).then_inc(scaled, 1)
                    dve.wait_ge(scaled, 2 * n + 1)
                    dve.reciprocal(scale[:, one], w_mean[:, one]).then_inc(scaled, 1)
                    dve.wait_ge(scaled, 2 * n + 2)
                    dve.tensor_scalar(raw[n][:, :], raw[n][:, :], scale[:, one], 1.0, ALU.mult, ALU.min).then_inc(spread, 1)
                    dve.wait_ge(spread, 2 * n + 1)
                    dve.tensor_scalar(raw[n][:, :], raw[n][:, :], -1.0, ROUND, ALU.max, ALU.add).then_inc(spread, 1)

        xn = sb("xn", [P, TB, D])
        xq = sb("xq", [P, TB, D], BF16)
        xqt = sb("xqt", [P, C, TB, P], BF16)
        sg = sb("sg", [P, 2, 512])
        h = sb("h", [P, 2, F])
        hw = sb("hw", [P, 2, F])
        hq = sb("hq", [P, 2, F], BF16)
        hqt = sb("hqt", [P, FC, P], BF16)
        junk = sb("junk", [P, 512], BF16)
        h_var, h_tmp = sb("h_var", [P, 1]), sb("h_tmp", [P, 1])
        x_peak, x_scale = sb("x_peak", [P, TB]), sb("x_scale", [P, TB])
        up_scale, gate_scale = sb("up_scale", [P, TB]), sb("gate_scale", [P, TB])
        sq_sum, h_peak = sb("sq_sum", [P, 2, NB]), sb("h_peak", [P, 2, NB])
        sq_all, h_all, h_rstd, h_scale, down_scale = (sb(n, [P, 2]) for n in ("sq_all", "h_all", "h_rstd", "h_scale", "down_scale"))
        g_ps = ctx.enter_context(nc.psum_tensor("b_g_ps", [P, 2, 512], F32))
        u_ps = ctx.enter_context(nc.psum_tensor("b_u_ps", [P, 2, 512], F32))
        xt_ps = ctx.enter_context(nc.psum_tensor("b_xt_ps", [P, C, TB, P], BF16))
        ht_ps = ctx.enter_context(nc.psum_tensor("b_ht_ps", [P, 2, FC // 2, P], BF16))
        d_ps = ctx.enter_context(nc.psum_tensor("b_d_ps", [P, 512], F32))
        steps, xn_done, spread_x, xq_done, xt_ready, xqt_done = (sem(n) for n in ("steps", "xn_done", "spread_x", "xq_done", "xt_ready", "xqt_done"))
        g_ready, u_ready, sg_done, h_done, hw_done, squared = (sem(n) for n in ("g_ready", "u_ready", "sg_done", "h_done", "hw_done", "squared"))
        spread_h, hq_done, ht_ready, hqt_dve, hqt_act, d_ready, x_done = (
            sem(n) for n in ("spread_h", "hq_done", "ht_ready", "hqt_dve", "hqt_act", "d_ready", "x_done"))
        scales_half, scales_done, down_done = sem("scales_half"), sem("scales_done"), sem("down_done")
        down_gain = sb("down_gain", [P, 1])
        block = ctx.enter_context(nc.Block())
        w_gate, w_up = (wq[n][:, :].rearrange("p (c n) -> p c n", c=C) for n in (0, 1))
        w_down = wq[2][:, :].rearrange("p (k n) -> p k n", k=FC)
        PAIRS = TILES // 2

        @block.gpsimd
        def _(pool):
            def weight(n, par):
                if not isinstance(n, int):
                    pool.wait_ge(hq_done, n - 1)
                for k in range(NB):
                    pool.wait_ge(h_done, n * NB + k + 1)
                    cols = slice(k * 512, (k + 1) * 512)
                    pool.tensor_tensor(hw[:, par, cols], h[:, par, cols], lnw[:, cols], ALU.mult).then_inc(hw_done, 1)

            weight(0, 0)
            weight(1, 1)
            with pool.Fori(1, PAIRS) as i:
                for par in range(2):
                    weight(i * 2 + par, par)

        @block.tensor
        def _(pe):
            def turn_x(i):
                pe.wait_ge(xq_done, i + 1)
                pe.wait_ge(xqt_done, i)
                for t in range(TB):
                    for c in range(C):
                        mm = pe.transpose(xt_ps[:, c, t, :], xq[:, t, c * P:(c + 1) * P], ident_b[:, :])
                mm.then_inc(xt_ready, 1)

            def up(i, t):
                n = i * 2 + t
                pe.wait_ge(xqt_done, i + 1)
                for k in range(NB):
                    for ps, w, free, ready in ((g_ps, w_gate, sg_done, g_ready), (u_ps, w_up, h_done, u_ready)):
                        if not isinstance(n, int) or n * NB + k >= 2:
                            pe.wait_ge(free, n * NB + (k - 1))
                        for c in range(C):
                            mm = pe.matmul(ps[:, k % 2, :], xqt[:, c, t, :], w[:, c, k * 512:(k + 1) * 512], start=c == 0, stop=c == C - 1)
                        mm.then_inc(ready, 1)

            def down(n, par):
                pe.wait_ge(hq_done, n + 1)
                pe.wait_ge(hqt_dve, n)
                pe.wait_ge(hqt_act, n)
                for k in range(FC):
                    mm = pe.transpose(ht_ps[:, k // 8, k % 8, :], hq[:, par, k * P:(k + 1) * P], ident_b[:, :])
                    if k % 8 == 7:
                        mm.then_inc(ht_ready, 1)
                pe.wait_ge(x_done, n)
                for k in range(FC):
                    if k % 8 == 0:
                        pe.wait_ge((hqt_dve, hqt_act)[k // 8], n + 1)
                    mm = pe.matmul(d_ps[:, :], hqt[:, k, :], w_down[:, k, :], start=k == 0, stop=k == FC - 1)
                mm.then_inc(d_ready, 1)

            def pair(i, first, last):
                up(i, 0)
                if not first:
                    down(i * 2 - 1, 1)
                up(i, 1)
                if not last:
                    turn_x(i + 1)
                down(i * 2, 0)

            turn_x(0)
            pair(0, True, False)
            with pe.Fori(1, PAIRS - 1) as i:
                pair(i, False, False)
            pair(PAIRS - 1, False, True)
            down(TILES - 1, 1)

        @block.scalar
        def _(act):
            def round_x(i):
                act.wait_ge(spread_x, i * TB + TB)
                act.wait_ge(xt_ready, i)
                act.activation(xq[:, :, :], xn[:, :, :], ACT.Copy, bias=-ROUND).then_inc(xq_done, 1)

            def copy_x(i, first):
                act.wait_ge(xt_ready, i + 1)
                if not first:
                    act.wait_ge(u_ready, i * 2 * NB)
                act.activation(xqt[:, :, :, :], xt_ps[:, :, :, :], ACT.Copy).then_inc(xqt_done, 1)

            def up(i, t, first=False):
                n = i * 2 + t

                def square(k):
                    act.wait_ge(h_done, n * NB + k + 1)
                    act.wait_ge(squared, n * NB + k)
                    act.activation(junk[:, :], h[:, t, k * 512:(k + 1) * 512], ACT.Square, accum_out=sq_sum[:, t, k:k + 1]).then_inc(squared, 1)

                act.wait_ge(scales_done, i + 1)
                for k in range(NB):
                    act.wait_ge(g_ready, n * NB + k + 1)
                    if not isinstance(n, int) or n * NB + k >= 2:
                        act.wait_ge(h_done, n * NB + (k - 1))
                    act.activation(sg[:, k % 2, :], g_ps[:, k % 2, :], ACT.Silu, scale=gate_scale[:, t:t + 1]).then_inc(sg_done, 1)
                    if k == 1 and not first:
                        round_h(n - 1, 1 - t)
                    if k >= 1:
                        square(k - 1)
                square(NB - 1)

            def round_h(n, par):
                act.wait_ge(spread_h, n + 1)
                act.activation(hq[:, par, :], hw[:, par, :], ACT.Copy, bias=-ROUND).then_inc(hq_done, 1)

            def copy_h(n):
                act.wait_ge(ht_ready, n * 2 + 2)
                act.wait_ge(d_ready, n)
                act.activation(hqt[:, FC // 2:, :], ht_ps[:, 1], ACT.Copy).then_inc(hqt_act, 1)

            def pair(i, first, last):
                up(i, 0, first)
                if not first:
                    copy_h(i * 2 - 1)
                up(i, 1)
                if not last:
                    round_x(i + 1)
                    copy_x(i + 1, False)
                copy_h(i * 2)

            round_x(0)
            copy_x(0, True)
            pair(0, True, False)
            with act.Fori(1, PAIRS - 1) as i:
                pair(i, False, False)
            pair(PAIRS - 1, False, True)
            round_h(TILES - 1, 1)
            copy_h(TILES - 1)

        @block.vector
        def _(dve):
            chain = Chain(dve, steps, begun)
            X_STEPS = 3
            H_STEPS = INVERSE_SQRT_STEPS + 7
            PAIR_STEPS = X_STEPS + 2 * H_STEPS

            def quantise_x(i):
                dve.wait_ge(xq_done, i)
                for t in range(TB):
                    norm_of.normalised(dve, xn[:, t, :], i * TB + t).then_inc(xn_done, 1)
                dve.wait_ge(xn_done, i * TB + TB)
                chain.step(dve.tensor_reduce(x_peak[:, :], xn[:, :, :], AX.X, ALU.max, apply_absolute_value=True))
                chain.wait()
                chain.step(dve.tensor_scalar(x_peak[:, :], x_peak[:, :], 1e-5, 1.0 / 127.0, ALU.max, ALU.mult))
                chain.wait()
                chain.step(dve.reciprocal(x_scale[:, :], x_peak[:, :]))
                chain.wait()
                for t in range(TB):
                    dve.tensor_scalar(xn[:, t, :], xn[:, t, :], x_scale[:, t:t + 1], ROUND, ALU.mult, ALU.add).then_inc(spread_x, 1)

            def scales(i):
                dve.wait_ge(squared, i * 2 * NB)
                dve.tensor_scalar(up_scale[:, :], x_peak[:, :], w_mean[:, 1:2], None, ALU.mult).then_inc(scales_half, 1)
                dve.tensor_scalar(gate_scale[:, :], x_peak[:, :], w_mean[:, 0:1], None, ALU.mult).then_inc(scales_done, 1)

            def up(i, t):
                n = i * 2 + t
                dve.wait_ge(scales_half, i + 1)
                dve.wait_ge(squared, i * 2 * NB)
                dve.wait_ge(hw_done, i * 2 * NB)
                for k in range(NB):
                    dve.wait_ge(u_ready, n * NB + k + 1)
                    dve.wait_ge(sg_done, n * NB + k + 1)
                    cols = slice(k * 512, (k + 1) * 512)
                    dve.scalar_tensor_tensor(h[:, t, cols], u_ps[:, k % 2, :], up_scale[:, t:t + 1], sg[:, k % 2, :],
                                             ALU.mult, ALU.mult).then_inc(h_done, 1)
                    if k >= 2:
                        peak(n, t, k - 2)

            def peak(n, t, k):
                dve.wait_ge(hw_done, n * NB + k + 1)
                return dve.tensor_reduce(h_peak[:, t, k:k + 1], hw[:, t, k * 512:(k + 1) * 512], AX.X, ALU.max, apply_absolute_value=True)

            def quantise_h(n, t):
                one = slice(t, t + 1)
                peak(n, t, NB - 2)
                chain.step(peak(n, t, NB - 1))
                dve.wait_ge(squared, n * NB + NB)
                chain.step(dve.tensor_reduce(sq_all[:, one], sq_sum[:, t, :], AX.X, ALU.add))
                chain.wait()
                chain.step(dve.tensor_scalar(h_var[:, :], sq_all[:, one], 1.0 / F, RMS_EPS, ALU.mult, ALU.add))
                chain.wait()
                inverse_sqrt(dve, chain, h_rstd[:, one], h_var[:, :], h_tmp[:, :])
                chain.wait()
                chain.step(dve.tensor_reduce(h_all[:, one], h_peak[:, t, :], AX.X, ALU.max))
                chain.wait()
                chain.step(dve.tensor_scalar(h_all[:, one], h_all[:, one], h_rstd[:, one], 1e-5, ALU.mult, ALU.max))
                chain.wait()
                chain.step(dve.reciprocal(h_scale[:, one], h_all[:, one]))
                dve.tensor_scalar(down_scale[:, one], h_all[:, one], down_gain[:, 0:1], None, ALU.mult).then_inc(down_done, 1)
                chain.wait()
                chain.step(dve.tensor_scalar(h_scale[:, one], h_scale[:, one], h_rstd[:, one], 127.0, ALU.mult, ALU.mult))
                chain.wait()
                dve.tensor_scalar(hw[:, t, :], hw[:, t, :], h_scale[:, one], ROUND, ALU.mult, ALU.add).then_inc(spread_h, 1)

            def copy_h(n):
                dve.wait_ge(ht_ready, n * 2 + 1)
                dve.wait_ge(d_ready, n)
                dve.tensor_copy(hqt[:, 0:FC // 2, :], ht_ps[:, 0]).then_inc(hqt_dve, 1)

            def add_to_x(n, par):
                dve.wait_ge(d_ready, n + 1)
                dve.wait_ge(down_done, n + 1)
                x = tile_of(x_res, n)
                dve.scalar_tensor_tensor(x, d_ps[:, :], down_scale[:, par:par + 1], x, ALU.mult, ALU.add).then_inc(x_done, 1)

            def pair(i, first, last):
                chain.turn(PAIR_STEPS * i + (X_STEPS + 1))
                scales(i)
                up(i, 0)
                if not first:
                    copy_h(i * 2 - 1)
                quantise_h(i * 2, 0)
                if not first:
                    add_to_x(i * 2 - 1, 1)
                if not last:
                    quantise_x(i + 1)
                up(i, 1)
                copy_h(i * 2)
                quantise_h(i * 2 + 1, 1)
                add_to_x(i * 2, 0)

            chain.turn(0)
            chain.step(dve.tensor_scalar(down_gain[:, :], w_mean[:, 2:3], gain[:, 0:1], 1.0 / 127.0, ALU.mult, ALU.mult))
            quantise_x(0)
            pair(0, True, False)
            with dve.Fori(1, PAIRS - 1) as i:
                pair(i, False, False)
            pair(PAIRS - 1, False, True)
            copy_h(TILES - 1)
            add_to_x(TILES - 1, 1)


def cross_attention(nc, x_res, ident, begun, xnt_dram, ctx_t, w_t, gate):
    HD = 2048 // NH
    GROUPS = NH // 4
    SCALE = float(HD) ** -0.5
    FRONT, TURN = 6, 6 + TB

    with ExitStack() as ctx:
        def sb(name, shape, dt=F32):
            return ctx.enter_context(nc.sbuf_tensor(f"cn_{name}", shape, dt))

        def sem(name):
            return nc.alloc_semaphore(f"cn_{name}")

        xn, xt = sb("xn", [P, 2, TB, D]), sb("xt", [P, 2, C, SEQ])
        norm_of = Norm(nc, "cn", x_res, begun, ctx.enter_context)
        bank = ctx.enter_context(nc.psum_tensor("cn_bank", [P, 2, TB, 512], F32))
        xn_done, turned, copied, stored = sem("xn_done"), sem("turned"), sem("copied"), [sem("stored0"), sem("stored1")]
        block = ctx.enter_context(nc.Block())

        @block.vector
        def _(dve):
            norm_of.find_spread(dve, Chain(dve, norm_of.steps, begun), 0, TILES)

            def norm(b, par):
                if not isinstance(b, int):
                    dve.wait_ge(turned, b - 1)
                for t in range(TB):
                    ins = norm_of.normalised(dve, xn[:, par, t, :], b * TB + t)
                ins.then_inc(xn_done, 1)

            norm(0, 0)
            norm(1, 1)
            with dve.Fori(1, BATCH // 2) as i:
                for par in range(2):
                    norm(i * 2 + par, par)

        @block.tensor
        def _(pe):
            def turn(b, par):
                pe.wait_ge(xn_done, b + 1)
                if not isinstance(b, int):
                    pe.wait_ge(copied, b - 1)
                for t in range(TB):
                    for c in range(C):
                        mm = pe.transpose(bank[:, par, t, c * P:(c + 1) * P], xn[:, par, t, c * P:(c + 1) * P], ident[:, :])
                mm.then_inc(turned, 1)

            turn(0, 0)
            turn(1, 1)
            with pe.Fori(1, BATCH // 2) as i:
                for par in range(2):
                    turn(i * 2 + par, par)

        @block.scalar
        def _(act):
            with act.Fori(0, BATCH // 2) as i:
                for par in range(2):
                    b = i * 2 + par
                    act.wait_ge(turned, b + 1)
                    act.wait_ge(stored[par], i * 16)
                    for t in range(TB):
                        ins = act.activation(xt[:, par, :, t * P:(t + 1) * P], chunks(bank[:, par, t, :]), ACT.Copy)
                    ins.then_inc(copied, 1)

        @block.sync
        def _(sp):
            with sp.Fori(0, BATCH // 2) as i:
                for par in range(2):
                    b = i * 2 + par
                    wait_apart(sp, copied, b + 1, begun)
                    sp.dma_start(xnt_dram[bass.ds(b, 1)].rearrange("b p c t -> p (b c) t"), xt[:, par]).then_inc(stored[par], 16)
            for par in range(2):
                sp.wait_ge(stored[par], 16 * BATCH // 2)

    with ExitStack() as ctx:
        def sb(name, shape, dt=F32):
            return ctx.enter_context(nc.sbuf_tensor(f"c_{name}", shape, dt))

        def sem(name):
            return nc.alloc_semaphore(f"c_{name}")

        w_hi = [sb(f"w_hi{n}", [P, C, D], F32R) for n in range(4)]
        w_lo = [sb(f"w_lo{n}", [P, C, D], F32R) for n in range(4)]
        raw = sb("raw", [P, 2, C, D])
        gate_sb, gain = sb("gate_sb", [P, 1]), sb("gain", [P, 1])
        xt_f, ctx_f = sb("xt_f", [P, C, SEQ]), sb("ctx_f", [P, C, SEQ])
        xt_hi, xt_lo = sb("xt_hi", [P, C, SEQ], F32R), sb("xt_lo", [P, C, SEQ], F32R)
        ctx_hi, ctx_lo = sb("ctx_hi", [P, C, SEQ], F32R), sb("ctx_lo", [P, C, SEQ], F32R)
        qt, kt = sb("qt", [P, 2, 4, SEQ]), sb("kt", [P, 2, 4, SEQ])
        v = sb("v", [P, 2, TB, 4 * HD])
        o_hi, o_lo = sb("o_hi", [P, 4, SEQ], F32R), sb("o_lo", [P, 4, SEQ], F32R)
        att = Attention(nc, ctx, "c", begun, ident, TB, SCALE, 1)
        ring = ctx.enter_context(nc.psum_tensor("c_ring", [P, 2, 512], F32))
        gate_in, w_in, w_hi_done, w_lo_done, gain_done = sem("gate_in"), [sem("w_in0"), sem("w_in1")], sem("w_hi_done"), sem("w_lo_done"), sem("gain_done")
        xt_in, ctx_in, xt_hi_done, xt_lo_done = sem("xt_in"), sem("ctx_in"), sem("xt_hi_done"), sem("xt_lo_done")
        ctx_hi_done, ctx_lo_done, ring_ready, ring_free = sem("ctx_hi_done"), sem("ctx_lo_done"), sem("ring_ready"), sem("ring_free")
        block = ctx.enter_context(nc.Block())
        USES = TURN * BATCH + TB

        def front_base(g, b):
            return g * USES + (b * TURN + TURN)

        def turns(eng, head, turn):
            def group(g, end):
                head(g)
                with eng.Fori(0, BATCH // 2 - 1) as i:
                    for par in range(2):
                        turn(g, i * 2 + par, par, False, False)
                turn(g, BATCH - 2, 0, False, False)
                turn(g, BATCH - 1, 1, True, end)

            with eng.Fori(0, GROUPS - 1) as g:
                group(g, False)
            group(GROUPS - 1, True)

        @block.sync
        def _(sp):
            sp.dma_start(gate_sb[:, :], gate).then_inc(gate_in, 16)

            def load_weights(g, n):
                if not isinstance(g, int) or 4 * g + n >= 2:
                    wait_apart(sp, w_lo_done, g * 4 + (n - 1), begun)
                sp.dma_start(raw[:, n % 2], w_t[g, n] if isinstance(g, int) else
                             w_t[bass.ds(g, 1), n].rearrange("g p c n -> p (g c) n")).then_inc(w_in[n % 2], 16)

            def load_inputs(n, b):
                if not isinstance(n, int) or n > 0:
                    wait_apart(sp, xt_lo_done, n, begun)
                of = xnt_dram[b] if isinstance(b, int) else xnt_dram[bass.ds(b, 1)].rearrange("b p c t -> p (b c) t")
                sp.dma_start(xt_f[:, :, :], of).then_inc(xt_in, 16)
                if not isinstance(n, int) or n > 0:
                    wait_apart(sp, ctx_lo_done, n, begun)
                of = ctx_t[b] if isinstance(b, int) else ctx_t[bass.ds(b, 1)].rearrange("b p c t -> p (b c) t")
                sp.dma_start(ctx_f[:, :, :], of).then_inc(ctx_in, 16)

            load_weights(0, 0)
            load_inputs(0, 0)
            load_weights(0, 1)

            def head(g):
                load_weights(g, 2)
                load_inputs(g * BATCH + 1, 1)
                load_weights(g, 3)

            def turn(g, b):
                load_inputs(g * BATCH + b + 2, (b + 2) % BATCH if isinstance(b, int) else b + 2)

            def group(g):
                head(g)
                with sp.Fori(0, BATCH // 2 - 1) as i:
                    for par in range(2):
                        turn(g, i * 2 + par)
                turn(g, BATCH - 2)

            with sp.Fori(0, GROUPS - 1) as g:
                group(g)
                load_weights(g + 1, 0)
                load_weights(g + 1, 1)
            group(GROUPS - 1)

        @block.gpsimd
        def _(pool):
            def inputs_low(n):
                pool.wait_ge(xt_hi_done, n + 1)
                pool.tensor_tensor(xt_lo[:, :, :], xt_f[:, :, :], f32(xt_hi[:, :, :]), ALU.subtract).then_inc(xt_lo_done, 1)

            def context_low(n):
                pool.wait_ge(ctx_hi_done, n + 1)
                pool.tensor_tensor(ctx_lo[:, :, :], ctx_f[:, :, :], f32(ctx_hi[:, :, :]), ALU.subtract).then_inc(ctx_lo_done, 1)

            inputs_low(0)
            context_low(0)

            def head(g):
                inputs_low(g * BATCH + 1)
                context_low(g * BATCH + 1)

            def turn(g, b, par, last, end):
                s = g * BATCH + b
                att.normalise(pool, s, 0)
                att.normalise(pool, s, 1)
                if not last:
                    inputs_low(s + 2)
                    context_low(s + 2)

            turns(pool, head, turn)

        @block.tensor
        def _(pe):
            def use(k0, k, emit, first=False, count=1):
                pe.wait_ge(ring_free, k0 if first else k0 + (k - 1))
                emit(ring[:, k % 2, :]).then_inc(ring_ready, count)

            def heads(n, hi, lo, k):
                def emit(bank):
                    for h in range(2):
                        cols = slice((2 * k + h) * HD, (2 * k + h + 1) * HD)
                        for c in range(C):
                            mm = split_product(pe, bank[:, h * SEQ:(h + 1) * SEQ], (w_hi[n][:, c, cols], w_lo[n][:, c, cols]),
                                               (hi[:, c, :], lo[:, c, :]), c == 0, c == C - 1)
                    return mm
                return emit

            def tokens(n, hi, lo, t):
                def emit(bank):
                    for c in range(C):
                        mm = split_product(pe, bank, (hi[:, c, t * P:(t + 1) * P], lo[:, c, t * P:(t + 1) * P]),
                                           (w_hi[n][:, c, :], w_lo[n][:, c, :]), c == 0, c == C - 1)
                    return mm
                return emit

            def front(k0, k, n, first=False, count=1):
                if k == 0:
                    pe.wait_ge(xt_lo_done, n + 1)
                    use(k0, 0, heads(0, xt_hi, xt_lo, 0), first)
                if k == 1:
                    use(k0, 1, heads(0, xt_hi, xt_lo, 1))
                if k == 2:
                    pe.wait_ge(ctx_lo_done, n + 1)
                if k in (2, 3):
                    use(k0, k, heads(1, ctx_hi, ctx_lo, k - 2))
                if k in (4, 5):
                    use(k0, k, tokens(2, ctx_hi, ctx_lo, k - 4), False, count)

            def head(g):
                for k in range(FRONT):
                    if k % 2 == 0:
                        pe.wait_ge(w_lo_done, g * 4 + (k // 2 + 1))
                    front(g * USES, k, g * BATCH, k == 0, 1 + TB * (k == FRONT - 1))

            def turn(g, b, par, last, end):
                s, k0 = g * BATCH + b, front_base(g, b)

                def fronts(*ks):
                    if not last:
                        for k in ks:
                            front(k0, k, s + 1)

                q_of, k_of = (lambda u, j: qt[:, par, j, u * P:(u + 1) * P]), (lambda u, j: kt[:, par, j, :])
                pe.wait_ge(ring_free, k0 - TB)
                att.scores(pe, s, 0, q_of, k_of)
                fronts(0, 1)
                att.scores(pe, s, 1, q_of, k_of)
                att.turn(pe, s, 0)
                fronts(2, 3)
                att.turn(pe, s, 1)
                fronts(4)
                att.weigh(pe, s, 0, par, lambda g_, j, t: v[:, par, t, j * HD:(j + 1) * HD],
                          lambda g_, j: att.o_ps[:, j // 2, (j % 2) * SEQ:(j % 2 + 1) * SEQ], 1)
                fronts(5)
                pe.wait_ge(w_lo_done, g * 4 + 4)
                pe.wait_ge(att.o_lo_done, s + 1)
                for t in range(TB):
                    use(k0 + (0 if last else FRONT), t, tokens(3, o_hi, o_lo, t))

            turns(pe, head, turn)

        @block.scalar
        def _(act):
            def inputs_high(n, after):
                act.wait_ge(xt_in, n * 16 + 16)
                if after is not None:
                    act.wait_ge(ring_ready, after)
                    act.wait_ge(xt_lo_done, n)
                act.activation(xt_hi[:, :, :], xt_f[:, :, :], ACT.Copy).then_inc(xt_hi_done, 1)

            def context_high(n, after):
                act.wait_ge(ctx_in, n * 16 + 16)
                if after is not None:
                    act.wait_ge(ring_ready, after)
                act.activation(ctx_hi[:, :, :], ctx_f[:, :, :], ACT.Copy).then_inc(ctx_hi_done, 1)

            def weights_high(g, n):
                act.wait_ge(w_in[n % 2], g * 32 + (16 * (n // 2) + 16))
                act.activation(w_hi[n][:, :, :], raw[:, n % 2], ACT.Copy).then_inc(w_hi_done, 1)

            act.wait_ge(gate_in, 16)
            act.activation(gain[:, :], gate_sb[:, :], ACT.Tanh).then_inc(gain_done, 1)
            inputs_high(0, None)
            weights_high(0, 0)
            context_high(0, None)
            weights_high(0, 1)
            weights_high(0, 2)

            def head(g):
                act.wait_ge(ring_ready, g * USES)
                weights_high(g, 3)
                inputs_high(g * BATCH + 1, g * USES + 2)
                context_high(g * BATCH + 1, g * USES + FRONT)

            def turn(g, b, par, last, end):
                s, k0 = g * BATCH + b, front_base(g, b)
                att.exponentials(act, s, 0)
                att.exponentials(act, s, 1)
                if not last:
                    inputs_high(s + 2, k0 + 2)
                elif not end:
                    act.wait_ge(ring_ready, k0)
                    weights_high(g + 1, 0)
                att.copy_turned(act, s, 0, 1, par)
                att.copy_turned(act, s, 1, 1, par)
                act.wait_ge(ring_ready, k0)
                att.output_high(act, s, 0, o_hi[:, :, :], att.o_ps[:, :, :].rearrange("p k (j q) -> p (k j) q", j=2))
                if not last:
                    context_high(s + 2, k0 + FRONT)
                elif not end:
                    weights_high(g + 1, 1)
                    weights_high(g + 1, 2)

            turns(act, head, turn)

        @block.vector
        def _(dve):
            def front(k0, k, par, count=1):
                dve.wait_ge(ring_ready, k0 + k + 1)
                to = ((qt, kt)[k // 2][:, par, 2 * (k % 2):2 * (k % 2) + 2, :].rearrange("p j q -> p (j q)") if k < 4
                      else v[:, par, k - 4, :])
                dve.tensor_copy(to, ring[:, k % 2, :]).then_inc(ring_free, count)

            def weights_low(g, n):
                dve.wait_ge(w_hi_done, g * 4 + n + 1)
                dve.tensor_tensor(w_lo[n][:, :, :], raw[:, n % 2], f32(w_hi[n][:, :, :]), ALU.subtract).then_inc(w_lo_done, 1)

            dve.wait_ge(gain_done, 1)
            for n in range(3):
                weights_low(0, n)

            def head(g):
                for k in range(FRONT):
                    front(g * USES, k, 0, 1 + TB * (k == FRONT - 1))
                    if k == 1:
                        weights_low(g, 3)

            def turn(g, b, par, last, end):
                s, k0 = g * BATCH + b, front_base(g, b)

                def fronts(*ks):
                    if not last:
                        for k in ks:
                            front(k0, k, 1 - par)

                att.find_peak(dve, s, 0)
                fronts(0)
                att.invert_mass(dve, s, 0)
                fronts(1)
                att.find_peak(dve, s, 1)
                att.copy_turned(dve, s, 0, 0, par)
                fronts(2)
                att.invert_mass(dve, s, 1)
                fronts(3)
                if last and not end:
                    weights_low(g + 1, 0)
                att.copy_turned(dve, s, 1, 0, par)
                fronts(4)
                att.output_low(dve, s, 0, o_lo[:, :, :], o_hi[:, :, :], att.o_ps[:, :, :].rearrange("p k (j q) -> p (k j) q", j=2))
                fronts(5)
                if last and not end:
                    weights_low(g + 1, 1)
                    weights_low(g + 1, 2)
                for t in range(TB):
                    x = tile_of(x_res, b * TB + t)
                    dve.wait_ge(ring_ready, k0 + (0 if last else FRONT) + t + 1)
                    dve.scalar_tensor_tensor(x, ring[:, t, :], gain[:, 0:1], x, ALU.mult, ALU.add).then_inc(ring_free, 1)

            turns(dve, head, turn)


def latent_attention(nc, x_res, h_res, ident, begun, w_dram, ln_row, rope_dram):
    HD = D // NH
    RD = HD // 2
    HALF = NH * RD
    SCALE = float(HD) ** -0.5
    UNITS = NH // 4 * TB
    FRONT = 14
    TURN = FRONT + TB
    WIDTHS = (("kv_d", C * P), ("q_d", C * P), ("k_u", HALF), ("q_u", 2 * HALF), ("v_u", D), ("rope_k", C * HALF), ("o", C * D))
    W = sum(n for _, n in WIDTHS)

    with ExitStack() as ctx:
        def sb(name, shape, dt=F32):
            return ctx.enter_context(nc.sbuf_tensor(f"d_{name}", shape, dt))

        def sem(name):
            return nc.alloc_semaphore(f"d_{name}")

        w_hi, w_lo = sb("w_hi", [P, W], F32R), sb("w_lo", [P, W], F32R)
        ln = sb("ln_row", [P, D])
        rope = sb("rope_sb", [P, 2, TB, RD])
        a_rstd = sb("a_rstd", [P, TILES])
        ident_b, mask = sb("ident_b", [P, P], BF16), sb("mask", [P, P], BF16)

        with ExitStack() as prep:
            raw = prep.enter_context(nc.sbuf_tensor("d_raw", [P, W], F32))
            blank = prep.enter_context(nc.sbuf_tensor("d_blank", [P, P], F32))
            norm_of = Norm(nc, "d", x_res, begun, prep.enter_context)
            sq_sum, var, tmp = (prep.enter_context(nc.sbuf_tensor(f"d_{n}", [P, TILES], F32)) for n in ("sq_sum", "var", "tmp"))
            junk = prep.enter_context(nc.sbuf_tensor("d_junk", [P, D], BF16))
            w_in, small_in, w_hi_done, zeroed, masked = (sem(n) for n in ("w_in", "small_in", "w_hi_done", "zeroed", "masked"))
            y_done, squared = sem("y_done"), sem("squared")
            block = prep.enter_context(nc.Block())

            @block.sync
            def _(sp):
                sp.dma_start(raw[:, :], w_dram).then_inc(w_in, 16)
                sp.dma_start(ln[:, :], ln_row).then_inc(small_in, 16)
                sp.dma_start(rope[:, :, :, :], rope_dram).then_inc(small_in, 16)
                sp.wait_ge(small_in, 32)

            @block.gpsimd
            def _(pool):
                pool.memset(blank[:, :], 0.0).then_inc(zeroed, 1)
                pool.wait_ge(zeroed, 1)
                pool.affine_select(out=blank[:, :], in_=blank[:, :], compare_op=ALU.is_ge, fill=-1e30, base=0,
                                   pattern=[[-1, P]], channel_multiplier=1).then_inc(masked, 1)
                pool.wait_ge(w_hi_done, 1)
                pool.tensor_tensor(w_lo[:, :], raw[:, :], f32(w_hi[:, :]), ALU.subtract)

            @block.scalar
            def _(act):
                act.wait_ge(w_in, 16)
                act.activation(w_hi[:, :], raw[:, :], ACT.Copy).then_inc(w_hi_done, 1)
                with act.Fori(0, TILES) as n:
                    act.wait_ge(y_done, n + 1)
                    act.wait_ge(squared, n)
                    act.activation(junk[:, :], tile_of(h_res, n), ACT.Square, accum_out=sq_sum[:, bass.ds(n, 1)]).then_inc(squared, 1)

            @block.vector
            def _(dve):
                dve.wait_ge(masked, 1)
                dve.tensor_copy(mask[:, :], blank[:, :])
                dve.tensor_copy(ident_b[:, :], ident[:, :])
                chain = Chain(dve, norm_of.steps, begun)
                norm_of.find_spread(dve, chain, 0, TILES)
                with dve.Fori(0, TILES) as n:
                    norm_of.normalised(dve, tile_of(h_res, n), n).then_inc(y_done, 1)
                dve.wait_ge(squared, TILES)
                chain.step(dve.tensor_scalar(var[:, :], sq_sum[:, :], 1.0 / D, LN_EPS, ALU.mult, ALU.add))
                chain.wait()
                inverse_sqrt(dve, chain, a_rstd[:, :], var[:, :], tmp[:, :])

        at_col, parts = 0, {}
        for name, n in WIDTHS:
            parts[name] = [w[:, at_col:at_col + n] for w in (w_hi, w_lo)]
            at_col += n
        for name in ("kv_d", "q_d", "rope_k", "o"):
            parts[name] = [w.rearrange("p (c n) -> p c n", c=C) for w in parts[name]]

        a = sb("a", [P, TB, D])
        at_hi, at_lo = sb("at_hi", [P, C, SEQ], F32R), sb("at_lo", [P, C, SEQ], F32R)
        lat_hi, lat_lo = sb("lat_hi", [P, 2, SEQ], F32R), sb("lat_lo", [P, 2, SEQ], F32R)
        kf, qf = sb("kf", [P, TB, NH, HD]), sb("qf", [P, TB, NH, HD])
        rot = sb("rot", [P, 2, NH, RD])
        q_head = sb("q_head", [P, 4, C, SEQ])
        kt = sb("kt", [P, C, SEQ])
        v = sb("v", [P, 2, TB, D])
        o_hi, o_lo = sb("o_hi", [P, C, SEQ], F32R), sb("o_lo", [P, C, SEQ], F32R)
        att = Attention(nc, ctx, "d", begun, ident, UNITS, SCALE, 1, causal=True)
        ring = ctx.enter_context(nc.psum_tensor("d_ring", [P, 2, 512], F32))
        zeroed2, a_done = sem("zeroed2"), sem("a_done")
        ring_ready, ring_free, hi_done, turned_k, rotated, q_act_done = (
            sem(n) for n in ("ring_ready", "ring_free", "hi_done", "turned_k", "rotated", "q_act_done"))
        plain_done, products = sem("plain_done"), sem("products")
        block = ctx.enter_context(nc.Block())

        def ring_base(b, ahead):
            return TURN * (b + ahead)

        def groups_done(u):
            return [g for g in range(UNITS // 2) if min(2 * g + 3, UNITS) == u]

        def output_uses(b, last):
            return TURN * (b + 1) + (0 if last else FRONT)

        @block.gpsimd
        def _(pool):
            pool.memset(q_head[:, :, :, :], 0.0)
            pool.memset(att.prob_t[:, :, 1, :, 0:P], 0.0).then_inc(zeroed2, 1)

            def sample(b):
                for u in range(UNITS):
                    att.normalise(pool, b, u)

            with pool.Fori(0, BATCH) as b:
                sample(b)

        @block.tensor
        def _(pe):
            def use(k0, k, emit, count=1):
                if not isinstance(k0, int) or k0 + k >= 2:
                    pe.wait_ge(ring_free, k0 + (k - 1))
                emit(ring[:, k % 2, :]).then_inc(ring_ready, count)

            def turned(of):
                def emit(bank):
                    for c in range(C):
                        mm = pe.transpose(bank[:, c * P:(c + 1) * P], of[:, c * P:(c + 1) * P], ident[:, :])
                    return mm
                return emit

            def latents(w):
                def emit(bank):
                    for c in range(C):
                        mm = split_product(pe, bank[:, 0:SEQ], (w[0][:, c, :], w[1][:, c, :]), (at_hi[:, c, :], at_lo[:, c, :]),
                                           c == 0, c == C - 1)
                    return mm
                return emit

            def from_latents(n, t, w, bank):
                tok = slice(t * P, (t + 1) * P)
                return split_product(pe, bank, (lat_hi[:, n, tok], lat_lo[:, n, tok]), w, True, True)

            def keys_of(t):
                def emit(bank):
                    from_latents(0, t, parts["k_u"], bank[:, 0:HALF])
                    for c in range(C):
                        mm = split_product(pe, bank[:, HALF:], (at_hi[:, c, t * P:(t + 1) * P], at_lo[:, c, t * P:(t + 1) * P]),
                                           [w[:, c, :] for w in parts["rope_k"]], c == 0, c == C - 1)
                    return mm
                return emit

            def outputs(t):
                def emit(bank):
                    for c in range(C):
                        mm = split_product(pe, bank, (o_hi[:, c, t * P:(t + 1) * P], o_lo[:, c, t * P:(t + 1) * P]),
                                           [w[:, c, :] for w in parts["o"]], c == 0, c == C - 1)
                    return mm
                return emit

            def front(b, ahead, u):
                k0 = ring_base(b, ahead)
                if u == 1:
                    pe.wait_ge(a_done, TB * (b + ahead) + TB)
                    for t in range(TB):
                        use(k0, t, turned(a[:, t, :]))
                if u == 2:
                    pe.wait_ge(ring_free, k0 + TB)
                    use(k0, 2, latents(parts["kv_d"]))
                    use(k0, 3, latents(parts["q_d"]))
                if u == 3:
                    pe.wait_ge(ring_free, k0 + 4)
                    for t in range(TB):
                        use(k0, 4 + t, keys_of(t))
                if u == 4:
                    for t in range(TB):
                        use(k0, 6 + t, lambda bank: from_latents(1, t, parts["q_u"], bank))
                if u == 5:
                    for t in range(TB):
                        use(k0, 8 + t, lambda bank: from_latents(0, t, parts["v_u"], bank))
                if u == 8:
                    pe.wait_ge(rotated, 4 * (b + ahead) + 4)
                    for t in range(TB):
                        use(k0, 10 + t, turned(kf[:, t].rearrange("p h d -> p (h d)")))
                    for t in range(TB):
                        use(k0, 12 + t, turned(qf[:, t].rearrange("p h d -> p (h d)")), 1 + TB * (t == TB - 1 and ahead == 0))

            def weigh(b, u, par):
                if u % 2 == 0 and u >= 2:
                    att.weigh(pe, b, u // 2 - 1, par, lambda g, j, t: v[:, par, t, (4 * g + j) * HD:(4 * g + j + 1) * HD],
                              lambda g, j: att.o_ps[HD * j:HD * (j + 1), g % 2, 0:SEQ], 2)

            def attend(b, u, par):
                if u < UNITS:
                    att.scores(pe, b, u, lambda u, j: q_head[:, j, u // 2, (u % 2) * P:(u % 2 + 1) * P], lambda u, j: kt[:, u // 2, :],
                               mask[:, :], ident_b[:, :])
                weigh(b, u - 1, par)
                if u >= 1:
                    att.turn(pe, b, u - 1)

            def sample(b, par, last):
                pe.wait_ge(ring_free, ring_base(b, 0) + FRONT)
                for u in range(UNITS):
                    attend(b, u, par)
                    if not last:
                        front(b, 1, u)
                if not last:
                    front(b, 1, 8)
                attend(b, UNITS, par)
                weigh(b, UNITS, par)
                pe.wait_ge(att.o_lo_done, UNITS // 2 * (b + 1))
                k0 = output_uses(b, last)
                for t in range(TB):
                    use(k0, t, outputs(t))

            for u in range(9):
                front(0, 0, u)
            with pe.Fori(0, BATCH // 2 - 1) as i:
                for par in range(2):
                    sample(i * 2 + par, par, False)
            sample(BATCH - 2, 0, False)
            sample(BATCH - 1, 1, True)

        @block.scalar
        def _(act):
            def front(b, ahead, u):
                k0 = ring_base(b, ahead)
                if u == 1:
                    for t in range(TB):
                        act.wait_ge(ring_ready, k0 + t + 1)
                        act.activation(at_hi[:, :, t * P:(t + 1) * P], chunks(ring[:, t, :]), ACT.Copy).then_inc(hi_done, 1)
                if u == 2:
                    for n in range(2):
                        act.wait_ge(ring_ready, k0 + 2 + n + 1)
                        act.activation(lat_hi[:, n, :], ring[:, n, 0:SEQ], ACT.Copy).then_inc(hi_done, 1)
                if u in (3, 4):
                    for t in range(TB):
                        act.wait_ge(ring_ready, k0 + 2 * u - 2 + t + 1)
                        act.activation((kf, qf)[u - 3][:, t, :, 0:RD], ring[:, t, 0:HALF].rearrange("p (h d) -> p h d", h=NH),
                                       ACT.Copy).then_inc(plain_done, 1)
                if u == 8:
                    for t in range(TB):
                        act.wait_ge(ring_ready, k0 + 12 + t + 1)
                        for j in range(3):
                            ins = act.activation(q_head[HD * j:HD * (j + 1), j, :, t * P:(t + 1) * P],
                                                 chunks(ring[HD * j:HD * (j + 1), t, :]), ACT.Copy)
                        ins.then_inc(q_act_done, 1)

            def output(b, u):
                for g in groups_done(u):
                    if g == 0:
                        act.wait_ge(ring_ready, ring_base(b, 1))
                    att.output_high(act, b, g, o_hi[:, g, :], att.o_ps[:, g % 2, 0:SEQ])

            def sample(b, par, last):
                for u in range(UNITS + 1):
                    if u < UNITS:
                        att.exponentials(act, b, u)
                    if u == UNITS and not last:
                        front(b, 1, 8)
                    if u >= 1:
                        att.copy_turned(act, b, u - 1, 1, par)
                    output(b, u)
                    if u < UNITS and not last:
                        front(b, 1, u)

            act.wait_ge(zeroed2, 1)
            for u in range(9):
                front(0, 0, u)
            with act.Fori(0, BATCH // 2 - 1) as i:
                for par in range(2):
                    sample(i * 2 + par, par, False)
            sample(BATCH - 2, 0, False)
            sample(BATCH - 1, 1, True)

        @block.vector
        def _(dve):
            def front(b, ahead, u, par):
                k0 = ring_base(b, ahead)
                if u == 0:
                    dve.wait_ge(ring_ready, k0)
                    for t in range(TB):
                        n = (b + ahead) * TB + t
                        dve.scalar_tensor_tensor(a[:, t, :], tile_of(h_res, n), a_rstd[:, bass.ds(n, 1)], ln[:, :],
                                                 ALU.mult, ALU.mult).then_inc(a_done, 1)
                if u == 1:
                    for t in range(TB):
                        dve.wait_ge(hi_done, 4 * (b + ahead) + t + 1)
                        dve.tensor_tensor(at_lo[:, :, t * P:(t + 1) * P], chunks(ring[:, t, :]),
                                          f32(at_hi[:, :, t * P:(t + 1) * P]), ALU.subtract).then_inc(ring_free, 1)
                if u == 2:
                    for n in range(2):
                        dve.wait_ge(hi_done, 4 * (b + ahead) + 2 + n + 1)
                        dve.tensor_tensor(lat_lo[:, n, :], ring[:, n, 0:SEQ], f32(lat_hi[:, n, :]), ALU.subtract).then_inc(ring_free, 1)
                if u in (3, 4):
                    for t in range(TB):
                        n = 4 * (b + ahead) + 2 * (u - 3) + t
                        half = ring[:, t, HALF:].rearrange("p (h d) -> p h d", h=NH)
                        cos, sin = (rope[:, m, t, :].unsqueeze(1).to_broadcast([P, NH, RD]) for m in range(2))
                        dve.wait_ge(plain_done, n + 1)
                        dve.wait_ge(rotated, n)
                        dve.tensor_tensor(rot[:, 0], half, cos, ALU.mult).then_inc(products, 1)
                        dve.tensor_tensor(rot[:, 1, :, 0:RD // 2], half[:, :, RD // 2:], sin[:, :, 0:RD // 2], ALU.mult).then_inc(products, 1)
                        dve.tensor_tensor(rot[:, 1, :, RD // 2:], half[:, :, 0:RD // 2], sin[:, :, RD // 2:], ALU.mult).then_inc(ring_free, 1)
                        dve.wait_ge(products, 2 * n + 2)
                        dve.wait_ge(ring_free, k0 + 2 * u - 2 + t + 1)
                        dve.tensor_tensor((kf, qf)[u - 3][:, t, :, RD:], rot[:, 0], rot[:, 1], ALU.add).then_inc(rotated, 1)
                if u == 5:
                    for t in range(TB):
                        dve.wait_ge(ring_ready, k0 + 8 + t + 1)
                        dve.tensor_copy(v[:, par, t, :], ring[:, t, :]).then_inc(ring_free, 1)
                if u == 8:
                    for t in range(TB):
                        dve.wait_ge(ring_ready, k0 + 10 + t + 1)
                        dve.tensor_copy(kt[:, :, t * P:(t + 1) * P], chunks(ring[:, t, :])).then_inc(ring_free, 1)
                    for t in range(TB):
                        dve.wait_ge(q_act_done, TB * (b + ahead) + t + 1)
                        dve.tensor_copy(q_head[3 * HD:, 3, :, t * P:(t + 1) * P], chunks(ring[3 * HD:, t, :])).then_inc(
                            ring_free, 1 + TB * (t == TB - 1 and ahead == 0))

            def sample(b, par, last):
                for u in range(UNITS + 1):
                    if u < UNITS:
                        att.find_peak(dve, b, u)
                    if u == UNITS and not last:
                        front(b, 1, 8, 1 - par)
                    if u >= 1:
                        att.copy_turned(dve, b, u - 1, 0, par)
                    if u < UNITS:
                        att.invert_mass(dve, b, u)
                    if u < UNITS and not last:
                        front(b, 1, u, 1 - par)
                    for g in groups_done(u):
                        att.output_low(dve, b, g, o_lo[:, g, :], o_hi[:, g, :], att.o_ps[:, g % 2, 0:SEQ])
                k0 = output_uses(b, last)
                for t in range(TB):
                    dve.wait_ge(ring_ready, k0 + t + 1)
                    y = tile_of(h_res, b * TB + t)
                    dve.tensor_tensor(y, ring[:, t, :], y, ALU.add).then_inc(ring_free, 1)

            for u in range(9):
                front(0, 0, u, 0)
            with dve.Fori(0, BATCH // 2 - 1) as i:
                for par in range(2):
                    sample(i * 2 + par, par, False)
            sample(BATCH - 2, 0, False)
            sample(BATCH - 1, 1, True)


def expert_ffn(nc, x_res, h_res, ident, begun, w_dram, ln_row, router_dram, bias_dram, gate, out):
    EXPERTS = w_dram.shape[0]
    ROUTED = EXPERTS - 1
    I = w_dram.shape[2] // (3 * C)
    IC = I // P
    W = w_dram.shape[2]
    SLOTS = 8

    with ExitStack() as ctx:
        def sb(name, shape, dt=F32, of=None):
            return (of or ctx).enter_context(nc.sbuf_tensor(f"e_{name}", shape, dt))

        def sem(name):
            return nc.alloc_semaphore(f"e_{name}")

        rt_hi, rt_lo = sb("rt_hi", [P, C, TOK], F32R), sb("rt_lo", [P, C, TOK], F32R)
        raw = sb("raw", [P, W])
        w_hi, w_lo = sb("w_hi", [P, 2, W], F32R), sb("w_lo", [P, 2, W], F32R)
        share = sb("share", [P, TILES, EXPERTS])
        gate_sb, gain = sb("gate_sb", [P, 1]), sb("gain", [P, 1])
        w_in, w_hi_done, w_lo_done, gate_in = sem("w_in"), sem("w_hi_done"), sem("w_lo_done"), sem("gate_in")

        with ExitStack() as prep:
            ln = sb("ln_row", [P, D], F32, prep)
            r = sb("r", [P, 2, TB, D], F32, prep)
            router = sb("router", [P, C, P], F32, prep)
            router_hi, router_lo = (w[:, 1, 0:C * P].rearrange("p (c n) -> p c n", c=C) for w in (w_hi, w_lo))
            bias = sb("bias", [P, 1], F32, prep)
            junk = sb("junk", [P, D], BF16, prep)
            sq_sum, var, rstd, tmp = (sb(n, [P, TILES], F32, prep) for n in ("sq_sum", "var", "rstd", "tmp"))
            prob_t = sb("prob_t", [P, 2, SEQ], F32, prep)
            prob, rank, place, first, second = (sb(n, [P, TILES, SLOTS], F32, prep) for n in ("prob", "rank", "place", "first", "second"))
            best, next_best, spot, total = (sb(n, [P, TILES], F32, prep) for n in ("best", "next_best", "spot", "total"))
            t_ps = prep.enter_context(nc.psum_tensor("e_t_ps", [P, 2, TB, 512], F32))
            lg_ps = prep.enter_context(nc.psum_tensor("e_lg_ps", [P, 2, 512], F32))
            pt_ps = prep.enter_context(nc.psum_tensor("e_pt_ps", [P, 2, 512], F32))
            small_in, blank, router_in, router_hi_done, router_done, squared, steps = (
                sem(n) for n in ("small_in", "blank", "router_in", "router_hi_done", "router_done", "squared", "steps"))
            r_done, t_ready, rt_hi_done, rt_done, lg_ready, prob_done, pt_ready, ranked = (
                sem(n) for n in ("r_done", "t_ready", "rt_hi_done", "rt_done", "lg_ready", "prob_done", "pt_ready", "ranked"))
            prob_in = sem("prob_in")
            block = prep.enter_context(nc.Block())

            def tokens(b, t=0, n=SEQ):
                return bass.ds(b * SEQ + t * P, n)

            @block.sync
            def _(sp):
                sp.dma_start(raw[:, :], w_dram[0]).then_inc(w_in, 16)
                sp.dma_start(ln[:, :], ln_row).then_inc(small_in, 16)
                sp.dma_start(bias[:, :], bias_dram).then_inc(small_in, 16)
                sp.dma_start(gate_sb[:, :], gate).then_inc(gate_in, 16)
                sp.wait_ge(blank, 1)
                sp.dma_start(router[:, :, 0:SLOTS], router_dram).then_inc(router_in, 16)
                sp.wait_ge(w_lo_done, 1)
                sp.dma_start(raw[:, :], w_dram[1]).then_inc(w_in, 16)

            @block.gpsimd
            def _(pool):
                pool.memset(router[:, :, :], 0.0).then_inc(blank, 1)
                for j in range(SLOTS):
                    ins = pool.memset(rank[:, :, j], float(SLOTS - j))
                ins.then_inc(ranked, 1)
                pool.wait_ge(w_hi_done, 1)
                pool.tensor_tensor(w_lo[:, 0, :], raw[:, :], f32(w_hi[:, 0, :]), ALU.subtract).then_inc(w_lo_done, 1)

            @block.tensor
            def _(pe):
                def turn(b, par):
                    pe.wait_ge(r_done, b + 1)
                    if not isinstance(b, int) or b > 1:
                        pe.wait_ge(rt_done, TB * (b - 1))
                    for t in range(TB):
                        for c in range(C):
                            mm = pe.transpose(t_ps[:, par, t, c * P:(c + 1) * P], r[:, par, t, c * P:(c + 1) * P], ident[:, :])
                        mm.then_inc(t_ready, 1)

                def logits(b, par):
                    pe.wait_ge(rt_done, TB * b + TB)
                    for c in range(C):
                        mm = split_product(pe, lg_ps[:, par, 0:SEQ], (router_hi[:, c, :], router_lo[:, c, :]),
                                           (rt_hi[:, c, tokens(b)], rt_lo[:, c, tokens(b)]), c == 0, c == C - 1)
                    mm.then_inc(lg_ready, 1)
                    pe.wait_ge(prob_done, b + 1)
                    if not isinstance(b, int) or b > 1:
                        pe.wait_ge(prob_in, b - 1)
                    for t in range(TB):
                        mm = pe.transpose(pt_ps[:, par, t * P:(t + 1) * P], prob_t[:, par, t * P:(t + 1) * P], ident[:, :])
                    mm.then_inc(pt_ready, 1)

                pe.wait_ge(router_done, 1)
                turn(0, 0)
                turn(1, 1)
                logits(0, 0)
                turn(2, 0)
                logits(1, 1)
                with pe.Fori(1, BATCH // 2 - 1) as i:
                    for k in (0, 1):
                        turn(i * 2 + (k + 1), (k + 1) % 2)
                        logits(i * 2 + k, k)
                turn(BATCH - 1, 1)
                logits(BATCH - 2, 0)
                logits(BATCH - 1, 1)

            @block.scalar
            def _(act):
                def split(b, par):
                    for t in range(TB):
                        act.wait_ge(t_ready, TB * b + t + 1)
                        act.activation(rt_hi[:, :, tokens(b, t, P)], chunks(t_ps[:, par, t, :]), ACT.Copy).then_inc(rt_hi_done, 1)

                def sigmoid(b, par):
                    act.wait_ge(lg_ready, b + 1)
                    act.activation(prob_t[:, par, :], lg_ps[:, par, 0:SEQ], ACT.Sigmoid, bias=bias[:, :]).then_inc(prob_done, 1)

                with act.Fori(0, TILES) as n:
                    act.wait_ge(squared, n)
                    act.activation(junk[:, :], tile_of(h_res, n), ACT.Square, accum_out=sq_sum[:, bass.ds(n, 1)]).then_inc(squared, 1)
                act.wait_ge(router_in, 16)
                act.activation(router_hi[:, :, :], router[:, :, :], ACT.Copy).then_inc(router_hi_done, 1)
                act.wait_ge(gate_in, 16)
                act.activation(gain[:, :], gate_sb[:, :], ACT.Tanh)
                act.wait_ge(w_in, 16)
                act.activation(w_hi[:, 0, :], raw[:, :], ACT.Copy).then_inc(w_hi_done, 1)
                act.wait_ge(small_in, 32)
                split(0, 0)
                with act.Fori(0, BATCH // 2 - 1) as i:
                    for k in (0, 1):
                        split(i * 2 + (k + 1), (k + 1) % 2)
                        sigmoid(i * 2 + k, k % 2)
                split(BATCH - 1, 1)
                sigmoid(BATCH - 2, 0)
                sigmoid(BATCH - 1, 1)

            @block.vector
            def _(dve):
                chain = Chain(dve, steps, begun)

                def norm(b, par):
                    for t in range(TB):
                        ins = dve.scalar_tensor_tensor(r[:, par, t, :], tile_of(h_res, b * TB + t), rstd[:, bass.ds(b * TB + t, 1)],
                                                       ln[:, :], ALU.mult, ALU.mult)
                    ins.then_inc(r_done, 1)

                def split_low(b, par):
                    for t in range(TB):
                        dve.wait_ge(rt_hi_done, TB * b + t + 1)
                        dve.tensor_tensor(rt_lo[:, :, tokens(b, t, P)], chunks(t_ps[:, par, t, :]), f32(rt_hi[:, :, tokens(b, t, P)]),
                                          ALU.subtract).then_inc(rt_done, 1)

                def collect(b, par):
                    dve.wait_ge(pt_ready, b + 1)
                    if isinstance(b, int):
                        dve.wait_ge(steps, 1)
                    dve.tensor_copy(prob[:, bass.ds(b * TB, TB), 0:ROUTED],
                                    pt_ps[:, par, 0:TB * P].rearrange("p (t s) -> p t s", s=P)[:, :, 0:ROUTED]).then_inc(prob_in, 1)

                def spread(x):
                    return x[:, :].unsqueeze(2).to_broadcast([P, TILES, SLOTS])

                chain.step(dve.memset(prob[:, :, :], -1.0))
                dve.memset(share[:, :, 0], 1.0)
                dve.wait_ge(router_hi_done, 1)
                dve.tensor_tensor(router_lo[:, :, :], router[:, :, :], f32(router_hi[:, :, :]), ALU.subtract).then_inc(router_done, 1)
                dve.wait_ge(squared, TILES)
                chain.step(dve.tensor_scalar(var[:, :], sq_sum[:, :], 1.0 / D, LN_EPS, ALU.mult, ALU.add))
                chain.wait()
                inverse_sqrt(dve, chain, rstd[:, :], var[:, :], tmp[:, :])
                chain.wait()
                dve.wait_ge(small_in, 32)
                norm(0, 0)
                norm(1, 1)
                with dve.Fori(0, BATCH // 2 - 1) as i:
                    for k in (0, 1):
                        split_low(i * 2 + k, k)
                        norm(i * 2 + (k + 2), k)
                        collect(i * 2 + k, k)
                for k in (0, 1):
                    split_low(BATCH - 2 + k, k)
                for k in (0, 1):
                    collect(BATCH - 2 + k, k)

                dve.wait_ge(prob_in, BATCH)
                dve.wait_ge(ranked, 1)
                for value, hot in ((best, first), (next_best, second)):
                    chain.step(dve.tensor_reduce(value[:, :], prob[:, :, :], AX.X, ALU.max))
                    chain.wait()
                    chain.step(dve.tensor_tensor(place[:, :, :], prob[:, :, :], spread(value), ALU.is_equal))
                    chain.wait()
                    chain.step(dve.tensor_tensor(place[:, :, :], place[:, :, :], rank[:, :, :], ALU.mult))
                    chain.wait()
                    chain.step(dve.tensor_reduce(spot[:, :], place[:, :, :], AX.X, ALU.max))
                    chain.wait()
                    chain.step(dve.tensor_tensor(hot[:, :, :], place[:, :, :], spread(spot), ALU.is_equal))
                    chain.wait()
                    if hot is first:
                        chain.step(dve.scalar_tensor_tensor(prob[:, :, :], first[:, :, :], -2.0, prob[:, :, :], ALU.mult, ALU.add))
                        chain.wait()
                chain.step(dve.tensor_tensor(first[:, :, :], first[:, :, :], spread(best), ALU.mult))
                chain.step(dve.tensor_tensor(second[:, :, :], second[:, :, :], spread(next_best), ALU.mult))
                chain.step(dve.tensor_tensor(total[:, :], best[:, :], next_best[:, :], ALU.add))
                chain.wait()
                chain.step(dve.tensor_tensor(first[:, :, :], first[:, :, :], second[:, :, :], ALU.add))
                chain.step(dve.reciprocal(spot[:, :], total[:, :]))
                chain.wait()
                dve.tensor_tensor(share[:, :, 1:EXPERTS], first[:, :, 0:ROUTED], spot[:, :].unsqueeze(2).to_broadcast([P, TILES, ROUTED]), ALU.mult)

        sg = sb("sg", [P, 2, IC * SEQ])
        act_f = sb("act_f", [P, IC * SEQ])
        act_hi, act_lo = sb("act_hi", [P, 2, IC, SEQ], F32R), sb("act_lo", [P, 2, IC, SEQ], F32R)
        g_ps = ctx.enter_context(nc.psum_tensor("e_g_ps", [P, 2, IC * SEQ], F32))
        u_ps = ctx.enter_context(nc.psum_tensor("e_u_ps", [P, 2, IC * SEQ], F32))
        d_ps = ctx.enter_context(nc.psum_tensor("e_d_ps", [P, 2, TB, D], F32))
        g_ready, u_ready, sg_done, act_done, hi_done, lo_done, d_ready, added, x_done, stored = (
            sem(n) for n in ("g_ready", "u_ready", "sg_done", "act_done", "hi_done", "lo_done", "d_ready", "added", "x_done", "stored"))
        block = ctx.enter_context(nc.Block())

        def weights(par):
            of = [[w[:, par, k * C * I:(k + 1) * C * I] for w in (w_hi, w_lo)] for k in range(3)]
            gate_w, up_w = ([w.rearrange("p (c i) -> p c i", c=C) for w in of[k]] for k in range(2))
            return gate_w, up_w, [w.rearrange("p (c n) -> p c n", c=IC) for w in of[2]]

        def unit(e, s):
            return e * BATCH + s

        def experts(eng, one):
            one(0, 0)
            with eng.Fori(0, (EXPERTS - 2) // 2) as i:
                one(i * 2 + 1, 1)
                one(i * 2 + 2, 0)
            one(EXPERTS - 1, 1)

        @block.sync
        def _(sp):
            with sp.Fori(2, EXPERTS) as e:
                wait_apart(sp, w_lo_done, e, begun)
                sp.dma_start(raw[:, :], w_dram[bass.ds(e, 1)].rearrange("o p n -> (o p) n")).then_inc(w_in, 16)
            for b in range(BATCH):
                sp.wait_ge(x_done, b + 1)
                sp.dma_start(out[:, b * TB:(b + 1) * TB, :], x_res[:, b * TB:(b + 1) * TB, :]).then_inc(stored, 16)
            sp.wait_ge(stored, 16 * BATCH)

        @block.gpsimd
        def _(pool):
            def split_low(e, par):
                pool.wait_ge(w_hi_done, e + 1)
                pool.tensor_tensor(w_lo[:, par, :], raw[:, :], f32(w_hi[:, par, :]), ALU.subtract).then_inc(w_lo_done, 1)

            with pool.Fori(0, (EXPERTS - 2) // 2) as i:
                split_low(i * 2 + 1, 1)
                split_low(i * 2 + 2, 0)
            split_low(EXPERTS - 1, 1)

        @block.tensor
        def _(pe):
            def up(e, s, par, w):
                n = unit(e, s)
                if not isinstance(n, int) or n > 1:
                    pe.wait_ge(act_done, n - 1)
                here = bass.ds(s * SEQ, SEQ)
                for ps, side, ready in ((g_ps, w[0], g_ready), (u_ps, w[1], u_ready)):
                    for k in range(IC):
                        for c in range(C):
                            cols = slice(k * P, (k + 1) * P)
                            mm = split_product(pe, ps[:, par, k * SEQ:(k + 1) * SEQ], (side[0][:, c, cols], side[1][:, c, cols]),
                                               (rt_hi[:, c, here], rt_lo[:, c, here]), c == 0, c == C - 1)
                    mm.then_inc(ready, 1)

            def down(e, s, par, w):
                n = unit(e, s)
                pe.wait_ge(lo_done, n + 1)
                if not isinstance(n, int) or n > 1:
                    pe.wait_ge(added, n - 1)
                for t in range(TB):
                    for k in range(IC):
                        tok = slice(t * P, (t + 1) * P)
                        mm = split_product(pe, d_ps[:, par, t, :], (act_hi[:, par, k, tok], act_lo[:, par, k, tok]),
                                           (w[2][0][:, k, :], w[2][1][:, k, :]), k == 0, k == IC - 1)
                mm.then_inc(d_ready, 1)

            def expert(e, par_w):
                w = weights(par_w)
                pe.wait_ge(w_lo_done, e + 1)
                up(e, 0, 0, w)
                if not isinstance(e, int) or e > 0:
                    down(e - 1, BATCH - 1, 1, weights(1 - par_w))
                up(e, 1, 1, w)
                down(e, 0, 0, w)
                with pe.Fori(1, BATCH // 2) as i:
                    for par in range(2):
                        up(e, i * 2 + par, par, w)
                        down(e, i * 2 + (par - 1), 1 - par, w)

            experts(pe, expert)
            down(EXPERTS - 1, BATCH - 1, 1, weights((EXPERTS - 1) % 2))

        @block.scalar
        def _(act):
            def split_weights(e, par):
                act.wait_ge(w_in, 16 * e + 16)
                act.wait_ge(d_ready, unit(e - 1, 0))
                act.activation(w_hi[:, par, :], raw[:, :], ACT.Copy).then_inc(w_hi_done, 1)

            def sample(e, s, par):
                n = unit(e, s)
                act.wait_ge(g_ready, n + 1)
                if not isinstance(n, int) or n > 1:
                    act.wait_ge(act_done, n - 1)
                act.activation(sg[:, par, :], g_ps[:, par, :], ACT.Silu).then_inc(sg_done, 1)
                act.wait_ge(act_done, n + 1)
                if not isinstance(n, int) or n > 1:
                    act.wait_ge(d_ready, n - 1)
                act.activation(act_hi[:, par, :, :].rearrange("p k q -> p (k q)"), act_f[:, :], ACT.Copy).then_inc(hi_done, 1)

            def expert(e, par_w):
                sample(e, 0, 0)
                sample(e, 1, 1)
                if not isinstance(e, int) or e < EXPERTS - 1:
                    split_weights(e + 1, 1 - par_w)
                with act.Fori(1, BATCH // 2) as i:
                    for par in range(2):
                        sample(e, i * 2 + par, par)

            experts(act, expert)

        @block.vector
        def _(dve):
            def middle(e, s, par):
                n = unit(e, s)
                dve.wait_ge(u_ready, n + 1)
                dve.wait_ge(sg_done, n + 1)
                if not isinstance(n, int) or n > 0:
                    dve.wait_ge(lo_done, n)
                dve.scalar_tensor_tensor(act_f[:, :], u_ps[:, par, :], 0.125, sg[:, par, :], ALU.mult, ALU.mult).then_inc(act_done, 1)
                dve.wait_ge(hi_done, n + 1)
                dve.tensor_tensor(act_lo[:, par, :, :].rearrange("p k q -> p (k q)"), act_f[:, :],
                                  f32(act_hi[:, par, :, :]).rearrange("p k q -> p (k q)"), ALU.subtract).then_inc(lo_done, 1)

            def add(e, s, par):
                n = unit(e, s)
                dve.wait_ge(d_ready, n + 1)
                for t in range(TB):
                    tile = s * TB + t
                    mine = share[:, bass.ds(tile, 1), bass.ds(e, 1)].rearrange("p o e -> p (o e)")
                    h = tile_of(h_res, tile)
                    ins = dve.scalar_tensor_tensor(h, d_ps[:, par, t, :], mine, h, ALU.mult, ALU.add)
                ins.then_inc(added, 1)
                if isinstance(e, int) and e == EXPERTS - 1:
                    dve.wait_ge(added, n + 1)
                    for t in range(TB):
                        x = tile_of(x_res, s * TB + t)
                        ins = dve.scalar_tensor_tensor(x, tile_of(h_res, s * TB + t), gain[:, 0:1], x, ALU.mult, ALU.add)
                    ins.then_inc(x_done, 1)

            def expert(e, par_w):
                middle(e, 0, 0)
                if not isinstance(e, int) or e > 0:
                    add(e - 1, BATCH - 1, 1)
                middle(e, 1, 1)
                add(e, 0, 0)
                with dve.Fori(1, BATCH // 2) as i:
                    for par in range(2):
                        middle(e, i * 2 + par, par)
                        add(e, i * 2 + (par - 1), 1 - par)

            experts(dve, expert)
            add(EXPERTS - 1, BATCH - 1, 1)


def decoder(nc, a, out):
    with ExitStack() as ctx:
        x_res = ctx.enter_context(nc.sbuf_tensor("x_res", [P, TILES, D], F32))
        ident = ctx.enter_context(nc.sbuf_tensor("ident", [P, P], F32))
        begun = ctx.enter_context(nc.semaphore("begun"))
        blank = ctx.enter_context(nc.semaphore("blank"))
        with nc.Block() as block:
            @block.gpsimd
            def _(pool):
                pool.memset(ident[:, :], 0.0).then_inc(blank, 1)
                pool.wait_ge(blank, 1)
                pool.affine_select(out=ident[:, :], in_=ident[:, :], compare_op=ALU.not_equal, fill=1.0, base=0,
                                   pattern=[[-1, P]], channel_multiplier=1).then_inc(begun, 1)
        with nc.cleanup_on_exit():
            image_attention(nc, x_res, ident, begun, a["x"], a["ctx_t"], a["a_w"], a["a_rows"], a["g_xattn0"])
        with nc.cleanup_on_exit():
            quantised_ffn(nc, x_res, ident, begun, a["b_w"], a["b_ln"], a["g_ffn0"])
        xnt_dram = nc.dram_tensor("xnt_scratch", (BATCH, P, C, SEQ), F32, kind="Internal").ap()
        with nc.cleanup_on_exit():
            cross_attention(nc, x_res, ident, begun, xnt_dram, a["ctx_t"], a["c_w"], a["g_xattn1"])
        h_res = ctx.enter_context(nc.sbuf_tensor("h_res", [P, TILES, D], F32))
        with nc.cleanup_on_exit():
            latent_attention(nc, x_res, h_res, ident, begun, a["d_w"], a["d_ln"], a["rope"])
        with nc.cleanup_on_exit():
            expert_ffn(nc, x_res, h_res, ident, begun, a["e_w"], a["e_ln"], a["router"], a["router_b"], a["g_ffn1"], out)


def tiled(x):
    return np.ascontiguousarray(np.asarray(x).reshape(TILES, P, D).transpose(1, 0, 2))


def rows_on_partitions(w):
    return np.ascontiguousarray(w.reshape(-1, P, w.shape[1]).transpose(1, 0, 2))


def on_all_partitions(*vectors):
    return np.ascontiguousarray(np.broadcast_to(np.stack(vectors), (P, len(vectors), vectors[0].shape[0])))


def rope_table():
    half = D // NH // 4
    freq = (np.float32(1) / np.float32(10000) ** (np.arange(0, 2 * half, 2, dtype=np.float32) / np.float32(2 * half))).astype(np.float32)
    angle = np.outer(np.arange(SEQ, dtype=np.float32), freq).astype(np.float32)
    cos, sin = np.cos(angle, dtype=np.float32), np.sin(angle, dtype=np.float32)
    table = np.stack([np.concatenate([cos, cos], 1), np.concatenate([-sin, sin], 1)])
    return np.ascontiguousarray(table.reshape(2, TB, P, 2 * half).transpose(2, 0, 1, 3))


def layouts(i):
    a = {}
    a["x"] = tiled(i["x"])
    a["ctx_t"] = np.ascontiguousarray(i["ctx_2048"].reshape(BATCH, SEQ, C, P).transpose(0, 3, 2, 1))
    a["a_w"] = np.stack([rows_on_partitions(i[f"L0_xattn_{n}_w"].T) for n in ("q", "k_img", "v_img", "o")])
    a["a_rows"] = on_all_partitions(*(i[f"L0_xattn_{n}"] for n in ("q_b", "k_img_b", "v_img_b", "o_b", "norm_q_w", "norm_k_img_w")))
    a["b_w"] = np.stack([rows_on_partitions(i[f"L0_ffn_w_{n}"].T).reshape(P, -1) for n in ("gate", "up", "down")])
    a["b_ln"] = np.ascontiguousarray(np.broadcast_to(i["L0_ffn_ln_weight"], (P, 2048)))
    heads = [i[f"L1_xattn_W{n}"].reshape(C, P, NH // 4, D).transpose(2, 1, 0, 3) for n in "qkv"]
    a["c_w"] = np.ascontiguousarray(np.stack([*heads, i["L1_xattn_Wo"].reshape(NH // 4, 4, P, D).transpose(0, 2, 1, 3)], 1))
    f = {n: i[f"L1_ffn_{n}"] for n in ("kv_d_w", "q_d_w", "k_u_w", "q_u_w", "v_u_w", "rope_k_w", "rope_q_w", "o_w", "ln1_w", "ln2_w")}
    a["d_w"] = np.concatenate([rows_on_partitions(w).reshape(P, -1) for w in (
        f["kv_d_w"], f["q_d_w"], f["k_u_w"], np.concatenate([f["q_u_w"], f["rope_q_w"]], 1), f["v_u_w"], f["rope_k_w"], f["o_w"])], 1)
    a["d_ln"] = np.ascontiguousarray(np.broadcast_to(f["ln1_w"], (P, D)))
    a["rope"] = rope_table()
    f = {n: i[f"L1_ffn_{n}"] for n in ("sh_gate", "sh_up", "sh_down", "r_gate", "r_up", "r_down", "router_w", "router_b")}
    experts = [(f["sh_gate"], f["sh_up"], f["sh_down"]), *zip(f["r_gate"], f["r_up"], f["r_down"])]
    a["e_w"] = np.stack([np.concatenate([rows_on_partitions(w).reshape(P, -1) for w in e], 1) for e in experts])
    a["e_ln"] = np.ascontiguousarray(np.broadcast_to(i["L1_ffn_ln2_w"], (P, D)))
    a["router"] = rows_on_partitions(np.concatenate([f["router_w"], np.zeros((D, 1), np.float32)], 1))
    a["router_b"] = np.concatenate([f["router_b"], np.zeros(P - len(f["router_b"]), np.float32)]).reshape(P, 1)
    for n, g in (("g_xattn0", i["g_xattn"][0:1]), ("g_xattn1", i["g_xattn"][1:2]), ("g_ffn0", i["g_ffn"][0:1]), ("g_ffn1", i["g_ffn"][1:2])):
        a[n] = np.ascontiguousarray(np.broadcast_to(g, (P, 1)))
    return a


def kernel(**inputs):
    import concourse.bacc as bacc
    from concourse.bass_utils import run_bass_kernel_spmd

    nc = bacc.Bacc("TRN2", target_bir_lowering=False, num_devices=1)
    arrays = layouts({name: np.asarray(value) for name, value in inputs.items()})
    a = {name: nc.dram_tensor(name, value.shape, mybir.dt.from_np(value.dtype), kind="ExternalInput").ap() for name, value in arrays.items()}
    out = nc.dram_tensor("out", (P, TILES, D), F32, kind="ExternalOutput").ap()
    decoder(nc, a, out)
    result = run_bass_kernel_spmd(nc, [arrays], core_ids=[0])
    return np.asarray(result.results[0]["out"]).transpose(1, 0, 2).reshape(BATCH, SEQ, D)
```
